# Optimizing a Trainium2 kernel written in Bass

```python
import numpy as np
import jax
import jax.numpy as jnp

def _softmax(x, axis=-1):
    return jax.nn.softmax(x, axis=axis)

def _gelu(x):
    return jax.nn.gelu(x, approximate=True)

def _silu(x):
    return jax.nn.silu(x)

def _sigmoid(x):
    return jax.nn.sigmoid(x)

def _layernorm(x, axis=-1, eps=1e-05):
    m = jnp.mean(x, axis=axis, keepdims=True)
    v = jnp.var(x, axis=axis, keepdims=True)
    return (x - m) / jnp.sqrt(v + eps)

def _scatter_add(tgt, idx, src, axis=0):
    return tgt.at[idx].add(src)

def _segment_sum(src, seg, n):
    return jax.ops.segment_sum(src, seg, n)
kernel_name = 'mk_lm_tower_d1_tok_ids1024_r4_670ab5'

def setup_inputs(seed: int=0):
    np.random.seed(seed)
    _w = jnp.asarray

    def _rec_inputs():
        import jax
        import jax.numpy as jnp
        _rk = jax.random.key(seed)
        x = jax.random.randint(jax.random.fold_in(_rk, 1), (8, 256), 0, 8000, jnp.int32)
        return x
    x = _rec_inputs()

    def _L0_tok_setup():
        import jax, jax.numpy as jnp
        import numpy as np
        VOCAB, HID, OUT = (8000, 128, 256)
        B, S = (8, 1024)
        key = jax.random.key(seed)
        k1, k2, k3 = jax.random.split(key, 3)
        inputs = jax.random.randint(k1, (B, S), 0, VOCAB, dtype=jnp.int32)
        embeddings = jax.random.normal(k2, (VOCAB, HID), dtype=jnp.float32) * 0.02
        project_kernel = jax.random.normal(k3, (HID, OUT), dtype=jnp.float32) * 0.02
        return {'inputs': inputs, 'embeddings': embeddings, 'project_kernel': project_kernel}
    _L0_tok_all = _L0_tok_setup()
    _L0_tok_in = {k: v for k, v in _L0_tok_all.items() if k in ('embeddings', 'project_kernel')}
    del _L0_tok_all

    def _L0_attn_setup():
        import jax, jax.numpy as jnp
        import numpy as np
        NUM_HEADS = 32
        EPS = 1e-15
        key = jax.random.key(seed)
        k1, k2, k3, k4 = jax.random.split(key, 4)
        B, N, C = (8, 1024, 256)
        x = jax.random.normal(k1, (B, N, C), dtype=jnp.float32)
        qkv_weight = jax.random.normal(k2, (3 * C, C), dtype=jnp.float32) * C ** (-0.5)
        proj_weight = jax.random.normal(k3, (C, C), dtype=jnp.float32) * C ** (-0.5)
        proj_bias = jax.random.normal(k4, (C,), dtype=jnp.float32) * 0.01
        return {'x': x, 'qkv_weight': qkv_weight, 'proj_weight': proj_weight, 'proj_bias': proj_bias}
    _L0_attn_all = _L0_attn_setup()
    _L0_attn_in = {k: v for k, v in _L0_attn_all.items() if k in ('qkv_weight', 'proj_weight', 'proj_bias')}
    del _L0_attn_all

    def _L0_ffn_setup():
        import jax, jax.numpy as jnp
        import numpy as np
        B, N, C, H, REG = (1, 2309, 256, 16, 5)
        D = C // H
        key = jax.random.key(seed)
        k0, k1, k2, k3 = jax.random.split(key, 4)
        x = jax.random.normal(k0, (B, N, C), dtype=jnp.float32)
        g_info = jax.random.normal(k1, (12, 2, C), dtype=jnp.float32)
        W_qkv = jax.random.normal(k2, (C, 3 * C), dtype=jnp.float32) * 0.02
        W_proj = jax.random.normal(k3, (C, C), dtype=jnp.float32) * 0.02
        b_proj = jnp.zeros((C,), dtype=jnp.float32)
        return {'x': x, 'g_info': g_info, 'W_qkv': W_qkv, 'W_proj': W_proj, 'b_proj': b_proj}
    _L0_ffn_all = _L0_ffn_setup()
    _L0_ffn_in = {k: v for k, v in _L0_ffn_all.items() if k in ('g_info', 'W_qkv', 'W_proj', 'b_proj')}
    del _L0_ffn_all
    return {'x': x, 'L0_tok_embeddings': _L0_tok_in['embeddings'], 'L0_tok_project_kernel': _L0_tok_in['project_kernel'], 'L0_attn_qkv_weight': _L0_attn_in['qkv_weight'], 'L0_attn_proj_weight': _L0_attn_in['proj_weight'], 'L0_attn_proj_bias': _L0_attn_in['proj_bias'], 'L0_ffn_g_info': _L0_ffn_in['g_info'], 'L0_ffn_W_qkv': _L0_ffn_in['W_qkv'], 'L0_ffn_W_proj': _L0_ffn_in['W_proj'], 'L0_ffn_b_proj': _L0_ffn_in['b_proj']}

def reference(x, L0_tok_embeddings, L0_tok_project_kernel, L0_attn_qkv_weight, L0_attn_proj_weight, L0_attn_proj_bias, L0_ffn_g_info, L0_ffn_W_qkv, L0_ffn_W_proj, L0_ffn_b_proj):
    import jax
    import jax.numpy as jnp

    def _L0_tok_ref(inputs, embeddings, project_kernel):
        import jax, jax.numpy as jnp
        import numpy as np
        VOCAB, HID, OUT = (8000, 128, 256)
        B, S = (8, 1024)
        low = jnp.take(embeddings, inputs, axis=0)
        return jnp.einsum('bsh,ho->bso', low, project_kernel)

    def _L0_attn_ref(x, qkv_weight, proj_weight, proj_bias):
        import jax, jax.numpy as jnp
        import numpy as np
        NUM_HEADS = 32
        EPS = 1e-15
        B, N, C = x.shape
        H = NUM_HEADS
        D = C // H
        qkv = jax.nn.relu(jnp.einsum('bnc,oc->bno', x, qkv_weight))
        qkv = qkv.reshape(B, N, 3, H, D)
        q, k, v = (qkv[:, :, 0], qkv[:, :, 1], qkv[:, :, 2])
        v_pad = jnp.concatenate([v, jnp.ones((B, N, H, 1), dtype=v.dtype)], axis=-1)
        vk = jnp.einsum('bnhe,bnhd->bhed', v_pad.astype(jnp.float32), k.astype(jnp.float32))
        vk_q = jnp.einsum('bhed,bnhd->bnhe', vk, q.astype(jnp.float32))
        proj_input = (vk_q[..., :D] / (vk_q[..., D:] + EPS)).astype(qkv.dtype)
        proj_input = proj_input.reshape(B, N, C)
        y = jnp.einsum('bnc,oc->bno', proj_input, proj_weight) + proj_bias
        return y

    def _L0_ffn_ref(x, g_info, W_qkv, W_proj, b_proj):
        import jax, jax.numpy as jnp
        import numpy as np
        B, N, C, H, REG = (1, 2309, 256, 16, 5)
        D = C // H
        Bx, Nx, Cx = x.shape
        scale = D ** (-0.5)
        qkv = (x @ W_qkv).reshape(Bx, Nx, 3, H, D)
        q, k, v = (qkv[:, :, 0], qkv[:, :, 1], qkv[:, :, 2])
        g_layer = g_info[0].reshape(-1, H, D)
        q_g = g_layer[0]
        q_pure = q[:, REG:]
        q_n = q_pure / jnp.linalg.norm(q_pure, axis=-1, keepdims=True)
        qg_n = q_g / jnp.linalg.norm(q_g, axis=-1, keepdims=True)
        sim = (qg_n[None, None] * q_n).sum(-1).mean(-1)
        sim = (sim - sim.min()) / (sim.max() - sim.min())
        pos = sim > 0.9
        logits = jnp.einsum('bqhd,bkhd->bhqk', q * scale, k)

        def masked_attn(tok_mask):
            key_mask = jnp.concatenate([jnp.ones((Bx, REG), bool), tok_mask], axis=1)
            l = jnp.where(key_mask[:, None, None, :], logits, -jnp.inf)
            a = jax.nn.softmax(l, axis=-1)
            return jnp.einsum('bhqk,bkhd->bqhd', a, v)
        x_pos = masked_attn(pos)
        x_neg = masked_attn(~pos)
        reg_out = (x_pos[:, :REG] + x_neg[:, :REG]) * 0.5
        tok_out = jnp.where(pos[:, :, None, None], x_pos[:, REG:], x_neg[:, REG:])
        out = jnp.concatenate([reg_out, tok_out], axis=1).reshape(Bx, Nx, Cx)
        return out @ W_proj + b_proj
    h = _L0_tok_ref(x, L0_tok_embeddings, L0_tok_project_kernel)
    h = h + _L0_attn_ref(_layernorm(h, axis=-1), L0_attn_qkv_weight, L0_attn_proj_weight, L0_attn_proj_bias)
    h = h + _L0_ffn_ref(_layernorm(h, axis=-1), L0_ffn_g_info, L0_ffn_W_qkv, L0_ffn_W_proj, L0_ffn_b_proj)
    return h

_drawn_inputs = setup_inputs


def setup_inputs(seed=0):
    import zlib

    import numpy as np

    out = dict(_drawn_inputs(seed))
    spreads = {'L0_ffn_b_proj': (0.0, 0.1)}
    factors = {}
    for name, (base, spread) in spreads.items():
        noise = np.random.default_rng([zlib.crc32(name.encode()), seed]).standard_normal(out[name].shape)
        drawn = base * np.exp(spread * noise) if base else spread * noise
        out[name] = jnp.asarray(drawn.astype(out[name].dtype))
    for name, factor in factors.items():
        out[name] = (out[name] * factor).astype(out[name].dtype)
    return out
```

```python
from contextlib import ExitStack

import concourse.bass as bass
from concourse import mybir

F32 = mybir.dt.float32
BF16 = mybir.dt.bfloat16
I32 = mybir.dt.int32
U32 = mybir.dt.uint32
ALU = mybir.AluOpType
ACT = mybir.ActivationFunctionType
AX = mybir.AxisListType
RMAX = bass.bass_isa.ReduceOp.max

P = 128
LN_EPS = 1e-5
DEN_EPS = 1e-15
BIG = 1e30


def lm_tower(nc, x, embeddings, tok_kernel, attn_qkv_t, attn_proj_t, attn_bias,
             ffn_g, ffn_qkv, ffn_proj, ffn_bias, out):
    NB, S = 8, 256
    assert tuple(x.shape) == (P, NB * S // P)
    C = tok_kernel.shape[1]
    VOCAB = embeddings.shape[0]
    T = S // P
    KC = C // P
    AD = 8
    AH = P // AD
    FD = 16
    FH = C // FD
    HH = FH // 2
    REG = 5
    NQ = S + REG
    PARTS = 3
    Q_PART = (0, 0, 0, 1, 1, 2)
    K_PART = (0, 1, 2, 0, 1, 0)
    ROW_CLASS = FD * len(Q_PART)
    ROW_MAX = ROW_CLASS + 2
    ROWS = ROW_MAX + 2
    NSTORE = 4 * len(Q_PART)
    GH = 4
    NG = FH // GH
    UNITS = FH + 2
    WIN = 32

    q_img = nc.dram_tensor("q_image", [NB, ROW_MAX, FH, S], BF16).ap()
    k_img = nc.dram_tensor("k_image", [NB, ROW_MAX, FH, S], BF16).ap()
    class_dram = nc.dram_tensor("class_rows", [4, NB * S], BF16).ap()

    with ExitStack() as ctx:
        def sb(name, shape, dt=F32):
            return ctx.enter_context(nc.sbuf_tensor(name, shape, dt))

        def sem(name):
            return ctx.enter_context(nc.semaphore(name))

        ps = ctx.enter_context(nc.psum_tensor("ps", [P, 8, 512], F32))

        ident = sb("ident", [P, P])
        ones = sb("ones", [P, P])
        blk8 = sb("blk8", [P, AH, AD])
        blk16 = sb("blk16", [P, HH, FD])
        head_of = sb("head_of", [P, 32])
        g_dot = sb("g_dot", [P, KC, 32])
        reg_is = sb("reg_is", [P, NB * T])
        quad = sb("quad", [P, GH])
        reg_row = sb("reg_row", [P, REG])
        eps_t = sb("eps_t", [P, 1])
        gvec = sb("gvec", [P, KC])
        parts_mark = sb("parts_mark", [1, 1])
        carry_dve = sb("carry_dve", [P, 32])
        carry_pool = sb("carry_pool", [P, 32])
        gtmp = sb("gtmp", [P, KC])
        gnrm = sb("gnrm", [P, KC])
        w_tok = sb("w_tok", [P, C])
        w_aqkv = sb("w_aqkv", [P, KC, 3 * C])
        w_aproj = sb("w_aproj", [P, KC, C])
        w_fqkv = sb("w_fqkv", [P, KC, 3 * C])
        w_fproj = sb("w_fproj", [P, KC, C])
        b_attn = sb("b_attn", [P, C])
        b_ffn = sb("b_ffn", [P, C])
        ids = sb("ids", [P, NB * T], I32)
        ids_now = sb("ids_now", [P, T], I32)
        emb = sb("emb", [P, T, P])
        emb_t = sb("emb_t", [P, S])
        h_all = sb("h_all", [P, NB, T * C])
        v_all = sb("v_all", [P, NB, T * C])
        sim_all = sb("sim_all", [P, NB * T])
        bst1 = sb("bst1", [P, T, 6])
        mv1 = sb("mv1", [P, T, 2])
        sd1 = sb("sd1", [P, T])
        rs1 = sb("rs1", [P, T])
        xn1 = sb("xn1", [P, T, C])
        xn1_t = sb("xn1_t", [P, KC, S])
        q1_t = sb("q1_t", [P, KC, S])
        kv = sb("kv", [P, T, 4, P + 1])
        vk = sb("vk", [P, KC, P + AH])
        den = sb("den", [P, T, KC, AH])
        rden = sb("rden", [P, T, KC, AH])
        mix = sb("mix", [P, T, KC, AH, AD])
        mix_t = sb("mix_t", [P, KC, S])
        bst2 = sb("bst2", [P, T, 6])
        mv2 = sb("mv2", [P, T, 2])
        sd2 = sb("sd2", [P, T])
        rs2 = sb("rs2", [P, T])
        xn2 = sb("xn2", [P, T, C])
        xn2_t = sb("xn2_t", [P, KC, S])
        qkf = sb("qkf", [P, KC, 2, S])
        qsq = sb("qsq", [P, KC, S])
        qk_parts = sb("qk_parts", [P, KC * 2, PARTS, S], BF16)
        qk_rest = sb("qk_rest", [P, KC * 2, S])
        dots = sb("dots", [P, S])
        nrm = sb("nrm", [P, T, KC, HH])
        rnrm = sb("rnrm", [P, T, KC, HH])
        cosb = sb("cosb", [P, T, KC, HH])
        ext = sb("ext", [P, 2])
        exta = sb("exta", [P, 2])
        zsum = sb("zsum", [P, 2])
        thr = sb("thr", [P, 2])
        pos = sb("pos", [P, NB * T])
        neg = sb("neg", [P, NB * T])
        cls = sb("cls", [P, 4, NB * T])
        cls_t = sb("cls_t", [4 * NB * T, P], BF16)
        q_st = [sb(f"q_st{u}", [ROWS, FH, NQ], BF16) for u in range(2)]
        k_st = [sb(f"k_st{u}", [ROWS, FH, S], BF16) for u in range(2)]
        v_st = [sb(f"v_st{u}", [P, T, FH, 2 * FD]) for u in range(2)]
        mx = sb("mx", [P, 2, 2 * HH + 2])
        mxr = sb("mxr", [P, 2, HH // GH, GH])
        mrow = sb("mrow", [HH, 2, 2, NQ], BF16)
        ex = [sb(f"ex{u}", [P, GH, T, NQ]) for u in range(2)]
        pv = [sb(f"pv{u}", [P, NG, NQ]) for u in range(2)]
        rsum = sb("rsum", [P, FH])
        rsumx = sb("rsumx", [REG, FH])
        att = sb("att", [P, T, FH, FD])
        attx = sb("attx", [REG, FH, FD])
        att_t = sb("att_t", [P, KC, S])
        resid = [sb(f"resid{u}", [P, T * C]) for u in range(2)]
        fin = [sb(f"fin{u}", [P, T * C]) for u in range(2)]

        loaded = sem("loaded")
        const_pool = sem("const_pool")
        const_dve = sem("const_dve")
        g_sq = sem("g_sq")
        g_sum = sem("g_sum")
        g_root = sem("g_root")
        g_step = sem("g_step")
        g_ready = sem("g_ready")
        ids_ready = sem("ids_ready")
        gathered = sem("gathered")
        embt_tr = sem("embt_tr")
        embt_ready = sem("embt_ready")
        h_mm = sem("h_mm")
        h_saved = sem("h_saved")
        ln1_stats = sem("ln1_stats")
        ln1_var = sem("ln1_var")
        ln1_root = sem("ln1_root")
        ln1_scale = sem("ln1_scale")
        xn1_ready = sem("xn1_ready")
        hb_ready = sem("hb_ready")
        xn1t_tr = sem("xn1t_tr")
        xn1t_ready = sem("xn1t_ready")
        q1_mm = sem("q1_mm")
        kv_mm = sem("kv_mm")
        q1_ready = sem("q1_ready")
        kv0_ready = sem("kv0_ready")
        kv1_ready = sem("kv1_ready")
        vk_mm = sem("vk_mm")
        vk_ready = sem("vk_ready")
        nd_mm = sem("nd_mm")
        den_ready = sem("den_ready")
        rden_ready = sem("rden_ready")
        mix_ready = sem("mix_ready")
        mixt_tr = sem("mixt_tr")
        mixt_ready = sem("mixt_ready")
        proj_mm = sem("proj_mm")
        h1_ready = sem("h1_ready")
        ln2_stats = sem("ln2_stats")
        ln2_var = sem("ln2_var")
        ln2_root = sem("ln2_root")
        ln2_scale = sem("ln2_scale")
        xn2_ready = sem("xn2_ready")
        xn2t_tr = sem("xn2t_tr")
        xn2t_ready = sem("xn2t_ready")
        qk2_mm = sem("qk2_mm")
        qkf_ready = sem("qkf_ready")
        qsq_ready = sem("qsq_ready")
        part0_ready = sem("part0_ready")
        rest_ready = sem("rest_ready")
        part1_ready = sem("part1_ready")
        part2_ready = sem("part2_ready")
        parts_stored = sem("parts_stored")
        v2_mm = sem("v2_mm")
        v2_ready = sem("v2_ready")
        dots_mm = sem("dots_mm")
        dots_ready = sem("dots_ready")
        dott_tr = sem("dott_tr")
        nrm_ready = sem("nrm_ready")
        rnrm_ready = sem("rnrm_ready")
        cos_ready = sem("cos_ready")
        sim_ready = sem("sim_ready")
        ext_ready = sem("ext_ready")
        exta_ready = sem("exta_ready")
        zsum_ready = sem("zsum_ready")
        zall_mm = sem("zall_mm")
        cls_step = sem("cls_step")
        cls_ready = sem("cls_ready")
        clst_tr = sem("clst_tr")
        clst_ready = sem("clst_ready")
        cls_stored = sem("cls_stored")
        st_const = sem("st_const")
        stack_in = [sem(f"stack_in{i}") for i in range(2)]
        qx_ready = [sem(f"qx_ready{i}") for i in range(2)]
        vst_ready = sem("vst_ready")
        resid_ready = sem("resid_ready")
        s1_mm = sem("s1_mm")
        max_ready = sem("max_ready")
        mxt_tr = sem("mxt_tr")
        mhi_ready = sem("mhi_ready")
        mrow_ready = sem("mrow_ready")
        mxr_ready = sem("mxr_ready")
        mrow_in = [sem(f"mrow_in{i}") for i in range(2)]
        img_done = sem("img_done")
        s2_mm = sem("s2_mm")
        ex_ready = sem("ex_ready")
        pv_mm = sem("pv_mm")
        pv_ready = sem("pv_ready")
        tok_tr = sem("tok_tr")
        rsum_ready = sem("rsum_ready")
        tok_ready = sem("tok_ready")
        reg_sum = sem("reg_sum")
        att_ready = sem("att_ready")
        attt_tr = sem("attt_tr")
        attt_ready = sem("attt_ready")
        out_mm = sem("out_mm")
        out_ready = sem("out_ready")
        out_stored = sem("out_stored")

        LOADS = 10

        def wait(eng, s, value):
            if not isinstance(value, int) or value > 0:
                eng.wait_ge(s, value)

        carriers = []

        def wait_apart(eng, s, value):
            eng.wait_ge(s, value)
            if not isinstance(value, int):
                carriers.append(s)
                own = slice(len(carriers), len(carriers) + 1)
                if eng is nc.vector:
                    nc.vector.memset(carry_dve[:, own], 0.0)
                else:
                    nc.gpsimd.tensor_tensor(carry_pool[:, own], carry_pool[:, 0:1], carry_pool[:, 0:1], ALU.add)

        def phase1(eng, body):
            body(-1, False, False, True)
            body(0, True, False, True)
            with eng.Fori(1, NB - 1) as b:
                body(b, True, True, True)
            body(NB - 1, True, True, False)
            body(NB, False, True, False)

        def phase2(eng, body):
            body(-1, 1, False, False, True)
            body(0, 0, True, False, True)
            with eng.Fori(0, NB // 2 - 1) as i:
                body(i * 2 + 1, 1, True, True, True)
                body(i * 2 + 2, 0, True, True, True)
            body(NB - 1, 1, True, True, False)
            body(NB, 0, False, True, False)

        block = ctx.enter_context(nc.Block())

        @block.sync
        def _(sp):
            sp.dma_start(ids[:, :], x).then_inc(loaded, 16)
            sp.dma_start(w_tok[:, :], tok_kernel).then_inc(loaded, 16)
            sp.dma_start(w_aqkv[:, :, :], attn_qkv_t.rearrange("(k p) n -> p k n", p=P)).then_inc(loaded, 16)
            sp.dma_start(w_aproj[:, :, :], attn_proj_t.rearrange("(k p) n -> p k n", p=P)).then_inc(loaded, 16)
            sp.dma_start(b_attn[:, :], attn_bias.unsqueeze(0).to_broadcast([P, C])).then_inc(loaded, 16)
            sp.dma_start(w_fqkv[:, :, :], ffn_qkv.rearrange("(k p) n -> p k n", p=P)).then_inc(loaded, 16)
            sp.dma_start(w_fproj[:, :, :], ffn_proj.rearrange("(k p) n -> p k n", p=P)).then_inc(loaded, 16)
            sp.dma_start(b_ffn[:, :], ffn_bias.unsqueeze(0).to_broadcast([P, C])).then_inc(loaded, 16)
            for k in range(KC):
                sp.dma_start(gvec[:, k:k + 1], ffn_g[0, 0, k * P:(k + 1) * P].unsqueeze(1)).then_inc(loaded, 16)

            def store_parts(p):
                for part, ready in enumerate((part0_ready, part1_ready, part2_ready)):
                    sp.wait_ge(ready, p + 1)
                    for i, (img, which) in enumerate(((q_img, Q_PART), (k_img, K_PART))):
                        for n in range(len(which)):
                            if which[n] == part:
                                for k in range(KC):
                                    dst = img[p, n * FD:(n + 1) * FD, k * HH:(k + 1) * HH, :]
                                    sp.dma_start(dst.rearrange("d h t -> h d t"),
                                                 qk_parts[:, 2 * k + i, part, :]).then_inc(parts_stored, 16)

            with sp.Fori(0, NB) as p:
                store_parts(p)

            def load_stack(b, u, half, rows):
                heads = slice(half * HH, (half + 1) * HH)
                sp.dma_start(q_st[u][0:rows, heads, 0:S], q_img[b, 0:rows, heads, :]).then_inc(stack_in[half], 16)
                sp.dma_start(k_st[u][0:rows, heads, :], k_img[b, 0:rows, heads, :]).then_inc(stack_in[half], 16)

            def load_classes(b, u, half):
                heads = slice(half * HH, (half + 1) * HH)
                for st, c in ((q_st, 0), (k_st, 2)):
                    src = class_dram.rearrange("c (b t) -> b c t", b=NB)[b, c:c + 2, :]
                    sp.dma_start(st[u][ROW_CLASS:ROW_MAX, heads, 0:S],
                                 src.unsqueeze(1).to_broadcast([2, HH, S])).then_inc(stack_in[half], 16)

            def send_max_rows(b, u, half):
                sp.wait_ge(mrow_ready, 2 * b + half + 1)
                for c in range(2):
                    sp.dma_start(q_st[u][ROW_MAX + c:ROW_MAX + c + 1, half * HH:(half + 1) * HH, :],
                                 mrow[:, half, c, :]).then_inc(mrow_in[half], 16)

            sp.wait_ge(st_const, 5)
            sp.wait_ge(parts_stored, 16 + 16 * NSTORE)
            for half in range(2):
                load_stack(0, 0, half, ROW_CLASS)
            sp.wait_ge(clst_ready, 1)
            sp.dma_start(class_dram.rearrange("c (s t) -> (c s) t", t=P), cls_t[:, :]).then_inc(cls_stored, 16)
            sp.wait_ge(cls_stored, 16)
            for half in range(2):
                load_classes(0, 0, half)
            sp.wait_ge(parts_stored, 16 + 16 * NSTORE * NB)
            for half in range(2):
                sp.wait_ge(stack_in[half], 64)
                load_stack(1, 1, half, ROW_CLASS)
                load_classes(1, 1, half)
            for img, c0 in ((q_img, 0), (k_img, 2)):
                for c in range(2):
                    src = class_dram.rearrange("c (b t) -> c b t", b=NB)[c0 + c, 2:NB, :]
                    sp.dma_start(img[2:NB, ROW_CLASS + c, :, :],
                                 src.unsqueeze(1).to_broadcast([NB - 2, FH, S])).then_inc(img_done, 16)

            def body(b, u, cur, prev, nxt, load):
                if cur:
                    send_max_rows(b, u, 1)
                if load:
                    sp.wait_ge(s2_mm, b * FH + HH)
                    sp.wait_ge(img_done, 64)
                    load_stack(b + 2, u, 0, ROW_MAX)
                if nxt:
                    send_max_rows(b + 1, 1 - u, 0)
                if prev:
                    sp.wait_ge(out_ready, b)
                    sp.dma_start(out[b - 1].rearrange("(t p) c -> p t c", p=P),
                                 fin[1 - u][:, :].rearrange("p (t c) -> p t c", t=T)).then_inc(out_stored, 16)
                if load:
                    sp.wait_ge(s2_mm, b * FH + FH)
                if prev and cur:
                    sp.wait_ge(out_stored, b * 16)
                if load:
                    load_stack(b + 2, u, 1, ROW_MAX)

            body(-1, 1, False, False, True, False)
            body(0, 0, True, False, True, True)
            with sp.Fori(0, (NB - 4) // 2) as i:
                body(i * 2 + 1, 1, True, True, True, True)
                body(i * 2 + 2, 0, True, True, True, True)
            body(NB - 3, 1, True, True, True, True)
            body(NB - 2, 0, True, True, True, False)
            body(NB - 1, 1, True, True, False, False)
            body(NB, 0, False, True, False, False)
            sp.wait_ge(out_stored, 16 * NB)

        @block.gpsimd
        def _(pool):
            def gather(n):
                if not isinstance(n, int) or n > 0:
                    wait_apart(pool, gathered, n * 16 * T)
                nc.gpsimd.tensor_copy(ids_now[:, :], ids[:, bass.ds(n * T, T)]).then_inc(ids_ready, 1)
                wait(pool, embt_tr, n)
                wait_apart(pool, ids_ready, n + 1)
                for t in range(T):
                    nc.gpsimd.indirect_dma_start(
                        out=emb[:, t, :], out_offset=None, in_=embeddings,
                        in_offset=bass.IndirectOffsetOnAxis(ap=ids_now[:, t:t + 1].bitcast(U32), axis=0),
                    ).then_inc(gathered, 16)

            nc.gpsimd.memset(carry_pool[:, 0:1], 0.0)
            nc.gpsimd.memset(ident[:, :], 0.0).then_inc(const_pool, 1)
            nc.gpsimd.memset(blk8[:, :, :], 1.0).then_inc(const_pool, 1)
            nc.gpsimd.memset(blk16[:, :, :], 1.0).then_inc(const_pool, 1)
            pool.wait_ge(const_pool, 3)
            nc.gpsimd.affine_select(out=ident[:, :], in_=ident[:, :], compare_op=ALU.not_equal, fill=1.0, base=0,
                                    pattern=[[-1, P]], channel_multiplier=1).then_inc(const_pool, 1)
            nc.gpsimd.memset(quad[:, :], 1.0).then_inc(const_pool, 1)
            nc.gpsimd.memset(reg_row[:, :], 0.0).then_inc(const_pool, 1)
            nc.gpsimd.affine_select(out=blk8[:, :, :], in_=blk8[:, :, :], compare_op=ALU.is_ge, fill=0.0, base=0,
                                    pattern=[[-AD, AH], [0, AD]], channel_multiplier=1).then_inc(const_pool, 1)
            nc.gpsimd.affine_select(out=blk16[:, :, :], in_=blk16[:, :, :], compare_op=ALU.is_ge, fill=0.0, base=0,
                                    pattern=[[-FD, HH], [0, FD]], channel_multiplier=1).then_inc(const_pool, 1)
            pool.wait_ge(const_pool, 8)
            nc.gpsimd.affine_select(out=blk8[:, :, :], in_=blk8[:, :, :], compare_op=ALU.is_ge, fill=0.0, base=AD - 1,
                                    pattern=[[AD, AH], [0, AD]], channel_multiplier=-1).then_inc(const_pool, 1)
            nc.gpsimd.affine_select(out=blk16[:, :, :], in_=blk16[:, :, :], compare_op=ALU.is_ge, fill=0.0,
                                    base=FD - 1, pattern=[[FD, HH], [0, FD]],
                                    channel_multiplier=-1).then_inc(const_pool, 1)
            pool.wait_ge(loaded, 16 * LOADS)
            gather(0)
            nc.gpsimd.affine_select(out=quad[:, :], in_=quad[:, :], compare_op=ALU.is_ge, fill=0.0, base=0,
                                    pattern=[[-32, GH]], channel_multiplier=1).then_inc(const_pool, 1)
            pool.wait_ge(const_pool, 11)
            nc.gpsimd.affine_select(out=quad[:, :], in_=quad[:, :], compare_op=ALU.is_ge, fill=0.0, base=31,
                                    pattern=[[32, GH]], channel_multiplier=-1).then_inc(const_pool, 1)
            for g in range(GH):
                pool.wait_ge(const_pool, 12 + g)
                nc.gpsimd.affine_select(out=reg_row[:, :], in_=reg_row[:, :], compare_op=ALU.not_equal, fill=1.0,
                                        base=-(32 * g + WIN - REG), pattern=[[-1, REG]],
                                        channel_multiplier=1).then_inc(const_pool, 1)

            def body(b, cur, prev, nxt):
                n, p = b + 1, b - 1
                if nxt:
                    pool.wait_ge(xn1_ready, n + 1)
                    nc.gpsimd.tensor_tensor(
                        h_all[:, n, :].rearrange("p (t c) -> p t c", t=T),
                        h_all[:, n, :].rearrange("p (t c) -> p t c", t=T),
                        b_attn[:, :].unsqueeze(1).to_broadcast([P, T, C]), ALU.add).then_inc(hb_ready, 1)
                if cur and nxt:
                    gather_next(n)
                if prev:
                    pool.wait_ge(part1_ready, p + 1)
                    nc.gpsimd.tensor_tensor(qk_parts[:, :, 2, :], qk_rest[:, :, :], qk_parts[:, :, 1, :],
                                            ALU.subtract).then_inc(part2_ready, 1)

            def gather_next(n):
                gather(n + 1)

            body(-1, False, False, True)
            gather(1)
            body(0, True, False, True)
            with pool.Fori(1, NB - 2) as b:
                body(b, True, True, True)
            pool.wait_ge(xn1_ready, NB)
            nc.gpsimd.tensor_tensor(
                h_all[:, NB - 1, :].rearrange("p (t c) -> p t c", t=T),
                h_all[:, NB - 1, :].rearrange("p (t c) -> p t c", t=T),
                b_attn[:, :].unsqueeze(1).to_broadcast([P, T, C]), ALU.add).then_inc(hb_ready, 1)
            for p in range(NB - 3, NB):
                pool.wait_ge(part1_ready, p + 1)
                nc.gpsimd.tensor_tensor(qk_parts[:, :, 2, :], qk_rest[:, :, :], qk_parts[:, :, 1, :],
                                        ALU.subtract).then_inc(part2_ready, 1)

            pool.wait_ge(ext_ready, 2)
            nc.gpsimd.partition_all_reduce(exta[:, :], ext[:, :], P, RMAX).then_inc(exta_ready, 1)

            def fill(b, u):
                for half in range(2):
                    heads = slice(half * HH, (half + 1) * HH)
                    wait_apart(pool, stack_in[half], 64 if isinstance(b, int) and b == 0 else b * 32 + 96)
                    nc.gpsimd.tensor_copy(q_st[u][0:ROW_CLASS, heads, S:NQ],
                                          q_st[u][0:ROW_CLASS, heads, 0:REG]).then_inc(qx_ready[half], 1)
                wait(pool, v2_ready, NB)
                if not isinstance(b, int) or b > 1:
                    wait_apart(pool, pv_mm, b * NG - NG)
                nc.gpsimd.tensor_copy(v_st[u][:, :, :, 0:FD],
                                      v_all[:, b, :].rearrange("p (t h d) -> p t h d", t=T, h=FH)
                                      ).then_inc(vst_ready, 1)
                wait(pool, out_ready, b - 1)
                nc.gpsimd.tensor_tensor(
                    resid[u][:, :].rearrange("p (t c) -> p t c", t=T),
                    h_all[:, b, :].rearrange("p (t c) -> p t c", t=T),
                    b_ffn[:, :].unsqueeze(1).to_broadcast([P, T, C]), ALU.add).then_inc(resid_ready, 1)

            pool.wait_ge(st_const, 5)
            fill(0, 0)
            fill(1, 1)
            with pool.Fori(1, NB // 2) as i:
                fill(i * 2, 0)
                fill(i * 2 + 1, 1)

        @block.scalar
        def _(act):
            act.wait_ge(g_sum, 1)
            nc.scalar.activation(gnrm[:, :], ps[:, 0, 0:KC], ACT.Sqrt).then_inc(g_root, 1)
            act.wait_ge(const_dve, 4)

            def body(b, cur, prev, nxt):
                n, p = b + 1, b - 1
                if cur:
                    act.wait_ge(q1_mm, b + 1)
                    nc.scalar.activation(q1_t[:, :, :], ps[:, 3, :].rearrange("p (k t) -> p k t", k=KC),
                                         ACT.Relu).then_inc(q1_ready, 1)
                    act.wait_ge(kv_mm, b * T + 2)
                    nc.scalar.activation(kv[:, 1, :, 0:P], ps[:, 5, :].rearrange("p (k t) -> p k t", k=4),
                                         ACT.Relu).then_inc(kv1_ready, 1)
                if prev:
                    act.wait_ge(xn2t_tr, p + 1)
                    nc.scalar.activation(xn2_t[:, :, :], ps[:, 2, :].rearrange("p (k t) -> p k t", k=KC),
                                         ACT.Copy).then_inc(xn2t_ready, 1)
                if nxt:
                    act.wait_ge(embt_tr, n + 1)
                    nc.scalar.activation(emb_t[:, :], ps[:, 0, 0:S], ACT.Copy).then_inc(embt_ready, 1)
                    act.wait_ge(h_mm, n + 1)
                    nc.scalar.activation(h_all[:, n, :], ps[:, 1, :], ACT.Copy).then_inc(h_saved, 1)
                    act.wait_ge(ln1_var, n + 1)
                    nc.scalar.activation(sd1[:, :], mv1[:, :, 1], ACT.Sqrt, bias=eps_t[:, 0:1]).then_inc(ln1_root, 1)
                if prev:
                    for i in range(2):
                        act.wait_ge(qk2_mm, p * 2 + i + 1)
                        nc.scalar.activation(qkf[:, :, i, :], ps[:, 6 + i, :].rearrange("p (k t) -> p k t", k=KC),
                                             ACT.Copy).then_inc(qkf_ready, 1)
                    act.wait_ge(qkf_ready, p * 2 + 1)
                    nc.scalar.activation(qsq[:, :, :], qkf[:, :, 0, :], ACT.Square).then_inc(qsq_ready, 1)
                    act.wait_ge(v2_mm, p + 1)
                    nc.scalar.activation(v_all[:, p, :], ps[:, 3, :], ACT.Copy).then_inc(v2_ready, 1)
                    act.wait_ge(rest_ready, p + 1)
                    nc.scalar.activation(qk_parts[:, :, 1, :], qk_rest[:, :, :], ACT.Copy).then_inc(part1_ready, 1)
                    act.wait_ge(dots_mm, p + 1)
                    nc.scalar.activation(dots[:, 0:REG], ps[:, 0, REG:2 * REG], ACT.Copy)
                    nc.scalar.activation(dots[:, REG:S], ps[:, 0, REG:S], ACT.Copy).then_inc(dots_ready, 1)
                if cur:
                    act.wait_ge(mixt_tr, b + 1)
                    nc.scalar.activation(mix_t[:, :, :], ps[:, 2, :].rearrange("p (k t) -> p k t", k=KC),
                                         ACT.Copy).then_inc(mixt_ready, 1)
                if prev:
                    act.wait_ge(dott_tr, p + 1)
                    by = ps[:, 5, 0:T * P].rearrange("p (t g c) -> p t g c", t=T, g=4)
                    nc.scalar.activation(nrm[:, :, :, :], by[:, :, 2:4, 0:HH], ACT.Sqrt).then_inc(nrm_ready, 1)
                if nxt:
                    act.wait_ge(xn1t_tr, n + 1)
                    nc.scalar.activation(xn1_t[:, :, :], ps[:, 2, :].rearrange("p (k t) -> p k t", k=KC),
                                         ACT.Copy).then_inc(xn1t_ready, 1)
                if cur:
                    act.wait_ge(ln2_var, b + 1)
                    nc.scalar.activation(sd2[:, :], mv2[:, :, 1], ACT.Sqrt, bias=eps_t[:, 0:1]).then_inc(ln2_root, 1)

            phase1(act, body)

            act.wait_ge(clst_tr, 1)
            nc.scalar.activation(cls_t[:, :], ps[0:4 * NB * T, 7, 0:P], ACT.Copy).then_inc(clst_ready, 1)

            def group_out(b, u, j):
                act.wait_ge(pv_mm, b * NG + j + 1)
                nc.scalar.activation(pv[u][:, j, :], ps[:, 6, 0:NQ], ACT.Copy).then_inc(pv_ready, 1)

            def body(b, u, cur, prev, nxt):
                for h in range(FH):
                    if cur:
                        j = h // GH
                        act.wait_ge(s2_mm, b * FH + h + 1)
                        if h % GH == 0:
                            wait(act, pv_mm, b * NG + j - 1)
                        nc.scalar.activation(ex[j % 2][:, h % GH, :, :],
                                             ps[:, 2 + 2 * (h % 2):4 + 2 * (h % 2), 0:NQ],
                                             ACT.Exp).then_inc(ex_ready, 1)
                    if prev and h == 3:
                        group_out(b - 1, 1 - u, NG - 1)
                    if cur and h in (6, 10, 14):
                        group_out(b, u, (h - 6) // 4)
                    if prev and h == 12:
                        act.wait_ge(attt_tr, b)
                        nc.scalar.activation(att_t[:, :, :], ps[:, 7, :].rearrange("p (k t) -> p k t", k=KC),
                                             ACT.Copy).then_inc(attt_ready, 1)

            phase2(act, body)

        @block.vector
        def _(dve):
            nc.vector.memset(parts_mark[:, :], 0.0).then_inc(parts_stored, 16)
            nc.vector.memset(ones[:, :], 1.0).then_inc(const_dve, 1)
            nc.vector.memset(eps_t[:, :], LN_EPS).then_inc(const_dve, 1)
            nc.vector.memset(kv[:, :, :, P:P + 1], 1.0).then_inc(const_dve, 1)
            nc.vector.memset(reg_is[:, :], 0.0).then_inc(const_dve, 1)
            dve.wait_ge(const_dve, 4)
            nc.vector.memset(reg_is[0:REG, 0:NB * T:T], 1.0).then_inc(const_dve, 1)
            for u in range(2):
                nc.vector.memset(q_st[u][ROW_CLASS:ROW_MAX, :, S:NQ], 1.0).then_inc(cls_step, 1)
                dve.wait_ge(cls_step, 2 * u + 1)
                nc.vector.memset(q_st[u][ROW_CLASS:ROW_CLASS + 1, :, S:NQ], 0.0).then_inc(st_const, 1)
                nc.vector.memset(k_st[u][ROW_CLASS:ROWS, :, :], 1.0).then_inc(st_const, 1)
                nc.vector.memset(v_st[u][:, :, :, FD:2 * FD], 1.0).then_inc(cls_step, 1)
            nc.vector.memset(mxr[:, :, :, :], 0.0).then_inc(st_const, 1)
            dve.wait_ge(const_pool, 10)
            dve.wait_ge(loaded, 16 * LOADS)
            nc.vector.memset(head_of[:, :], 0.0).then_inc(g_step, 1)
            dve.wait_ge(g_step, 1)
            nc.vector.tensor_copy(head_of[:, 0:HH], blk16[:, :, 0]).then_inc(g_step, 1)
            nc.vector.tensor_tensor(gtmp[:, :], gvec[:, :], gvec[:, :], ALU.mult).then_inc(g_sq, 1)
            nc.vector.tensor_scalar(w_fqkv[:, :, 0:C], w_fqkv[:, :, 0:C], float(FD) ** -0.5, None,
                                    ALU.mult).then_inc(g_step, 1)
            dve.wait_ge(g_root, 1)
            dve.wait_ge(g_sum, 1)
            nc.vector.reciprocal(gtmp[:, :], gnrm[:, :]).then_inc(g_step, 1)
            dve.wait_ge(g_step, 4)
            nc.vector.scalar_tensor_tensor(out=gnrm[:, :], in0=gvec[:, :], scalar=1.0 / FH, in1=gtmp[:, :],
                                           op0=ALU.mult, op1=ALU.mult).then_inc(g_step, 1)
            dve.wait_ge(g_step, 5)
            for k in range(KC):
                nc.vector.tensor_scalar(g_dot[:, k, :], head_of[:, :], gnrm[:, k:k + 1], None,
                                        ALU.mult).then_inc(g_ready, 1)

            def body(b, cur, prev, nxt):
                n, p = b + 1, b - 1
                if cur:
                    dve.wait_ge(kv_mm, b * T + 1)
                    nc.vector.tensor_scalar(kv[:, 0, :, 0:P], ps[:, 4, :].rearrange("p (k t) -> p k t", k=4),
                                            0.0, None, ALU.max).then_inc(kv0_ready, 1)
                    dve.wait_ge(vk_mm, b + 1)
                    prod = ps[:, 3, 0:KC * (P + 1)].rearrange("p (k c) -> p k c", k=KC)
                    nc.vector.tensor_tensor(
                        vk[:, :, 0:P], prod[:, :, 0:P],
                        blk8[:, :, :].rearrange("p h e -> p (h e)").unsqueeze(1).to_broadcast([P, KC, P]), ALU.mult)
                    nc.vector.tensor_tensor(
                        vk[:, :, P:P + AH], prod[:, :, P:P + 1].to_broadcast([P, KC, AH]),
                        blk8[:, :, 0].unsqueeze(1).to_broadcast([P, KC, AH]), ALU.mult).then_inc(vk_ready, 1)
                if nxt:
                    wait_apart(dve, h_saved, n + 1)
                    hv = h_all[:, n, :].rearrange("p (t c) -> p t c", t=T)
                    for t in range(T):
                        nc.vector.bn_stats(bst1[:, t, :], hv[:, t, :]).then_inc(ln1_stats, 1)
                    wait_apart(dve, ln1_stats, n * T + T)
                    for t in range(T):
                        ins = nc.vector.bn_aggr(mv1[:, t, :], bst1[:, t, :])
                    ins.then_inc(ln1_var, 1)
                    dve.wait_ge(ln1_root, n + 1)
                    nc.vector.reciprocal(rs1[:, :], sd1[:, :]).then_inc(ln1_scale, 1)
                    dve.wait_ge(ln1_scale, n + 1)
                    for t in range(T):
                        ins = nc.vector.tensor_scalar(xn1[:, t, :], hv[:, t, :], mv1[:, t, 0:1], rs1[:, t:t + 1],
                                                      ALU.subtract, ALU.mult)
                    ins.then_inc(xn1_ready, 1)
                if prev:
                    dve.wait_ge(qkf_ready, p * 2 + 2)
                    dve.wait_ge(parts_stored, p * (16 * NSTORE) + 16)
                    src = qkf[:, :, :, :].rearrange("p k c t -> p (k c) t")
                    nc.vector.tensor_copy(qk_parts[:, :, 0, :], src).then_inc(part0_ready, 1)
                    dve.wait_ge(part0_ready, p + 1)
                    nc.vector.tensor_tensor(qk_rest[:, :, :], src, qk_parts[:, :, 0, :],
                                            ALU.subtract).then_inc(rest_ready, 1)
                if cur:
                    dve.wait_ge(nd_mm, b + 1)
                    by = ps[:, 4:6, 0:KC * (P + AH)].rearrange("p t (k c) -> p t k c", k=KC)
                    nc.vector.tensor_scalar(den[:, :, :, :], by[:, :, :, P:P + AH], DEN_EPS, None,
                                            ALU.add).then_inc(den_ready, 1)
                    dve.wait_ge(den_ready, b + 1)
                    nc.vector.reciprocal(rden[:, :, :, :], den[:, :, :, :]).then_inc(rden_ready, 1)
                    dve.wait_ge(rden_ready, b + 1)
                    for t in range(T):
                        ins = nc.vector.tensor_tensor(
                            mix[:, t, :, :, :], by[:, t, :, 0:P].rearrange("p k (h e) -> p k h e", h=AH),
                            rden[:, t, :, :].unsqueeze(3).to_broadcast([P, KC, AH, AD]), ALU.mult)
                    ins.then_inc(mix_ready, 1)
                if prev:
                    dve.wait_ge(nrm_ready, p + 1)
                    nc.vector.reciprocal(rnrm[:, :, :, :], nrm[:, :, :, :]).then_inc(rnrm_ready, 1)
                    dve.wait_ge(rnrm_ready, p + 1)
                    sims = ps[:, 5, 0:T * P].rearrange("p (t g c) -> p t g c", t=T, g=4)
                    nc.vector.tensor_tensor(cosb[:, :, :, :], sims[:, :, 0:2, 0:HH], rnrm[:, :, :, :],
                                            ALU.mult).then_inc(cos_ready, 1)
                    dve.wait_ge(cos_ready, p + 1)
                    nc.vector.tensor_reduce(sim_all[:, bass.ds(p * T, T)], cosb[:, :, :, :], axis=AX.XY,
                                            op=ALU.add).then_inc(sim_ready, 1)
                if cur:
                    dve.wait_ge(proj_mm, b + 1)
                    dve.wait_ge(hb_ready, b + 1)
                    nc.vector.tensor_tensor(h_all[:, b, :], ps[:, 4, :], h_all[:, b, :], ALU.add).then_inc(h1_ready, 1)
                    wait_apart(dve, h1_ready, b + 1)
                    h1v = h_all[:, b, :].rearrange("p (t c) -> p t c", t=T)
                    for t in range(T):
                        nc.vector.bn_stats(bst2[:, t, :], h1v[:, t, :]).then_inc(ln2_stats, 1)
                    wait_apart(dve, ln2_stats, b * T + T)
                    for t in range(T):
                        ins = nc.vector.bn_aggr(mv2[:, t, :], bst2[:, t, :])
                    ins.then_inc(ln2_var, 1)
                    dve.wait_ge(ln2_root, b + 1)
                    nc.vector.reciprocal(rs2[:, :], sd2[:, :]).then_inc(ln2_scale, 1)
                    dve.wait_ge(ln2_scale, b + 1)
                    for t in range(T):
                        ins = nc.vector.tensor_scalar(xn2[:, t, :], h1v[:, t, :], mv2[:, t, 0:1], rs2[:, t:t + 1],
                                                      ALU.subtract, ALU.mult)
                    ins.then_inc(xn2_ready, 1)

            phase1(dve, body)

            dve.wait_ge(sim_ready, NB)
            nc.vector.tensor_reduce(ext[:, 0:1], sim_all[:, :], axis=AX.X, op=ALU.max).then_inc(ext_ready, 1)
            nc.vector.tensor_reduce(ext[:, 1:2], sim_all[:, :], axis=AX.X, op=ALU.min,
                                    negate=True).then_inc(ext_ready, 1)
            nc.vector.tensor_reduce(zsum[:, 0:1], sim_all[:, :], axis=AX.X, op=ALU.add).then_inc(cls_step, 1)
            dve.wait_ge(cls_step, 5)
            nc.vector.tensor_scalar(zsum[:, 1:2], zsum[:, 0:1], 0.0, None, ALU.mult).then_inc(zsum_ready, 1)
            dve.wait_ge(exta_ready, 1)
            nc.vector.tensor_tensor(thr[:, 0:1], exta[:, 0:1], exta[:, 1:2], ALU.add).then_inc(cls_step, 1)
            dve.wait_ge(zall_mm, 1)
            dve.wait_ge(cls_step, 6)
            nc.vector.scalar_tensor_tensor(out=thr[:, 1:2], in0=thr[:, 0:1], scalar=0.9, in1=ps[:, 7, 0:1],
                                           op0=ALU.mult, op1=ALU.add).then_inc(cls_step, 1)
            dve.wait_ge(cls_step, 7)
            nc.vector.tensor_scalar(pos[:, :], sim_all[:, :], exta[:, 1:2], thr[:, 1:2], ALU.add,
                                    ALU.is_gt).then_inc(cls_step, 1)
            dve.wait_ge(cls_step, 8)
            nc.vector.tensor_tensor(cls[:, 0, :], pos[:, :], reg_is[:, :], ALU.max).then_inc(cls_step, 1)
            nc.vector.tensor_scalar(neg[:, :], pos[:, :], -1.0, 1.0, ALU.mult, ALU.add).then_inc(cls_step, 1)
            dve.wait_ge(cls_step, 10)
            nc.vector.tensor_tensor(pos[:, :], neg[:, :], reg_is[:, :], ALU.max).then_inc(cls_step, 1)
            nc.vector.tensor_scalar(cls[:, 1, :], cls[:, 0, :], -1.0, 1.0, ALU.mult, ALU.add)
            nc.vector.tensor_scalar(cls[:, 2, :], cls[:, 0, :], -1.0, BIG, ALU.add, ALU.mult)
            dve.wait_ge(cls_step, 11)
            nc.vector.tensor_scalar(cls[:, 3, :], pos[:, :], -1.0, BIG, ALU.add, ALU.mult).then_inc(cls_ready, 1)

            def split_max(b, half):
                dve.wait_ge(mxt_tr, b * 2 + half + 1)
                wait(dve, mrow_in[half], b * 32)
                nc.vector.tensor_scalar(mrow[:, half, 0, :], ps[0:HH, 7, 0:NQ], -1.0, None,
                                        ALU.mult).then_inc(mhi_ready, 1)
                dve.wait_ge(mhi_ready, b * 2 + half + 1)
                nc.vector.scalar_tensor_tensor(out=mrow[:, half, 1, :], in0=ps[0:HH, 7, 0:NQ], scalar=-1.0,
                                               in1=mrow[:, half, 0, :], op0=ALU.mult,
                                               op1=ALU.subtract).then_inc(mrow_ready, 1)

            def max_of(b, v, half, to):
                dve.wait_ge(s1_mm, b * UNITS + v + 1)
                if v % (HH + 1) == 0:
                    wait(dve, mxt_tr, b * 2 + half - 1)
                nc.vector.tensor_reduce(to, ps[:, v % 2, :].rearrange("p (t q) -> p t q", t=2), axis=AX.X,
                                        op=ALU.max).then_inc(max_ready, 1)

            def normalise(b, what):
                rows, dst, rs = ((P, att[:, 0], rsum), (P, att[:, 1], rsum), (REG, attx[:, :, :], rsumx))[what]
                by = ps[0:rows, 7, :].rearrange("p (h c) -> p h c", h=FH)
                dve.wait_ge(tok_tr, b * 3 + what + 1)
                nc.vector.reciprocal(rs[:, :], by[:, :, FD]).then_inc(rsum_ready, 1)
                dve.wait_ge(rsum_ready, b * 3 + what + 1)
                nc.vector.tensor_tensor(dst, by[:, :, 0:FD], rs[:, :].unsqueeze(2).to_broadcast([rows, FH, FD]),
                                        ALU.mult).then_inc(tok_ready, 1)

            def body(b, u, cur, prev, nxt):
                for h in range(FH):
                    half, hh = h // HH, h % HH
                    if nxt:
                        max_of(b + 1, h + half, half, mx[:, half, hh:hh + HH + 1:HH])
                        if hh == HH - 1:
                            max_of(b + 1, h + half + 1, half, mx[:, half, 2 * HH:2 * HH + 2])
                            dve.wait_ge(max_ready, b * UNITS + UNITS + (HH + 1) * (half + 1))
                            nc.vector.tensor_tensor(
                                mxr[:, half, :, :],
                                mx[:, half, 2 * HH:2 * HH + 2].unsqueeze(2).to_broadcast([P, HH // GH, GH]),
                                quad[:, :].unsqueeze(1).to_broadcast([P, HH // GH, GH]),
                                ALU.mult).then_inc(mxr_ready, 1)
                    if cur and h == 1:
                        split_max(b, 1)
                    if prev and h == 4:
                        normalise(b - 1, 0)
                    if prev and h == 6:
                        normalise(b - 1, 1)
                    if prev and h == 8:
                        normalise(b - 1, 2)
                        dve.wait_ge(tok_ready, b * 3)
                        nc.vector.tensor_tensor(att[0:REG, 0], att[0:REG, 0], attx[:, :, :],
                                                ALU.add).then_inc(reg_sum, 1)
                        dve.wait_ge(reg_sum, b)
                        nc.vector.tensor_scalar(att[0:REG, 0], att[0:REG, 0], 0.5, None,
                                                ALU.mult).then_inc(att_ready, 1)
                    if nxt and h == 10:
                        split_max(b + 1, 0)
                    if prev and h == 13:
                        dve.wait_ge(out_mm, b)
                        dve.wait_ge(resid_ready, b)
                        if not cur and not nxt:
                            dve.wait_ge(out_stored, 16 * (NB - 2))
                        nc.vector.tensor_tensor(fin[1 - u][:, :], ps[:, 7, :], resid[1 - u][:, :],
                                                ALU.add).then_inc(out_ready, 1)

            phase2(dve, body)

        @block.tensor
        def _(pe):
            mm = nc.tensor.matmul
            pe.wait_ge(const_pool, 10)
            pe.wait_ge(g_sq, 1)
            mm(ps[:, 0, 0:KC], blk16[:, :, :].rearrange("p h d -> p (h d)"), gtmp[:, :],
               start=True, stop=True).then_inc(g_sum, 1)
            pe.wait_ge(loaded, 16 * LOADS)
            pe.wait_ge(g_root, 1)

            def to_channels(src, bank):
                for k in range(KC):
                    for t in range(T):
                        ins = nc.tensor.transpose(ps[:, bank, k * S + t * P:k * S + (t + 1) * P],
                                                  src[:, t, k * P:(k + 1) * P], ident[:, :])
                return ins

            def body(b, cur, prev, nxt):
                n, p = b + 1, b - 1
                if cur:
                    pe.wait_ge(xn1t_ready, b + 1)
                    for m in range(KC):
                        for k in range(KC):
                            ins = mm(ps[:, 3, m * S:(m + 1) * S], w_aqkv[:, k, m * P:(m + 1) * P], xn1_t[:, k, :],
                                     start=(k == 0), stop=(k == KC - 1))
                    ins.then_inc(q1_mm, 1)
                    wait(pe, h1_ready, b)
                    for t in range(T):
                        for k in range(KC):
                            ins = mm(ps[:, 4 + t, :], xn1_t[:, k, t * P:(t + 1) * P], w_aqkv[:, k, C:3 * C],
                                     start=(k == 0), stop=(k == KC - 1))
                        ins.then_inc(kv_mm, 1)
                if prev:
                    pe.wait_ge(xn2_ready, p + 1)
                    pe.wait_ge(xn1t_ready, NB if not nxt and not cur else n)
                    to_channels(xn2, 2).then_inc(xn2t_tr, 1)
                if nxt:
                    pe.wait_ge(gathered, n * (16 * T) + 16 * T)
                    for t in range(T):
                        ins = nc.tensor.transpose(ps[:, 0, t * P:(t + 1) * P], emb[:, t, :], ident[:, :])
                    ins.then_inc(embt_tr, 1)
                if cur:
                    pe.wait_ge(kv0_ready, b + 1)
                    pe.wait_ge(kv1_ready, b + 1)
                    pe.wait_ge(q1_ready, b + 1)
                    for k in range(KC):
                        for t in range(T):
                            ins = mm(ps[:, 3, k * (P + 1):(k + 1) * (P + 1)], kv[:, t, k, 0:P], kv[:, t, KC + k, :],
                                     start=(t == 0), stop=(t == T - 1))
                    ins.then_inc(vk_mm, 1)
                if nxt:
                    pe.wait_ge(embt_ready, n + 1)
                    wait(pe, h_saved, n)
                    for t in range(T):
                        ins = mm(ps[:, 1, t * C:(t + 1) * C], emb_t[:, t * P:(t + 1) * P], w_tok[:, :],
                                 start=True, stop=True)
                    ins.then_inc(h_mm, 1)
                if prev:
                    pe.wait_ge(xn2t_ready, p + 1)
                    wait(pe, g_step, 3)
                    for i in range(2):
                        for m in range(KC):
                            for k in range(KC):
                                ins = mm(ps[:, 6 + i, m * S:(m + 1) * S],
                                         w_fqkv[:, k, i * C + m * P:i * C + (m + 1) * P], xn2_t[:, k, :],
                                         start=(k == 0), stop=(k == KC - 1))
                        ins.then_inc(qk2_mm, 1)
                if cur:
                    pe.wait_ge(vk_ready, b + 1)
                    for t in range(T):
                        for k in range(KC):
                            ins = mm(ps[:, 4 + t, k * (P + AH):(k + 1) * (P + AH)], q1_t[:, k, t * P:(t + 1) * P],
                                     vk[:, k, :], start=True, stop=True)
                    ins.then_inc(nd_mm, 1)
                if prev:
                    if cur:
                        pe.wait_ge(vk_ready, b + 1)
                    for t in range(T):
                        for k in range(KC):
                            ins = mm(ps[:, 3, t * C:(t + 1) * C], xn2_t[:, k, t * P:(t + 1) * P],
                                     w_fqkv[:, k, 2 * C:3 * C], start=(k == 0), stop=(k == KC - 1))
                    ins.then_inc(v2_mm, 1)
                    pe.wait_ge(qsq_ready, p + 1)
                    pe.wait_ge(g_ready, KC)
                    for g in range(4):
                        w = g_dot[:, g, :] if g < KC else head_of[:, :]
                        r = qkf[:, g, 0, :] if g < KC else qsq[:, g - KC, :]
                        ins = mm(ps[32 * g:32 * g + 32, 0, 0:S], w, r, start=True, stop=True)
                    ins.then_inc(dots_mm, 1)
                if cur:
                    pe.wait_ge(mix_ready, b + 1)
                    if prev:
                        pe.wait_ge(xn2t_ready, p + 1)
                    to_channels(mix[:, :, :, :, :].rearrange("p t k h e -> p t (k h e)"), 2).then_inc(mixt_tr, 1)
                if prev:
                    pe.wait_ge(dots_ready, p + 1)
                    for t in range(T):
                        ins = nc.tensor.transpose(ps[:, 5, t * P:(t + 1) * P], dots[:, t * P:(t + 1) * P], ident[:, :])
                    ins.then_inc(dott_tr, 1)
                if cur:
                    pe.wait_ge(mixt_ready, b + 1)
                    for t in range(T):
                        for k in range(KC):
                            ins = mm(ps[:, 4, t * C:(t + 1) * C], mix_t[:, k, t * P:(t + 1) * P], w_aproj[:, k, :],
                                     start=(k == 0), stop=(k == KC - 1))
                    ins.then_inc(proj_mm, 1)
                if nxt:
                    pe.wait_ge(xn1_ready, n + 1)
                    to_channels(xn1, 2).then_inc(xn1t_tr, 1)

            phase1(pe, body)
            pe.wait_ge(const_pool, 12 + GH)

            pe.wait_ge(zsum_ready, 1)
            pe.wait_ge(qkf_ready, 2 * NB)
            mm(ps[:, 7, 0:1], ones[:, :], zsum[:, 1:2], start=True, stop=True).then_inc(zall_mm, 1)
            pe.wait_ge(cls_ready, 1)
            nc.tensor.transpose(ps[0:4 * NB * T, 7, 0:P], cls[:, :, :].rearrange("p c s -> p (c s)"),
                                ident[:, :]).then_inc(clst_tr, 1)
            pe.wait_ge(clst_ready, 1)
            pe.wait_ge(v2_ready, NB)
            pe.wait_ge(dots_ready, NB)
            pe.wait_ge(cos_ready, NB)
            pe.wait_ge(h1_ready, NB)

            def send_max(b, half):
                pe.wait_ge(mxr_ready, b * 2 + half + 1)
                for t in range(T):
                    nc.tensor.transpose(ps[0:HH, 7, t * P:(t + 1) * P], mx[:, half, t * HH:(t + 1) * HH],
                                        ident[:, :])
                mm(ps[0:HH, 7, S:NQ], mxr[:, half, :, :].rearrange("p j g -> p (j g)"), reg_row[:, :],
                   start=True, stop=True).then_inc(mxt_tr, 1)

            def group(b, u, j):
                pe.wait_ge(ex_ready, b * FH + GH * (j + 1))
                pe.wait_ge(vst_ready, b + 1)
                wait(pe, pv_ready, b * NG + j)
                for t in range(T):
                    for g in range(GH):
                        ins = mm(ps[32 * g:32 * g + 32, 6, 0:NQ], v_st[u][:, t, GH * j + g, :],
                                 ex[j % 2][:, g, t, :], start=(t == 0), stop=(t == T - 1))
                ins.then_inc(pv_mm, 1)

            def to_tokens(u, q0, nq):
                for j in range(NG):
                    ins = nc.tensor.transpose(ps[0:nq, 7, j * P:(j + 1) * P], pv[u][:, j, q0:q0 + nq], ident[:, :])
                ins.then_inc(tok_tr, 1)

            def body(b, u, cur, prev, nxt):
                o = 1 - u
                for h in range(FH):
                    half = h // HH
                    if cur:
                        if h % HH == 0:
                            pe.wait_ge(mrow_in[half], b * 32 + 32)
                        wait(pe, ex_ready, b * FH + h - 1)
                        for t in range(T):
                            ins = mm(ps[:, 2 + 2 * (h % 2) + t, 0:NQ], k_st[u][:, h, t * P:(t + 1) * P],
                                     q_st[u][:, h, :], start=True, stop=True)
                        ins.then_inc(s2_mm, 1)
                    if nxt:
                        v = h + half
                        if h % HH == 0:
                            pe.wait_ge(qx_ready[half], b + 2)
                        wait(pe, max_ready, b * UNITS + UNITS + v - 1)
                        for t in range(T):
                            ins = mm(ps[:, v % 2, t * S:(t + 1) * S], q_st[o][0:ROW_MAX, h, t * P:(t + 1) * P],
                                     k_st[o][0:ROW_MAX, h, :], start=True, stop=True)
                        ins.then_inc(s1_mm, 1)
                        if h % HH == HH - 1:
                            v = v + 1
                            wait(pe, max_ready, b * UNITS + UNITS + v - 1)
                            for j in range(HH // GH):
                                for g in range(GH):
                                    ins = mm(ps[32 * g:32 * g + 32, v % 2, j * S:(j + 1) * S],
                                             q_st[o][0:ROW_MAX, half * HH + j * GH + g, NQ - WIN:NQ],
                                             k_st[o][0:ROW_MAX, half * HH + j * GH + g, :],
                                             start=True, stop=True)
                            ins.then_inc(s1_mm, 1)
                    if cur and h == 1:
                        send_max(b, 1)
                    if prev and h == 2:
                        group(b - 1, o, NG - 1)
                    if prev and h == 4:
                        pe.wait_ge(pv_ready, b * NG)
                        if cur:
                            pe.wait_ge(mrow_ready, b * 2 + 2)
                        else:
                            pe.wait_ge(out_ready, b - 1)
                        to_tokens(o, 0, P)
                    if cur and h == 5:
                        group(b, u, 0)
                    if prev and h == 6:
                        pe.wait_ge(tok_ready, b * 3 - 2)
                        to_tokens(o, P, P)
                    if prev and h == 8:
                        pe.wait_ge(tok_ready, b * 3 - 1)
                        to_tokens(o, S, REG)
                    if cur and h == 9:
                        group(b, u, 1)
                    if nxt and h == 10:
                        if prev:
                            pe.wait_ge(tok_ready, b * 3)
                        elif cur:
                            pe.wait_ge(mrow_ready, 2)
                        send_max(b + 1, 0)
                    if prev and h == 11:
                        pe.wait_ge(att_ready, b)
                        if nxt:
                            pe.wait_ge(mrow_ready, b * 2 + 3)
                        to_channels(att[:, :, :, :].rearrange("p t h d -> p t (h d)"), 7).then_inc(attt_tr, 1)
                    if prev and h == 13:
                        pe.wait_ge(attt_ready, b)
                        for t in range(T):
                            for k in range(KC):
                                ins = mm(ps[:, 7, t * C:(t + 1) * C], att_t[:, k, t * P:(t + 1) * P],
                                         w_fproj[:, k, :], start=(k == 0), stop=(k == KC - 1))
                        ins.then_inc(out_mm, 1)
                    if cur and h == 13:
                        group(b, u, 2)

            phase2(pe, body)


def kernel(x, L0_tok_embeddings, L0_tok_project_kernel, L0_attn_qkv_weight, L0_attn_proj_weight,
           L0_attn_proj_bias, L0_ffn_g_info, L0_ffn_W_qkv, L0_ffn_W_proj, L0_ffn_b_proj):
    import numpy as np
    import concourse.bacc as bacc
    from concourse import mybir as mb
    from concourse.bass_utils import run_bass_kernel_spmd

    x = np.asarray(x)
    arrays = {
        "ids": np.ascontiguousarray(x.reshape(-1, P).T),
        "embeddings": np.ascontiguousarray(L0_tok_embeddings),
        "tok_kernel": np.ascontiguousarray(L0_tok_project_kernel),
        "attn_qkv_t": np.ascontiguousarray(np.asarray(L0_attn_qkv_weight).T),
        "attn_proj_t": np.ascontiguousarray(np.asarray(L0_attn_proj_weight).T),
        "attn_bias": np.ascontiguousarray(L0_attn_proj_bias),
        "ffn_g": np.ascontiguousarray(L0_ffn_g_info),
        "ffn_qkv": np.ascontiguousarray(L0_ffn_W_qkv),
        "ffn_proj": np.ascontiguousarray(L0_ffn_W_proj),
        "ffn_bias": np.ascontiguousarray(L0_ffn_b_proj),
    }
    nc = bacc.Bacc("TRN2", target_bir_lowering=False, num_devices=1)
    args = [nc.dram_tensor("in_" + n, a.shape, mb.dt.from_np(a.dtype), kind="ExternalInput").ap()
            for n, a in arrays.items()]
    out = nc.dram_tensor("out", (*x.shape, arrays["tok_kernel"].shape[1]), F32, kind="ExternalOutput").ap()
    lm_tower(nc, *args, out)
    r = run_bass_kernel_spmd(nc, [{"in_" + n: a for n, a in arrays.items()}], core_ids=[0])
    return r.results[0]["out"]
```

```python
from contextlib import ExitStack

import concourse.bass as bass
from concourse import mybir

F32 = mybir.dt.float32
BF16 = mybir.dt.bfloat16
I32 = mybir.dt.int32
U32 = mybir.dt.uint32
ALU = mybir.AluOpType
ACT = mybir.ActivationFunctionType
AX = mybir.AxisListType
RMAX = bass.bass_isa.ReduceOp.max

P = 128
LN_EPS = 1e-5
DEN_EPS = 1e-15
BIG = 1e30


def lm_tower(nc, x, embeddings, tok_kernel, attn_qkv_t, attn_proj_t, attn_bias,
             ffn_g, ffn_qkv, ffn_proj, ffn_bias, out):
    NB, S = 8, 256
    assert tuple(x.shape) == (P, NB * S // P)
    C = tok_kernel.shape[1]
    VOCAB = embeddings.shape[0]
    T = S // P
    KC = C // P
    AD = 8
    AH = P // AD
    FD = 16
    FH = C // FD
    HH = FH // 2
    REG = 5
    NQ = S + REG
    PARTS = 3
    Q_PART = (0, 0, 0, 1, 1, 2)
    K_PART = (0, 1, 2, 0, 1, 0)
    ROW_CLASS = FD * len(Q_PART)
    ROW_MAX = ROW_CLASS + 2
    ROWS = ROW_MAX + 2
    NSTORE = 4 * len(Q_PART)
    GH = 4
    NG = FH // GH
    UNITS = FH + 2
    WIN = 32

    q_img = nc.dram_tensor("q_image", [NB, ROW_MAX, FH, S], BF16).ap()
    k_img = nc.dram_tensor("k_image", [NB, ROW_MAX, FH, S], BF16).ap()
    class_dram = nc.dram_tensor("class_rows", [4, NB * S], BF16).ap()

    with ExitStack() as ctx:
        def sb(name, shape, dt=F32):
            return ctx.enter_context(nc.sbuf_tensor(name, shape, dt))

        def sem(name):
            return ctx.enter_context(nc.semaphore(name))

        ps = ctx.enter_context(nc.psum_tensor("ps", [P, 8, 512], F32))

        ident = sb("ident", [P, P])
        ones = sb("ones", [P, P])
        blk8 = sb("blk8", [P, AH, AD])
        blk16 = sb("blk16", [P, HH, FD])
        head_of = sb("head_of", [P, 32])
        g_dot = sb("g_dot", [P, KC, 32])
        reg_is = sb("reg_is", [P, NB * T])
        quad = sb("quad", [P, GH])
        reg_row = sb("reg_row", [P, REG])
        eps_t = sb("eps_t", [P, 1])
        gvec = sb("gvec", [P, KC])
        parts_mark = sb("parts_mark", [1, 1])
        carry_dve = sb("carry_dve", [P, 32])
        carry_pool = sb("carry_pool", [P, 32])
        gtmp = sb("gtmp", [P, KC])
        gnrm = sb("gnrm", [P, KC])
        w_tok = sb("w_tok", [P, C])
        w_aqkv = sb("w_aqkv", [P, KC, 3 * C])
        w_aproj = sb("w_aproj", [P, KC, C])
        w_fqkv = sb("w_fqkv", [P, KC, 3 * C])
        w_fproj = sb("w_fproj", [P, KC, C])
        b_attn = sb("b_attn", [P, C])
        b_ffn = sb("b_ffn", [P, C])
        ids = sb("ids", [P, NB * T], I32)
        ids_now = sb("ids_now", [P, T], I32)
        emb = sb("emb", [P, T, P])
        emb_t = sb("emb_t", [P, S])
        h_all = sb("h_all", [P, NB, T * C])
        v_all = sb("v_all", [P, NB, T * C])
        sim_all = sb("sim_all", [P, NB * T])
        bst1 = sb("bst1", [P, T, 6])
        mv1 = sb("mv1", [P, T, 2])
        sd1 = sb("sd1", [P, T])
        rs1 = sb("rs1", [P, T])
        xn1 = sb("xn1", [P, T, C])
        xn1_t = sb("xn1_t", [P, KC, S])
        q1_t = sb("q1_t", [P, KC, S])
        kv = sb("kv", [P, T, 4, P + 1])
        vk = sb("vk", [P, KC, P + AH])
        den = sb("den", [P, T, KC, AH])
        rden = sb("rden", [P, T, KC, AH])
        mix = sb("mix", [P, T, KC, AH, AD])
        mix_t = sb("mix_t", [P, KC, S])
        bst2 = sb("bst2", [P, T, 6])
        mv2 = sb("mv2", [P, T, 2])
        sd2 = sb("sd2", [P, T])
        rs2 = sb("rs2", [P, T])
        xn2 = sb("xn2", [P, T, C])
        xn2_t = sb("xn2_t", [P, KC, S])
        qkf = sb("qkf", [P, KC, 2, S])
        qsq = sb("qsq", [P, KC, S])
        qk_parts = sb("qk_parts", [P, KC * 2, PARTS, S], BF16)
        qk_rest = sb("qk_rest", [P, KC * 2, S])
        dots = sb("dots", [P, S])
        nrm = sb("nrm", [P, T, KC, HH])
        rnrm = sb("rnrm", [P, T, KC, HH])
        cosb = sb("cosb", [P, T, KC, HH])
        ext = sb("ext", [P, 2])
        exta = sb("exta", [P, 2])
        zsum = sb("zsum", [P, 2])
        thr = sb("thr", [P, 2])
        pos = sb("pos", [P, NB * T])
        neg = sb("neg", [P, NB * T])
        cls = sb("cls", [P, 4, NB * T])
        cls_t = sb("cls_t", [4 * NB * T, P], BF16)
        q_st = [sb(f"q_st{u}", [ROWS, FH, NQ], BF16) for u in range(2)]
        k_st = [sb(f"k_st{u}", [ROWS, FH, S], BF16) for u in range(2)]
        v_st = [sb(f"v_st{u}", [P, T, FH, 2 * FD]) for u in range(2)]
        mx = sb("mx", [P, 2, 2 * HH + 2])
        mxr = sb("mxr", [P, 2, HH // GH, GH])
        mneg = sb("mneg", [HH, 2, NQ])
        mrow = sb("mrow", [HH, 2, 2, NQ], BF16)
        ex = [sb(f"ex{u}", [P, GH, T, NQ]) for u in range(2)]
        pv = [sb(f"pv{u}", [P, NG, NQ]) for u in range(2)]
        rsum = sb("rsum", [P, FH])
        rsumx = sb("rsumx", [REG, FH])
        att = sb("att", [P, T, FH, FD])
        halves_t = sb("halves_t", [REG, 1])
        attx = sb("attx", [REG, FH, FD])
        att_t = sb("att_t", [P, KC, S])
        resid = [sb(f"resid{u}", [P, T * C]) for u in range(2)]
        raw = sb("raw", [P, T * C])
        fin = [sb(f"fin{u}", [P, T * C]) for u in range(2)]

        loaded = sem("loaded")
        const_pool = sem("const_pool")
        const_dve = sem("const_dve")
        g_sq = sem("g_sq")
        g_sum = sem("g_sum")
        g_root = sem("g_root")
        g_step = sem("g_step")
        g_ready = sem("g_ready")
        ids_loaded = sem("ids_loaded")
        ids_ready = sem("ids_ready")
        gathered = sem("gathered")
        embt_tr = sem("embt_tr")
        embt_ready = sem("embt_ready")
        h_mm = sem("h_mm")
        h_saved = sem("h_saved")
        ln1_stats = sem("ln1_stats")
        ln1_var = sem("ln1_var")
        ln1_root = sem("ln1_root")
        ln1_scale = sem("ln1_scale")
        xn1_ready = sem("xn1_ready")
        hb_ready = sem("hb_ready")
        xn1t_tr = sem("xn1t_tr")
        xn1t_ready = sem("xn1t_ready")
        q1_mm = sem("q1_mm")
        kv_mm = sem("kv_mm")
        q1_ready = sem("q1_ready")
        kv0_ready = sem("kv0_ready")
        kv1_ready = sem("kv1_ready")
        vk_mm = sem("vk_mm")
        vk_ready = sem("vk_ready")
        nd_mm = sem("nd_mm")
        den_ready = sem("den_ready")
        rden_ready = sem("rden_ready")
        mix_ready = sem("mix_ready")
        mixt_tr = sem("mixt_tr")
        mixt_ready = sem("mixt_ready")
        proj_mm = sem("proj_mm")
        h1_ready = sem("h1_ready")
        ln2_stats = sem("ln2_stats")
        ln2_var = sem("ln2_var")
        ln2_root = sem("ln2_root")
        ln2_scale = sem("ln2_scale")
        xn2_ready = sem("xn2_ready")
        xn2t_tr = sem("xn2t_tr")
        xn2t_ready = sem("xn2t_ready")
        qk2_mm = sem("qk2_mm")
        qkf_ready = sem("qkf_ready")
        qsq_ready = sem("qsq_ready")
        part0_ready = sem("part0_ready")
        rest_ready = sem("rest_ready")
        part1_ready = sem("part1_ready")
        part2_ready = sem("part2_ready")
        parts_stored = sem("parts_stored")
        v2_mm = sem("v2_mm")
        v2_ready = sem("v2_ready")
        dots_mm = sem("dots_mm")
        dots_ready = sem("dots_ready")
        dott_tr = sem("dott_tr")
        nrm_ready = sem("nrm_ready")
        rnrm_ready = sem("rnrm_ready")
        cos_ready = sem("cos_ready")
        sim_ready = sem("sim_ready")
        ext_ready = sem("ext_ready")
        exta_ready = sem("exta_ready")
        zsum_ready = sem("zsum_ready")
        zall_mm = sem("zall_mm")
        cls_step = sem("cls_step")
        cls_ready = sem("cls_ready")
        clst_tr = sem("clst_tr")
        clst_ready = sem("clst_ready")
        cls_stored = sem("cls_stored")
        st_const = sem("st_const")
        stack_in = [sem(f"stack_in{i}") for i in range(2)]
        class_in = [sem(f"class_in{b}") for b in range(2)]
        qx_ready = [sem(f"qx_ready{i}") for i in range(2)]
        vst_ready = sem("vst_ready")
        resid_ready = sem("resid_ready")
        s1_mm = sem("s1_mm")
        max_ready = sem("max_ready")
        mxt_tr = sem("mxt_tr")
        mhi_ready = sem("mhi_ready")
        raw_ready = sem("raw_ready")
        mrow_ready = sem("mrow_ready")
        mxr_ready = sem("mxr_ready")
        mrow_in = [sem(f"mrow_in{i}") for i in range(2)]
        img_done = sem("img_done")
        s2_mm = sem("s2_mm")
        ex_ready = sem("ex_ready")
        pv_mm = sem("pv_mm")
        pv_ready = sem("pv_ready")
        tok_tr = sem("tok_tr")
        rsum_ready = sem("rsum_ready")
        tok_ready = sem("tok_ready")
        reg_sum = sem("reg_sum")
        att_ready = sem("att_ready")
        attt_tr = sem("attt_tr")
        attt_ready = sem("attt_ready")
        out_mm = sem("out_mm")
        out_ready = sem("out_ready")
        out_stored = sem("out_stored")

        LOADS = 7 + KC

        def wait(eng, s, value):
            if not isinstance(value, int) or value > 0:
                eng.wait_ge(s, value)

        carriers = []

        def wait_apart(eng, s, value):
            eng.wait_ge(s, value)
            if not isinstance(value, int):
                carriers.append(s)
                own = slice(len(carriers), len(carriers) + 1)
                if eng is nc.vector:
                    nc.vector.memset(carry_dve[:, own], 0.0)
                else:
                    nc.gpsimd.tensor_tensor(carry_pool[:, own], carry_pool[:, 0:1], carry_pool[:, 0:1], ALU.add)

        def phase1(eng, body):
            body(-1, False, False, True)
            body(0, True, False, True)
            with eng.Fori(1, NB - 1) as b:
                body(b, True, True, True)
            body(NB - 1, True, True, False)
            body(NB, False, True, False)

        def phase2(eng, body):
            body(-1, 1, False, False, True)
            body(0, 0, True, False, True)
            with eng.Fori(0, NB // 2 - 1) as i:
                body(i * 2 + 1, 1, True, True, True)
                body(i * 2 + 2, 0, True, True, True)
            body(NB - 1, 1, True, True, False)
            body(NB, 0, False, True, False)

        def load_classes(eng, b, u):
            for st, c in ((q_st, 0), (k_st, 2)):
                src = class_dram.rearrange("c (b t) -> b c t", b=NB)[b, c:c + 2, :]
                eng.dma_start(st[u][ROW_CLASS:ROW_MAX, :, 0:S],
                              src.unsqueeze(1).to_broadcast([2, FH, S])).then_inc(class_in[b], 16)

        block = ctx.enter_context(nc.Block())

        @block.sync
        def _(sp):
            sp.dma_start(ids[:, :], x).then_inc(ids_loaded, 16)
            sp.dma_start(w_tok[:, :], tok_kernel).then_inc(loaded, 16)
            sp.dma_start(w_aqkv[:, :, :], attn_qkv_t.rearrange("(k p) n -> p k n", p=P)).then_inc(loaded, 16)
            sp.dma_start(w_aproj[:, :, :], attn_proj_t.rearrange("(k p) n -> p k n", p=P)).then_inc(loaded, 16)
            sp.dma_start(b_attn[:, :], attn_bias.unsqueeze(0).to_broadcast([P, C])).then_inc(loaded, 16)
            sp.dma_start(w_fqkv[:, :, :], ffn_qkv.rearrange("(k p) n -> p k n", p=P)).then_inc(loaded, 16)
            sp.dma_start(w_fproj[:, :, :], ffn_proj.rearrange("(k p) n -> p k n", p=P)).then_inc(loaded, 16)
            sp.dma_start(b_ffn[:, :], ffn_bias.unsqueeze(0).to_broadcast([P, C])).then_inc(loaded, 16)
            for k in range(KC):
                sp.dma_start(gvec[:, k:k + 1], ffn_g[0, 0, k * P:(k + 1) * P].unsqueeze(1)).then_inc(loaded, 16)

            def store_parts(p):
                for part, ready in enumerate((part0_ready, part1_ready, part2_ready)):
                    sp.wait_ge(ready, p + 1)
                    for i, (img, which) in enumerate(((q_img, Q_PART), (k_img, K_PART))):
                        for n in range(len(which)):
                            if which[n] == part:
                                for k in range(KC):
                                    dst = img[p, n * FD:(n + 1) * FD, k * HH:(k + 1) * HH, :]
                                    sp.dma_start(dst.rearrange("d h t -> h d t"),
                                                 qk_parts[:, 2 * k + i, part, :]).then_inc(parts_stored, 16)

            with sp.Fori(0, NB - 1) as p:
                store_parts(p)

            def load_stack(b, u, half, rows):
                heads = slice(half * HH, (half + 1) * HH)
                sp.dma_start(q_st[u][0:rows, heads, 0:S], q_img[b, 0:rows, heads, :]).then_inc(stack_in[half], 16)
                sp.dma_start(k_st[u][0:rows, heads, :], k_img[b, 0:rows, heads, :]).then_inc(stack_in[half], 16)

            def send_max_rows(b, u, half):
                for c, ready in enumerate((mhi_ready, mrow_ready)):
                    sp.wait_ge(ready, 2 * b + half + 1)
                    sp.dma_start(q_st[u][ROW_MAX + c:ROW_MAX + c + 1, half * HH:(half + 1) * HH, :],
                                 mrow[:, half, c, :]).then_inc(mrow_in[half], 16)

            sp.wait_ge(st_const, 5)
            sp.wait_ge(parts_stored, 16 + 16 * NSTORE * 2)
            for half in range(2):
                load_stack(0, 0, half, ROW_CLASS)
            store_parts(NB - 1)
            for half in range(2):
                sp.wait_ge(stack_in[half], 32)
                load_stack(1, 1, half, ROW_CLASS)
            sp.wait_ge(parts_stored, 16 + 16 * NSTORE * NB)
            sp.wait_ge(cls_stored, 16)
            load_classes(sp, 1, 1)
            for img, c0 in ((q_img, 0), (k_img, 2)):
                for c in range(2):
                    src = class_dram.rearrange("c (b t) -> c b t", b=NB)[c0 + c, 2:NB, :]
                    sp.dma_start(img[2:NB, ROW_CLASS + c, :, :],
                                 src.unsqueeze(1).to_broadcast([NB - 2, FH, S])).then_inc(img_done, 16)

            def store_output(b, u):
                sp.wait_ge(out_stored, (b + 2) * 16)
                sp.wait_ge(out_ready, b + 2)
                sp.dma_start(out[b].rearrange("(t p) c -> p t c", p=P),
                             fin[u][:, :].rearrange("p (t c) -> p t c", t=T)).then_inc(out_stored, 16)

            def body(b, u, cur, prev, nxt, load):
                if not isinstance(b, int) or b > 1:
                    store_output(b - 2, u)
                if cur:
                    send_max_rows(b, u, 1)
                if load:
                    sp.wait_ge(s2_mm, b * FH + HH)
                    sp.wait_ge(img_done, 64)
                    load_stack(b + 2, u, 0, ROW_MAX)
                if nxt:
                    send_max_rows(b + 1, 1 - u, 0)
                if load:
                    sp.wait_ge(s2_mm, b * FH + FH)
                    load_stack(b + 2, u, 1, ROW_MAX)

            body(-1, 1, False, False, True, False)
            body(0, 0, True, False, True, True)
            body(1, 1, True, True, True, True)
            with sp.Fori(0, (NB - 4) // 2) as i:
                body(i * 2 + 2, 0, True, True, True, True)
                body(i * 2 + 3, 1, True, True, True, True)
            body(NB - 2, 0, True, True, True, False)
            body(NB - 1, 1, True, True, False, False)
            store_output(NB - 2, 0)
            store_output(NB - 1, 1)
            sp.wait_ge(out_stored, 16 * (NB + 2))

        @block.gpsimd
        def _(pool):
            def gather(n):
                if not isinstance(n, int) or n > 0:
                    wait_apart(pool, gathered, n * 16 * T)
                nc.gpsimd.tensor_copy(ids_now[:, :], ids[:, bass.ds(n * T, T)]).then_inc(ids_ready, 1)
                wait(pool, embt_tr, n)
                wait_apart(pool, ids_ready, n + 1)
                for t in range(T):
                    nc.gpsimd.indirect_dma_start(
                        out=emb[:, t, :], out_offset=None, in_=embeddings,
                        in_offset=bass.IndirectOffsetOnAxis(ap=ids_now[:, t:t + 1].bitcast(U32), axis=0),
                    ).then_inc(gathered, 16)

            pool.wait_ge(ids_loaded, 16)
            gather(0)
            nc.gpsimd.memset(carry_pool[:, 0:1], 0.0)
            nc.gpsimd.memset(ident[:, :], 0.0).then_inc(const_pool, 1)
            nc.gpsimd.memset(blk8[:, :, :], 1.0).then_inc(const_pool, 1)
            nc.gpsimd.memset(blk16[:, :, :], 1.0).then_inc(const_pool, 1)
            pool.wait_ge(const_pool, 3)
            nc.gpsimd.affine_select(out=ident[:, :], in_=ident[:, :], compare_op=ALU.not_equal, fill=1.0, base=0,
                                    pattern=[[-1, P]], channel_multiplier=1).then_inc(const_pool, 1)
            nc.gpsimd.memset(quad[:, :], 1.0).then_inc(const_pool, 1)
            nc.gpsimd.memset(reg_row[:, :], 0.0).then_inc(const_pool, 1)
            nc.gpsimd.affine_select(out=blk8[:, :, :], in_=blk8[:, :, :], compare_op=ALU.is_ge, fill=0.0, base=0,
                                    pattern=[[-AD, AH], [0, AD]], channel_multiplier=1).then_inc(const_pool, 1)
            nc.gpsimd.affine_select(out=blk16[:, :, :], in_=blk16[:, :, :], compare_op=ALU.is_ge, fill=0.0, base=0,
                                    pattern=[[-FD, HH], [0, FD]], channel_multiplier=1).then_inc(const_pool, 1)
            pool.wait_ge(const_pool, 8)
            nc.gpsimd.affine_select(out=blk8[:, :, :], in_=blk8[:, :, :], compare_op=ALU.is_ge, fill=0.0, base=AD - 1,
                                    pattern=[[AD, AH], [0, AD]], channel_multiplier=-1).then_inc(const_pool, 1)
            nc.gpsimd.affine_select(out=blk16[:, :, :], in_=blk16[:, :, :], compare_op=ALU.is_ge, fill=0.0,
                                    base=FD - 1, pattern=[[FD, HH], [0, FD]],
                                    channel_multiplier=-1).then_inc(const_pool, 1)
            nc.gpsimd.affine_select(out=quad[:, :], in_=quad[:, :], compare_op=ALU.is_ge, fill=0.0, base=0,
                                    pattern=[[-32, GH]], channel_multiplier=1).then_inc(const_pool, 1)
            pool.wait_ge(const_pool, 11)
            nc.gpsimd.affine_select(out=quad[:, :], in_=quad[:, :], compare_op=ALU.is_ge, fill=0.0, base=31,
                                    pattern=[[32, GH]], channel_multiplier=-1).then_inc(const_pool, 1)
            for g in range(GH):
                pool.wait_ge(const_pool, 12 + g)
                nc.gpsimd.affine_select(out=reg_row[:, :], in_=reg_row[:, :], compare_op=ALU.not_equal, fill=1.0,
                                        base=-(32 * g + WIN - REG), pattern=[[-1, REG]],
                                        channel_multiplier=1).then_inc(const_pool, 1)

            def body(b, cur, prev, nxt):
                n, p = b + 1, b - 1
                if nxt:
                    pool.wait_ge(xn1_ready, n + 1)
                    nc.gpsimd.tensor_tensor(
                        h_all[:, n, :].rearrange("p (t c) -> p t c", t=T),
                        h_all[:, n, :].rearrange("p (t c) -> p t c", t=T),
                        b_attn[:, :].unsqueeze(1).to_broadcast([P, T, C]), ALU.add).then_inc(hb_ready, 1)
                if cur and nxt:
                    gather_next(n)
                if prev:
                    pool.wait_ge(part1_ready, p + 1)
                    nc.gpsimd.tensor_tensor(qk_parts[:, :, 2, :], qk_rest[:, :, :], qk_parts[:, :, 1, :],
                                            ALU.subtract).then_inc(part2_ready, 1)

            def gather_next(n):
                gather(n + 1)

            body(-1, False, False, True)
            gather(1)
            body(0, True, False, True)
            with pool.Fori(1, NB - 2) as b:
                body(b, True, True, True)
            pool.wait_ge(xn1_ready, NB)
            nc.gpsimd.tensor_tensor(
                h_all[:, NB - 1, :].rearrange("p (t c) -> p t c", t=T),
                h_all[:, NB - 1, :].rearrange("p (t c) -> p t c", t=T),
                b_attn[:, :].unsqueeze(1).to_broadcast([P, T, C]), ALU.add).then_inc(hb_ready, 1)
            for p in range(NB - 3, NB):
                pool.wait_ge(part1_ready, p + 1)
                nc.gpsimd.tensor_tensor(qk_parts[:, :, 2, :], qk_rest[:, :, :], qk_parts[:, :, 1, :],
                                        ALU.subtract).then_inc(part2_ready, 1)

            pool.wait_ge(ext_ready, 2)
            nc.gpsimd.partition_all_reduce(exta[:, :], ext[:, :], P, RMAX).then_inc(exta_ready, 1)

            def registers(b, u, half):
                heads = slice(half * HH, (half + 1) * HH)
                wait_apart(pool, stack_in[half], b * 32 + 32)
                nc.gpsimd.tensor_copy(q_st[u][0:ROW_CLASS, heads, S:NQ],
                                      q_st[u][0:ROW_CLASS, heads, 0:REG]).then_inc(qx_ready[half], 1)

            def values(b, u):
                if not isinstance(b, int) or b > 1:
                    wait_apart(pool, pv_mm, b * NG - NG)
                nc.gpsimd.tensor_copy(v_st[u][:, :, :, 0:FD],
                                      v_all[:, b, :].rearrange("p (t h d) -> p t h d", t=T, h=FH)
                                      ).then_inc(vst_ready, 1)

            def residual(b, u):
                wait(pool, out_ready, b)
                nc.gpsimd.tensor_tensor(
                    resid[u][:, :].rearrange("p (t c) -> p t c", t=T),
                    h_all[:, b, :].rearrange("p (t c) -> p t c", t=T),
                    b_ffn[:, :].unsqueeze(1).to_broadcast([P, T, C]), ALU.add).then_inc(resid_ready, 1)

            def max_rest(b, half):
                pool.wait_ge(mhi_ready, b * 2 + half + 1)
                nc.gpsimd.tensor_tensor(mrow[:, half, 1, :], mneg[:, half, :], mrow[:, half, 0, :],
                                        ALU.subtract).then_inc(mrow_ready, 1)

            def body(b, u, cur, prev, nxt, more):
                o = 1 - u
                if cur:
                    max_rest(b, 1)
                if cur and nxt:
                    registers(b + 1, o, 1)
                    values(b + 1, o)
                if cur:
                    residual(b, u)
                if prev:
                    pool.wait_ge(tok_ready, b * 3 - 1)
                    nc.gpsimd.tensor_tensor(attx[:, :, :], att[0:REG, 0], attx[:, :, :], ALU.add).then_inc(reg_sum, 1)
                    pool.wait_ge(reg_sum, b)
                    nc.gpsimd.tensor_tensor(att[0:REG, 0], attx[:, :, :],
                                            halves_t[:, :].unsqueeze(2).to_broadcast([REG, FH, FD]),
                                            ALU.mult).then_inc(att_ready, 1)
                if nxt:
                    max_rest(b + 1, 0)
                if more:
                    registers(b + 2, u, 0)
                if prev:
                    pool.wait_ge(out_stored, b * 16)
                    pool.wait_ge(raw_ready, b + 1)
                    pool.wait_ge(resid_ready, b)
                    nc.gpsimd.tensor_tensor(fin[o][:, :], raw[:, :], resid[o][:, :], ALU.add).then_inc(out_ready, 1)

            nc.gpsimd.memset(halves_t[:, :], 0.5).then_inc(const_pool, 1)
            pool.wait_ge(const_pool, 13 + GH)
            pool.wait_ge(st_const, 5)
            registers(0, 0, 0)
            registers(0, 0, 1)
            pool.wait_ge(v2_ready, NB)
            values(0, 0)
            registers(1, 1, 0)
            body(-1, 1, False, False, True, False)
            body(0, 0, True, False, True, True)
            with pool.Fori(0, (NB - 4) // 2) as i:
                body(i * 2 + 1, 1, True, True, True, True)
                body(i * 2 + 2, 0, True, True, True, True)
            body(NB - 3, 1, True, True, True, True)
            body(NB - 2, 0, True, True, True, False)
            body(NB - 1, 1, True, True, False, False)
            body(NB, 0, False, True, False, False)

        @block.scalar
        def _(act):
            act.wait_ge(g_sum, 1)
            nc.scalar.activation(gnrm[:, :], ps[:, 0, 0:KC], ACT.Sqrt).then_inc(g_root, 1)
            act.wait_ge(const_dve, 4)

            def halves(bank):
                return ps[:, bank, :].rearrange("p (k t) -> p k t", k=KC)

            def save_q2(p):
                act.wait_ge(qk2_mm, p * 2 + 1)
                nc.scalar.activation(qkf[:, :, 0, :], halves(6), ACT.Copy).then_inc(qkf_ready, 1)
                act.wait_ge(qkf_ready, p * 2 + 1)
                nc.scalar.activation(qsq[:, :, :], qkf[:, :, 0, :], ACT.Square).then_inc(qsq_ready, 1)

            def save_k2(p):
                act.wait_ge(qk2_mm, p * 2 + 2)
                nc.scalar.activation(qkf[:, :, 1, :], halves(7), ACT.Copy).then_inc(qkf_ready, 1)

            def save_v2(p):
                act.wait_ge(v2_mm, p + 1)
                nc.scalar.activation(v_all[:, p, :], ps[:, 3, :], ACT.Copy).then_inc(v2_ready, 1)

            def save_dots(p):
                act.wait_ge(dots_mm, p + 1)
                nc.scalar.activation(dots[:, 0:REG], ps[:, 0, REG:2 * REG], ACT.Copy)
                nc.scalar.activation(dots[:, REG:S], ps[:, 0, REG:S], ACT.Copy).then_inc(dots_ready, 1)

            def second_part(p):
                act.wait_ge(rest_ready, p + 1)
                nc.scalar.activation(qk_parts[:, :, 1, :], qk_rest[:, :, :], ACT.Copy).then_inc(part1_ready, 1)

            def norms(p):
                act.wait_ge(dott_tr, p + 1)
                by = ps[:, 5, 0:T * P].rearrange("p (t g c) -> p t g c", t=T, g=4)
                nc.scalar.activation(nrm[:, :, :, :], by[:, :, 2:4, 0:HH], ACT.Sqrt).then_inc(nrm_ready, 1)

            def save_xn2(p):
                act.wait_ge(xn2t_tr, p + 1)
                nc.scalar.activation(xn2_t[:, :, :], halves(2), ACT.Copy).then_inc(xn2t_ready, 1)

            def body(b, cur, prev, nxt):
                n, p = b + 1, b - 1
                if not cur and prev:
                    save_xn2(p)
                    save_q2(p)
                    save_k2(p)
                    save_dots(p)
                    norms(p)
                    second_part(p)
                    save_v2(p)
                    return
                if cur:
                    act.wait_ge(q1_mm, b + 1)
                    nc.scalar.activation(q1_t[:, :, :], halves(3), ACT.Relu).then_inc(q1_ready, 1)
                if prev:
                    save_xn2(p)
                if cur:
                    act.wait_ge(kv_mm, b * T + 2)
                    nc.scalar.activation(kv[:, 1, :, 0:P], ps[:, 5, :].rearrange("p (k t) -> p k t", k=4),
                                         ACT.Relu).then_inc(kv1_ready, 1)
                if nxt:
                    act.wait_ge(embt_tr, n + 1)
                    nc.scalar.activation(emb_t[:, :], ps[:, 0, 0:S], ACT.Copy).then_inc(embt_ready, 1)
                if prev:
                    save_q2(p)
                if nxt:
                    act.wait_ge(h_mm, n + 1)
                    nc.scalar.activation(h_all[:, n, :], ps[:, 1, :], ACT.Copy).then_inc(h_saved, 1)
                    act.wait_ge(ln1_var, n + 1)
                    nc.scalar.activation(sd1[:, :], mv1[:, :, 1], ACT.Sqrt, bias=eps_t[:, 0:1]).then_inc(ln1_root, 1)
                if prev:
                    save_k2(p)
                    save_v2(p)
                    save_dots(p)
                if cur:
                    act.wait_ge(mixt_tr, b + 1)
                    nc.scalar.activation(mix_t[:, :, :], halves(2), ACT.Copy).then_inc(mixt_ready, 1)
                if nxt:
                    act.wait_ge(xn1t_tr, n + 1)
                    nc.scalar.activation(xn1_t[:, :, :], halves(1), ACT.Copy).then_inc(xn1t_ready, 1)
                if prev:
                    norms(p)
                    second_part(p)
                if cur:
                    act.wait_ge(ln2_var, b + 1)
                    nc.scalar.activation(sd2[:, :], mv2[:, :, 1], ACT.Sqrt, bias=eps_t[:, 0:1]).then_inc(ln2_root, 1)

            phase1(act, body)

            act.wait_ge(clst_tr, 1)
            nc.scalar.activation(cls_t[:, :], ps[0:4 * NB * T, 7, 0:P], ACT.Copy).then_inc(clst_ready, 1)
            act.wait_ge(clst_ready, 1)
            act.dma_start(class_dram.rearrange("c (s t) -> (c s) t", t=P), cls_t[:, :]).then_inc(cls_stored, 16)
            act.wait_ge(cls_stored, 16)
            load_classes(act, 0, 0)

            def minus_max(b, half):
                act.wait_ge(mxt_tr, b * 2 + half + 1)
                wait(act, mrow_in[half], b * 32)
                nc.scalar.activation(mneg[:, half, :], ps[0:HH, 7, 0:NQ], ACT.Copy, scale=-1.0)
                nc.scalar.activation(mrow[:, half, 0, :], ps[0:HH, 7, 0:NQ], ACT.Copy,
                                     scale=-1.0).then_inc(mhi_ready, 1)

            def group_out(b, u, j):
                act.wait_ge(pv_mm, b * NG + j + 1)
                nc.scalar.activation(pv[u][:, j, :], ps[:, 6, 0:NQ], ACT.Copy).then_inc(pv_ready, 1)

            def body(b, u, cur, prev, nxt):
                for h in range(FH):
                    if cur:
                        j = h // GH
                        act.wait_ge(s2_mm, b * FH + h + 1)
                        if h % GH == 0:
                            wait(act, pv_mm, b * NG + j - 1)
                        nc.scalar.activation(ex[j % 2][:, h % GH, :, :],
                                             ps[:, 2 + 2 * (h % 2):4 + 2 * (h % 2), 0:NQ],
                                             ACT.Exp).then_inc(ex_ready, 1)
                    if prev and h == 1:
                        group_out(b - 1, 1 - u, NG - 1)
                    if cur and h == 2:
                        minus_max(b, 1)
                    if cur and h in (7, 11, 13):
                        group_out(b, u, (h - 7) // 3)
                    if nxt and h == 10:
                        minus_max(b + 1, 0)
                    if prev and h == 12:
                        act.wait_ge(attt_tr, b)
                        nc.scalar.activation(att_t[:, :, :], ps[:, 7, :].rearrange("p (k t) -> p k t", k=KC),
                                             ACT.Copy).then_inc(attt_ready, 1)
                    if prev and h == 15:
                        act.wait_ge(out_mm, b)
                        if not nxt:
                            act.wait_ge(out_ready, b)
                        nc.scalar.activation(raw[:, :], ps[:, 7, :], ACT.Copy).then_inc(raw_ready, 1)

            phase2(act, body)

        @block.vector
        def _(dve):
            nc.vector.memset(parts_mark[:, :], 0.0).then_inc(parts_stored, 16)
            nc.vector.memset(fin[0][:, 0:1], 0.0).then_inc(out_stored, 16)
            nc.vector.memset(fin[1][:, 0:1], 0.0).then_inc(out_stored, 16)
            nc.vector.memset(resid[1][:, 0:1], 0.0).then_inc(out_ready, 1)
            nc.vector.memset(raw[:, 0:1], 0.0).then_inc(raw_ready, 1)
            nc.vector.memset(ones[:, :], 1.0).then_inc(const_dve, 1)
            nc.vector.memset(eps_t[:, :], LN_EPS).then_inc(const_dve, 1)
            nc.vector.memset(kv[:, :, :, P:P + 1], 1.0).then_inc(const_dve, 1)
            nc.vector.memset(reg_is[:, :], 0.0).then_inc(const_dve, 1)
            dve.wait_ge(const_dve, 4)
            nc.vector.memset(reg_is[0:REG, 0:NB * T:T], 1.0).then_inc(const_dve, 1)
            for u in range(2):
                nc.vector.memset(q_st[u][ROW_CLASS:ROW_MAX, :, S:NQ], 1.0).then_inc(cls_step, 1)
                dve.wait_ge(cls_step, 2 * u + 1)
                nc.vector.memset(q_st[u][ROW_CLASS:ROW_CLASS + 1, :, S:NQ], 0.0).then_inc(st_const, 1)
                nc.vector.memset(k_st[u][ROW_CLASS:ROWS, :, :], 1.0).then_inc(st_const, 1)
                nc.vector.memset(v_st[u][:, :, :, FD:2 * FD], 1.0).then_inc(cls_step, 1)
            nc.vector.memset(mxr[:, :, :, :], 0.0).then_inc(st_const, 1)
            dve.wait_ge(const_pool, 10)
            dve.wait_ge(loaded, 16 * LOADS)
            nc.vector.memset(head_of[:, :], 0.0).then_inc(g_step, 1)
            dve.wait_ge(g_step, 1)
            nc.vector.tensor_copy(head_of[:, 0:HH], blk16[:, :, 0]).then_inc(g_step, 1)
            nc.vector.tensor_tensor(gtmp[:, :], gvec[:, :], gvec[:, :], ALU.mult).then_inc(g_sq, 1)
            nc.vector.tensor_scalar(w_fqkv[:, :, 0:C], w_fqkv[:, :, 0:C], float(FD) ** -0.5, None,
                                    ALU.mult).then_inc(g_step, 1)
            dve.wait_ge(g_root, 1)
            dve.wait_ge(g_sum, 1)
            nc.vector.reciprocal(gtmp[:, :], gnrm[:, :]).then_inc(g_step, 1)
            dve.wait_ge(g_step, 4)
            nc.vector.scalar_tensor_tensor(out=gnrm[:, :], in0=gvec[:, :], scalar=1.0 / FH, in1=gtmp[:, :],
                                           op0=ALU.mult, op1=ALU.mult).then_inc(g_step, 1)
            dve.wait_ge(g_step, 5)
            for k in range(KC):
                nc.vector.tensor_scalar(g_dot[:, k, :], head_of[:, :], gnrm[:, k:k + 1], None,
                                        ALU.mult).then_inc(g_ready, 1)

            def first_part(p):
                dve.wait_ge(qkf_ready, p * 2 + 2)
                dve.wait_ge(parts_stored, p * (16 * NSTORE) + 16)
                src = qkf[:, :, :, :].rearrange("p k c t -> p (k c) t")
                nc.vector.tensor_copy(qk_parts[:, :, 0, :], src).then_inc(part0_ready, 1)
                dve.wait_ge(part0_ready, p + 1)
                nc.vector.tensor_tensor(qk_rest[:, :, :], src, qk_parts[:, :, 0, :],
                                        ALU.subtract).then_inc(rest_ready, 1)

            def similarity(p):
                dve.wait_ge(nrm_ready, p + 1)
                nc.vector.reciprocal(rnrm[:, :, :, :], nrm[:, :, :, :]).then_inc(rnrm_ready, 1)
                dve.wait_ge(rnrm_ready, p + 1)
                sims = ps[:, 5, 0:T * P].rearrange("p (t g c) -> p t g c", t=T, g=4)
                nc.vector.tensor_tensor(cosb[:, :, :, :], sims[:, :, 0:2, 0:HH], rnrm[:, :, :, :],
                                        ALU.mult).then_inc(cos_ready, 1)
                dve.wait_ge(cos_ready, p + 1)
                nc.vector.tensor_reduce(sim_all[:, bass.ds(p * T, T)], cosb[:, :, :, :], axis=AX.XY,
                                        op=ALU.add).then_inc(sim_ready, 1)

            def body(b, cur, prev, nxt):
                n, p = b + 1, b - 1
                if not cur and prev:
                    similarity(p)
                    first_part(p)
                    return
                if cur:
                    dve.wait_ge(kv_mm, b * T + 1)
                    nc.vector.tensor_scalar(kv[:, 0, :, 0:P], ps[:, 4, :].rearrange("p (k t) -> p k t", k=4),
                                            0.0, None, ALU.max).then_inc(kv0_ready, 1)
                    dve.wait_ge(vk_mm, b + 1)
                    prod = ps[:, 3, 0:KC * (P + 1)].rearrange("p (k c) -> p k c", k=KC)
                    nc.vector.tensor_tensor(
                        vk[:, :, 0:P], prod[:, :, 0:P],
                        blk8[:, :, :].rearrange("p h e -> p (h e)").unsqueeze(1).to_broadcast([P, KC, P]), ALU.mult)
                    nc.vector.tensor_tensor(
                        vk[:, :, P:P + AH], prod[:, :, P:P + 1].to_broadcast([P, KC, AH]),
                        blk8[:, :, 0].unsqueeze(1).to_broadcast([P, KC, AH]), ALU.mult).then_inc(vk_ready, 1)
                if nxt:
                    wait_apart(dve, h_saved, n + 1)
                    hv = h_all[:, n, :].rearrange("p (t c) -> p t c", t=T)
                    for t in range(T):
                        nc.vector.bn_stats(bst1[:, t, :], hv[:, t, :]).then_inc(ln1_stats, 1)
                    wait_apart(dve, ln1_stats, n * T + T)
                    for t in range(T):
                        ins = nc.vector.bn_aggr(mv1[:, t, :], bst1[:, t, :])
                    ins.then_inc(ln1_var, 1)
                    dve.wait_ge(ln1_root, n + 1)
                    nc.vector.reciprocal(rs1[:, :], sd1[:, :]).then_inc(ln1_scale, 1)
                    dve.wait_ge(ln1_scale, n + 1)
                    for t in range(T):
                        ins = nc.vector.tensor_scalar(xn1[:, t, :], hv[:, t, :], mv1[:, t, 0:1], rs1[:, t:t + 1],
                                                      ALU.subtract, ALU.mult)
                    ins.then_inc(xn1_ready, 1)
                if cur:
                    dve.wait_ge(nd_mm, b + 1)
                    by = ps[:, 4:6, 0:KC * (P + AH)].rearrange("p t (k c) -> p t k c", k=KC)
                    nc.vector.tensor_scalar(den[:, :, :, :], by[:, :, :, P:P + AH], DEN_EPS, None,
                                            ALU.add).then_inc(den_ready, 1)
                    dve.wait_ge(den_ready, b + 1)
                    nc.vector.reciprocal(rden[:, :, :, :], den[:, :, :, :]).then_inc(rden_ready, 1)
                    dve.wait_ge(rden_ready, b + 1)
                    for t in range(T):
                        ins = nc.vector.tensor_tensor(
                            mix[:, t, :, :, :], by[:, t, :, 0:P].rearrange("p k (h e) -> p k h e", h=AH),
                            rden[:, t, :, :].unsqueeze(3).to_broadcast([P, KC, AH, AD]), ALU.mult)
                    ins.then_inc(mix_ready, 1)
                if prev:
                    first_part(p)
                    similarity(p)
                if cur:
                    dve.wait_ge(proj_mm, b + 1)
                    dve.wait_ge(hb_ready, b + 1)
                    nc.vector.tensor_tensor(h_all[:, b, :], ps[:, 4, :], h_all[:, b, :], ALU.add).then_inc(h1_ready, 1)
                    wait_apart(dve, h1_ready, b + 1)
                    h1v = h_all[:, b, :].rearrange("p (t c) -> p t c", t=T)
                    for t in range(T):
                        nc.vector.bn_stats(bst2[:, t, :], h1v[:, t, :]).then_inc(ln2_stats, 1)
                    wait_apart(dve, ln2_stats, b * T + T)
                    for t in range(T):
                        ins = nc.vector.bn_aggr(mv2[:, t, :], bst2[:, t, :])
                    ins.then_inc(ln2_var, 1)
                    dve.wait_ge(ln2_root, b + 1)
                    nc.vector.reciprocal(rs2[:, :], sd2[:, :]).then_inc(ln2_scale, 1)
                    dve.wait_ge(ln2_scale, b + 1)
                    for t in range(T):
                        ins = nc.vector.tensor_scalar(xn2[:, t, :], h1v[:, t, :], mv2[:, t, 0:1], rs2[:, t:t + 1],
                                                      ALU.subtract, ALU.mult)
                    ins.then_inc(xn2_ready, 1)

            phase1(dve, body)

            dve.wait_ge(sim_ready, NB)
            nc.vector.tensor_reduce(ext[:, 0:1], sim_all[:, :], axis=AX.X, op=ALU.max).then_inc(ext_ready, 1)
            nc.vector.tensor_reduce(ext[:, 1:2], sim_all[:, :], axis=AX.X, op=ALU.min,
                                    negate=True).then_inc(ext_ready, 1)
            nc.vector.tensor_reduce(zsum[:, 0:1], sim_all[:, :], axis=AX.X, op=ALU.add).then_inc(cls_step, 1)
            dve.wait_ge(cls_step, 5)
            nc.vector.tensor_scalar(zsum[:, 1:2], zsum[:, 0:1], 0.0, None, ALU.mult).then_inc(zsum_ready, 1)
            dve.wait_ge(exta_ready, 1)
            nc.vector.tensor_tensor(thr[:, 0:1], exta[:, 0:1], exta[:, 1:2], ALU.add).then_inc(cls_step, 1)
            dve.wait_ge(zall_mm, 1)
            dve.wait_ge(cls_step, 6)
            nc.vector.scalar_tensor_tensor(out=thr[:, 1:2], in0=thr[:, 0:1], scalar=0.9, in1=ps[:, 7, 0:1],
                                           op0=ALU.mult, op1=ALU.add).then_inc(cls_step, 1)
            dve.wait_ge(cls_step, 7)
            nc.vector.tensor_scalar(pos[:, :], sim_all[:, :], exta[:, 1:2], thr[:, 1:2], ALU.add,
                                    ALU.is_gt).then_inc(cls_step, 1)
            dve.wait_ge(cls_step, 8)
            nc.vector.tensor_tensor(cls[:, 0, :], pos[:, :], reg_is[:, :], ALU.max).then_inc(cls_step, 1)
            nc.vector.tensor_scalar(neg[:, :], pos[:, :], -1.0, 1.0, ALU.mult, ALU.add).then_inc(cls_step, 1)
            dve.wait_ge(cls_step, 10)
            nc.vector.tensor_tensor(pos[:, :], neg[:, :], reg_is[:, :], ALU.max).then_inc(cls_step, 1)
            nc.vector.tensor_scalar(cls[:, 1, :], cls[:, 0, :], -1.0, 1.0, ALU.mult, ALU.add)
            nc.vector.tensor_scalar(cls[:, 2, :], cls[:, 0, :], -1.0, BIG, ALU.add, ALU.mult)
            dve.wait_ge(cls_step, 11)
            nc.vector.tensor_scalar(cls[:, 3, :], pos[:, :], -1.0, BIG, ALU.add, ALU.mult).then_inc(cls_ready, 1)

            def max_of(b, v, half, to):
                dve.wait_ge(s1_mm, b * UNITS + v + 1)
                if v % (HH + 1) == 0:
                    wait(dve, mxt_tr, b * 2 + half - 1)
                nc.vector.tensor_reduce(to, ps[:, v % 2, :].rearrange("p (t q) -> p t q", t=2), axis=AX.X,
                                        op=ALU.max).then_inc(max_ready, 1)

            OUTS = ((REG, attx[:, :, :], rsumx), (P, att[:, 0], rsum), (P, att[:, 1], rsum))

            def normalise(b, what):
                rows, dst, rs = OUTS[what]
                by = ps[0:rows, 7, :].rearrange("p (h c) -> p h c", h=FH)
                dve.wait_ge(tok_tr, b * 3 + what + 1)
                nc.vector.reciprocal(rs[:, :], by[:, :, FD]).then_inc(rsum_ready, 1)
                dve.wait_ge(rsum_ready, b * 3 + what + 1)
                nc.vector.tensor_tensor(dst, by[:, :, 0:FD], rs[:, :].unsqueeze(2).to_broadcast([rows, FH, FD]),
                                        ALU.mult).then_inc(tok_ready, 1)

            def body(b, u, cur, prev, nxt):
                for h in range(FH):
                    half, hh = h // HH, h % HH
                    if nxt:
                        max_of(b + 1, h + half, half, mx[:, half, hh:hh + HH + 1:HH])
                        if hh == HH - 1:
                            max_of(b + 1, h + half + 1, half, mx[:, half, 2 * HH:2 * HH + 2])
                            dve.wait_ge(max_ready, b * UNITS + UNITS + (HH + 1) * (half + 1))
                            nc.vector.tensor_tensor(
                                mxr[:, half, :, :],
                                mx[:, half, 2 * HH:2 * HH + 2].unsqueeze(2).to_broadcast([P, HH // GH, GH]),
                                quad[:, :].unsqueeze(1).to_broadcast([P, HH // GH, GH]),
                                ALU.mult).then_inc(mxr_ready, 1)
                    if prev and h in (4, 6, 8):
                        normalise(b - 1, (h - 4) // 2)

            phase2(dve, body)

        @block.tensor
        def _(pe):
            mm = nc.tensor.matmul
            pe.wait_ge(const_pool, 10)
            pe.wait_ge(g_sq, 1)
            mm(ps[:, 0, 0:KC], blk16[:, :, :].rearrange("p h d -> p (h d)"), gtmp[:, :],
               start=True, stop=True).then_inc(g_sum, 1)
            pe.wait_ge(g_root, 1)

            def to_channels(src, bank):
                for k in range(KC):
                    for t in range(T):
                        ins = nc.tensor.transpose(ps[:, bank, k * S + t * P:k * S + (t + 1) * P],
                                                  src[:, t, k * P:(k + 1) * P], ident[:, :])
                return ins

            def q_product(b):
                pe.wait_ge(xn1t_ready, b + 1)
                for m in range(KC):
                    for k in range(KC):
                        ins = mm(ps[:, 3, m * S:(m + 1) * S], w_aqkv[:, k, m * P:(m + 1) * P], xn1_t[:, k, :],
                                 start=(k == 0), stop=(k == KC - 1))
                ins.then_inc(q1_mm, 1)

            def kv_product(b, t):
                if t == 0:
                    wait(pe, h1_ready, b)
                for k in range(KC):
                    ins = mm(ps[:, 4 + t, :], xn1_t[:, k, t * P:(t + 1) * P], w_aqkv[:, k, C:3 * C],
                             start=(k == 0), stop=(k == KC - 1))
                ins.then_inc(kv_mm, 1)

            def turn_xn2(p, cur):
                pe.wait_ge(xn2_ready, p + 1)
                if cur:
                    pe.wait_ge(xn1t_ready, p + 2)
                to_channels(xn2, 2).then_inc(xn2t_tr, 1)

            def turn_embeddings(n):
                pe.wait_ge(gathered, n * (16 * T) + 16 * T)
                for t in range(T):
                    ins = nc.tensor.transpose(ps[:, 0, t * P:(t + 1) * P], emb[:, t, :], ident[:, :])
                ins.then_inc(embt_tr, 1)

            def vk_product(b):
                pe.wait_ge(kv0_ready, b + 1)
                pe.wait_ge(kv1_ready, b + 1)
                pe.wait_ge(q1_ready, b + 1)
                for k in range(KC):
                    for t in range(T):
                        ins = mm(ps[:, 3, k * (P + 1):(k + 1) * (P + 1)], kv[:, t, k, 0:P], kv[:, t, KC + k, :],
                                 start=(t == 0), stop=(t == T - 1))
                ins.then_inc(vk_mm, 1)

            def token_product(n):
                pe.wait_ge(embt_ready, n + 1)
                if not isinstance(n, int) or n == 0:
                    pe.wait_ge(loaded, 16 * LOADS)
                for t in range(T):
                    ins = mm(ps[:, 1, t * C:(t + 1) * C], emb_t[:, t * P:(t + 1) * P], w_tok[:, :],
                             start=True, stop=True)
                ins.then_inc(h_mm, 1)

            def qk2_product(p, i):
                pe.wait_ge(xn2t_ready, p + 1)
                wait(pe, g_step, 3)
                for m in range(KC):
                    for k in range(KC):
                        ins = mm(ps[:, 6 + i, m * S:(m + 1) * S],
                                 w_fqkv[:, k, i * C + m * P:i * C + (m + 1) * P], xn2_t[:, k, :],
                                 start=(k == 0), stop=(k == KC - 1))
                ins.then_inc(qk2_mm, 1)

            def nd_product(b):
                pe.wait_ge(vk_ready, b + 1)
                for t in range(T):
                    for k in range(KC):
                        ins = mm(ps[:, 4 + t, k * (P + AH):(k + 1) * (P + AH)], q1_t[:, k, t * P:(t + 1) * P],
                                 vk[:, k, :], start=True, stop=True)
                ins.then_inc(nd_mm, 1)

            def v2_product(p, cur):
                if cur:
                    pe.wait_ge(vk_ready, p + 2)
                for t in range(T):
                    for k in range(KC):
                        ins = mm(ps[:, 3, t * C:(t + 1) * C], xn2_t[:, k, t * P:(t + 1) * P],
                                 w_fqkv[:, k, 2 * C:3 * C], start=(k == 0), stop=(k == KC - 1))
                ins.then_inc(v2_mm, 1)

            def dot_products(p):
                pe.wait_ge(qsq_ready, p + 1)
                pe.wait_ge(g_ready, KC)
                for g in range(4):
                    w = g_dot[:, g, :] if g < KC else head_of[:, :]
                    r = qkf[:, g, 0, :] if g < KC else qsq[:, g - KC, :]
                    ins = mm(ps[32 * g:32 * g + 32, 0, 0:S], w, r, start=True, stop=True)
                ins.then_inc(dots_mm, 1)

            def turn_mix(b, prev):
                pe.wait_ge(mix_ready, b + 1)
                if prev:
                    pe.wait_ge(xn2t_ready, b)
                to_channels(mix[:, :, :, :, :].rearrange("p t k h e -> p t (k h e)"), 2).then_inc(mixt_tr, 1)

            def turn_dots(p):
                pe.wait_ge(dots_ready, p + 1)
                for t in range(T):
                    ins = nc.tensor.transpose(ps[:, 5, t * P:(t + 1) * P], dots[:, t * P:(t + 1) * P], ident[:, :])
                ins.then_inc(dott_tr, 1)

            def turn_xn1(n):
                pe.wait_ge(xn1_ready, n + 1)
                to_channels(xn1, 1).then_inc(xn1t_tr, 1)

            def mix_projection(b):
                pe.wait_ge(mixt_ready, b + 1)
                for t in range(T):
                    for k in range(KC):
                        ins = mm(ps[:, 4, t * C:(t + 1) * C], mix_t[:, k, t * P:(t + 1) * P], w_aproj[:, k, :],
                                 start=(k == 0), stop=(k == KC - 1))
                ins.then_inc(proj_mm, 1)

            def body(b, cur, prev, nxt):
                n, p = b + 1, b - 1
                if not cur and prev:
                    turn_xn2(p, cur)
                    qk2_product(p, 0)
                    qk2_product(p, 1)
                    dot_products(p)
                    turn_dots(p)
                    v2_product(p, cur)
                    return
                if cur:
                    q_product(b)
                if nxt:
                    turn_embeddings(n)
                if cur:
                    kv_product(b, 0)
                if prev:
                    turn_xn2(p, cur)
                if cur:
                    kv_product(b, 1)
                if prev:
                    qk2_product(p, 0)
                if cur:
                    vk_product(b)
                if nxt:
                    token_product(n)
                if prev:
                    qk2_product(p, 1)
                if cur:
                    nd_product(b)
                if prev:
                    v2_product(p, cur)
                    dot_products(p)
                if cur:
                    turn_mix(b, prev)
                if nxt:
                    turn_xn1(n)
                if prev:
                    turn_dots(p)
                if cur:
                    mix_projection(b)

            phase1(pe, body)
            pe.wait_ge(const_pool, 12 + GH)

            pe.wait_ge(zsum_ready, 1)
            pe.wait_ge(qkf_ready, 2 * NB)
            mm(ps[:, 7, 0:1], ones[:, :], zsum[:, 1:2], start=True, stop=True).then_inc(zall_mm, 1)
            pe.wait_ge(cls_ready, 1)
            nc.tensor.transpose(ps[0:4 * NB * T, 7, 0:P], cls[:, :, :].rearrange("p c s -> p (c s)"),
                                ident[:, :]).then_inc(clst_tr, 1)
            pe.wait_ge(clst_ready, 1)
            pe.wait_ge(v2_ready, NB)
            pe.wait_ge(dots_ready, NB)
            pe.wait_ge(cos_ready, NB)
            pe.wait_ge(h1_ready, NB)

            def send_max(b, half):
                pe.wait_ge(mxr_ready, b * 2 + half + 1)
                for t in range(T):
                    nc.tensor.transpose(ps[0:HH, 7, t * P:(t + 1) * P], mx[:, half, t * HH:(t + 1) * HH],
                                        ident[:, :])
                mm(ps[0:HH, 7, S:NQ], mxr[:, half, :, :].rearrange("p j g -> p (j g)"), reg_row[:, :],
                   start=True, stop=True).then_inc(mxt_tr, 1)

            def group(b, u, j, t):
                if t == 0:
                    pe.wait_ge(ex_ready, b * FH + GH * (j + 1))
                    pe.wait_ge(vst_ready, b + 1)
                    wait(pe, pv_ready, b * NG + j)
                for g in range(GH):
                    ins = mm(ps[32 * g:32 * g + 32, 6, 0:NQ], v_st[u][:, t, GH * j + g, :],
                             ex[j % 2][:, g, t, :], start=(t == 0), stop=(t == T - 1))
                if t == T - 1:
                    ins.then_inc(pv_mm, 1)

            def to_tokens(u, q0, nq):
                for j in range(NG):
                    ins = nc.tensor.transpose(ps[0:nq, 7, j * P:(j + 1) * P], pv[u][:, j, q0:q0 + nq], ident[:, :])
                ins.then_inc(tok_tr, 1)

            def body(b, u, cur, prev, nxt):
                o = 1 - u
                for h in range(FH):
                    half = h // HH
                    if cur:
                        if h % HH == 0:
                            pe.wait_ge(mrow_in[half], b * 32 + 32)
                        wait(pe, ex_ready, b * FH + h - 1)
                        for t in range(T):
                            ins = mm(ps[:, 2 + 2 * (h % 2) + t, 0:NQ], k_st[u][:, h, t * P:(t + 1) * P],
                                     q_st[u][:, h, :], start=True, stop=True)
                        ins.then_inc(s2_mm, 1)
                    if nxt:
                        v = h + half
                        if h % HH == 0:
                            pe.wait_ge(qx_ready[half], b + 2)
                            if isinstance(b, int) and b < 1 and h == 0:
                                pe.wait_ge(class_in[b + 1], 32)
                        wait(pe, max_ready, b * UNITS + UNITS + v - 1)
                        for t in range(T):
                            ins = mm(ps[:, v % 2, t * S:(t + 1) * S], q_st[o][0:ROW_MAX, h, t * P:(t + 1) * P],
                                     k_st[o][0:ROW_MAX, h, :], start=True, stop=True)
                        ins.then_inc(s1_mm, 1)
                        if h % HH == HH - 1:
                            v = v + 1
                            wait(pe, max_ready, b * UNITS + UNITS + v - 1)
                            for j in range(HH // GH):
                                for g in range(GH):
                                    ins = mm(ps[32 * g:32 * g + 32, v % 2, j * S:(j + 1) * S],
                                             q_st[o][0:ROW_MAX, half * HH + j * GH + g, NQ - WIN:NQ],
                                             k_st[o][0:ROW_MAX, half * HH + j * GH + g, :],
                                             start=True, stop=True)
                            ins.then_inc(s1_mm, 1)
                    if prev and h in (0, 1):
                        group(b - 1, o, NG - 1, h)
                    if cur and h == 2:
                        if prev:
                            pe.wait_ge(raw_ready, b)
                        send_max(b, 1)
                    if prev and h == 4:
                        pe.wait_ge(pv_ready, b * NG)
                        if cur:
                            pe.wait_ge(mhi_ready, b * 2 + 2)
                        else:
                            pe.wait_ge(raw_ready, b)
                        to_tokens(o, S, REG)
                    if cur and h in (5, 7):
                        group(b, u, 0, (h - 5) // 2)
                    if prev and h == 6:
                        pe.wait_ge(tok_ready, b * 3 - 2)
                        to_tokens(o, 0, P)
                    if prev and h == 8:
                        pe.wait_ge(tok_ready, b * 3 - 1)
                        to_tokens(o, P, P)
                    if cur and h in (9, 11):
                        group(b, u, 1, (h - 9) // 2)
                    if nxt and h == 10:
                        if prev:
                            pe.wait_ge(tok_ready, b * 3)
                        elif cur:
                            pe.wait_ge(mhi_ready, 2)
                        send_max(b + 1, 0)
                    if prev and h == 12:
                        pe.wait_ge(att_ready, b)
                        if nxt:
                            pe.wait_ge(mhi_ready, b * 2 + 3)
                        else:
                            pe.wait_ge(tok_ready, b * 3)
                        to_channels(att[:, :, :, :].rearrange("p t h d -> p t (h d)"), 7).then_inc(attt_tr, 1)
                    if cur and h == 13:
                        group(b, u, 2, 0)
                        group(b, u, 2, 1)
                    if prev and h in (14, 15):
                        t = h - 14
                        if t == 0:
                            pe.wait_ge(attt_ready, b)
                        for k in range(KC):
                            ins = mm(ps[:, 7, t * C:(t + 1) * C], att_t[:, k, t * P:(t + 1) * P],
                                     w_fproj[:, k, :], start=(k == 0), stop=(k == KC - 1))
                        if t == T - 1:
                            ins.then_inc(out_mm, 1)

            phase2(pe, body)


def kernel(x, L0_tok_embeddings, L0_tok_project_kernel, L0_attn_qkv_weight, L0_attn_proj_weight,
           L0_attn_proj_bias, L0_ffn_g_info, L0_ffn_W_qkv, L0_ffn_W_proj, L0_ffn_b_proj):
    import numpy as np
    import concourse.bacc as bacc
    from concourse import mybir as mb
    from concourse.bass_utils import run_bass_kernel_spmd

    x = np.asarray(x)
    arrays = {
        "ids": np.ascontiguousarray(x.reshape(-1, P).T),
        "embeddings": np.ascontiguousarray(L0_tok_embeddings),
        "tok_kernel": np.ascontiguousarray(L0_tok_project_kernel),
        "attn_qkv_t": np.ascontiguousarray(np.asarray(L0_attn_qkv_weight).T),
        "attn_proj_t": np.ascontiguousarray(np.asarray(L0_attn_proj_weight).T),
        "attn_bias": np.ascontiguousarray(L0_attn_proj_bias),
        "ffn_g": np.ascontiguousarray(L0_ffn_g_info),
        "ffn_qkv": np.ascontiguousarray(L0_ffn_W_qkv),
        "ffn_proj": np.ascontiguousarray(L0_ffn_W_proj),
        "ffn_bias": np.ascontiguousarray(L0_ffn_b_proj),
    }
    nc = bacc.Bacc("TRN2", target_bir_lowering=False, num_devices=1)
    args = [nc.dram_tensor("in_" + n, a.shape, mb.dt.from_np(a.dtype), kind="ExternalInput").ap()
            for n, a in arrays.items()]
    out = nc.dram_tensor("out", (*x.shape, arrays["tok_kernel"].shape[1]), F32, kind="ExternalOutput").ap()
    lm_tower(nc, *args, out)
    r = run_bass_kernel_spmd(nc, [{"in_" + n: a for n, a in arrays.items()}], core_ids=[0])
    return r.results[0]["out"]
```

```python
from contextlib import ExitStack

import concourse.bass as bass
from concourse import mybir

F32 = mybir.dt.float32
BF16 = mybir.dt.bfloat16
F32R = mybir.dt.float32r
I32 = mybir.dt.int32
U32 = mybir.dt.uint32
ALU = mybir.AluOpType
ACT = mybir.ActivationFunctionType
AX = mybir.AxisListType
RMAX = bass.bass_isa.ReduceOp.max

P = 128
LN_EPS = 1e-5
DEN_EPS = 1e-15
BIG = 1e30


def lm_tower(nc, x, embeddings, tok_kernel, attn_qkv_t, attn_proj_t, attn_bias,
             ffn_g, ffn_qkv, ffn_proj, ffn_bias, out):
    NB, S = 8, 256
    assert tuple(x.shape) == (P, NB * S // P)
    C = tok_kernel.shape[1]
    VOCAB = embeddings.shape[0]
    T = S // P
    KC = C // P
    AD = 8
    AH = P // AD
    FD = 16
    FH = C // FD
    HH = FH // 2
    REG = 5
    NQ = S + REG
    PARTS = 3
    RUNS = tuple(range(PARTS, 0, -1))
    ROW_CLASS = FD * sum(RUNS)
    ROW_MAX = ROW_CLASS + 2
    ROWS = ROW_MAX + 2
    NSTORE = PARTS * 2 * KC
    NLOAD = 2 * len(RUNS)
    GH = 4
    NG = FH // GH
    UNITS = FH + 2
    WIN = 32

    q_img = nc.dram_tensor("q_image", [NB, PARTS * FD, FH, S], BF16).ap()
    k_img = nc.dram_tensor("k_image", [NB, PARTS * FD, FH, S], BF16).ap()
    class_dram = nc.dram_tensor("class_rows", [4, NB * S], BF16).ap()

    with ExitStack() as ctx:
        def sb(name, shape, dt=F32):
            return ctx.enter_context(nc.sbuf_tensor(name, shape, dt))

        def pair(name, shape):
            return [sb(name + part, shape, F32R) for part in ("_hi", "_lo")]

        def sem(name):
            return ctx.enter_context(nc.semaphore(name))

        ps = ctx.enter_context(nc.psum_tensor("ps", [P, 8, 512], F32))

        ident = sb("ident", [P, P])
        ones = sb("ones", [P, P])
        blk8 = sb("blk8", [P, AH, AD])
        blk16 = sb("blk16", [P, HH, FD])
        head_of = sb("head_of", [P, 32])
        g_dot = sb("g_dot", [P, KC, 32])
        reg_is = sb("reg_is", [P, NB * T])
        quad = sb("quad", [P, GH])
        reg_row = sb("reg_row", [P, REG])
        eps_t = sb("eps_t", [P, 1])
        gvec = sb("gvec", [P, KC])
        parts_mark = sb("parts_mark", [1, 1])
        carry_dve = sb("carry_dve", [P, 32])
        carry_pool = sb("carry_pool", [P, 32])
        gtmp = sb("gtmp", [P, KC])
        gnrm = sb("gnrm", [P, KC])
        w_tok = pair("w_tok", [P, C])
        w_aqkv = pair("w_aqkv", [P, KC, 3 * C])
        w_aproj = pair("w_aproj", [P, KC, C])
        w_fqkv = pair("w_fqkv", [P, KC, 3 * C])
        w_fproj = pair("w_fproj", [P, KC, C])
        b_attn = sb("b_attn", [P, C])
        b_ffn = sb("b_ffn", [P, C])
        ids = sb("ids", [P, NB * T], I32)
        ids_now = sb("ids_now", [P, T], I32)
        emb = sb("emb", [P, T, P])
        emb_t = pair("emb_t", [P, S])
        h_all = sb("h_all", [P, NB, T * C])
        v_all = sb("v_all", [P, NB, T * C])
        sim_all = sb("sim_all", [P, NB * T])
        bst1 = sb("bst1", [P, T, 6])
        mv1 = sb("mv1", [P, T, 2])
        sd1 = sb("sd1", [P, T])
        rs1 = sb("rs1", [P, T])
        xn1 = sb("xn1", [P, T, C])
        xn1_t = pair("xn1_t", [P, KC, S])
        q1_t = sb("q1_t", [P, KC, S])
        kv = sb("kv", [P, T, 4, P + 1])
        vk = sb("vk", [P, KC, P + AH])
        den = sb("den", [P, T, KC, AH])
        rden = sb("rden", [P, T, KC, AH])
        mix = sb("mix", [P, T, KC, AH, AD])
        mix_t = pair("mix_t", [P, KC, S])
        bst2 = sb("bst2", [P, T, 6])
        mv2 = sb("mv2", [P, T, 2])
        sd2 = sb("sd2", [P, T])
        rs2 = sb("rs2", [P, T])
        xn2 = sb("xn2", [P, T, C])
        xn2_t = pair("xn2_t", [P, KC, S])
        qkf = sb("qkf", [P, KC, 2, S])
        qsq = sb("qsq", [P, KC, S])
        qk_parts = sb("qk_parts", [P, KC * 2, PARTS, S], BF16)
        qk_rest = sb("qk_rest", [P, KC * 2, S])
        dots = sb("dots", [P, S])
        nrm = sb("nrm", [P, T, KC, HH])
        rnrm = sb("rnrm", [P, T, KC, HH])
        cosb = sb("cosb", [P, T, KC, HH])
        ext = sb("ext", [P, 2])
        exta = sb("exta", [P, 2])
        zsum = sb("zsum", [P, 2])
        thr = sb("thr", [P, 2])
        pos = sb("pos", [P, NB * T])
        neg = sb("neg", [P, NB * T])
        cls = sb("cls", [P, 4, NB * T])
        cls_t = sb("cls_t", [4 * NB * T, P], BF16)
        q_st = [sb(f"q_st{u}", [ROWS, FH, NQ], BF16) for u in range(2)]
        k_st = [sb(f"k_st{u}", [ROWS, FH, S], BF16) for u in range(2)]
        v_st = [sb(f"v_st{u}", [P, T, FH, 2 * FD]) for u in range(2)]
        mx = sb("mx", [P, 2, 2 * HH + 2])
        mxr = sb("mxr", [P, 2, HH // GH, GH])
        mneg = sb("mneg", [HH, 2, NQ])
        mrow = sb("mrow", [HH, 2, 2, NQ], BF16)
        ex = [sb(f"ex{u}", [P, GH, T, NQ]) for u in range(2)]
        pv = [sb(f"pv{u}", [P, NG, NQ]) for u in range(2)]
        rsum = sb("rsum", [P, FH])
        rsumx = sb("rsumx", [REG, FH])
        att = sb("att", [P, T, FH, FD])
        halves_t = sb("halves_t", [REG, 1])
        rsum2 = sb("rsum2", [P, FH])
        attx = sb("attx", [REG, FH, FD])
        att_t = pair("att_t", [P, KC, S])
        ex_flat = [x[:, :, :, :].rearrange("p g t q -> p (g t q)") for x in ex]
        w_aqkv.append(ex_flat[0][:, 0:KC * 3 * C].rearrange("p (k n) -> p k n", k=KC))
        w_fqkv.append(ex_flat[1][:, 0:KC * 3 * C].rearrange("p (k n) -> p k n", k=KC))
        pv_flat = [x[:, :, :].rearrange("p g q -> p (g q)") for x in pv]
        w_aproj.append(pv_flat[0][:, 0:KC * C].rearrange("p (k n) -> p k n", k=KC))
        w_tok.append(pv_flat[0][:, KC * C:(KC + 1) * C])
        w_fproj.append(pv_flat[1][:, 0:KC * C].rearrange("p (k n) -> p k n", k=KC))
        resid = [sb(f"resid{u}", [P, T * C]) for u in range(2)]
        raw = sb("raw", [P, T * C])
        fin = [sb(f"fin{u}", [P, T * C]) for u in range(2)]

        loaded_tok = sem("loaded_tok")
        loaded = sem("loaded")
        whi_ready = sem("whi_ready")
        wlo_ready = sem("wlo_ready")
        embl_ready = sem("embl_ready")
        xn1l_ready = sem("xn1l_ready")
        mixl_ready = sem("mixl_ready")
        xn2l_ready = sem("xn2l_ready")
        attl_ready = sem("attl_ready")
        loaded_ffn = sem("loaded_ffn")
        const_pool = sem("const_pool")
        const_dve = sem("const_dve")
        g_sq = sem("g_sq")
        g_sum = sem("g_sum")
        g_root = sem("g_root")
        g_step = sem("g_step")
        g_ready = sem("g_ready")
        ids_loaded = sem("ids_loaded")
        ids_ready = sem("ids_ready")
        gathered = sem("gathered")
        embt_tr = sem("embt_tr")
        embt_ready = sem("embt_ready")
        h_mm = sem("h_mm")
        h_saved = sem("h_saved")
        ln1_stats = sem("ln1_stats")
        ln1_var = sem("ln1_var")
        ln1_root = sem("ln1_root")
        ln1_scale = sem("ln1_scale")
        xn1_ready = sem("xn1_ready")
        hb_ready = sem("hb_ready")
        xn1t_tr = sem("xn1t_tr")
        xn1t_ready = sem("xn1t_ready")
        q1_mm = sem("q1_mm")
        kv_mm = sem("kv_mm")
        q1_ready = sem("q1_ready")
        kv0_ready = sem("kv0_ready")
        kv1_ready = sem("kv1_ready")
        vk_mm = sem("vk_mm")
        vk_ready = sem("vk_ready")
        nd_mm = sem("nd_mm")
        den_ready = sem("den_ready")
        rden_ready = sem("rden_ready")
        mix_ready = sem("mix_ready")
        mixt_tr = sem("mixt_tr")
        mixt_ready = sem("mixt_ready")
        proj_mm = sem("proj_mm")
        h1_ready = sem("h1_ready")
        ln2_stats = sem("ln2_stats")
        ln2_var = sem("ln2_var")
        ln2_root = sem("ln2_root")
        ln2_scale = sem("ln2_scale")
        xn2_ready = sem("xn2_ready")
        xn2t_tr = sem("xn2t_tr")
        xn2t_ready = sem("xn2t_ready")
        qk2_mm = sem("qk2_mm")
        qkf_ready = sem("qkf_ready")
        qsq_ready = sem("qsq_ready")
        part0_ready = sem("part0_ready")
        rest_ready = sem("rest_ready")
        part1_ready = sem("part1_ready")
        part2_ready = sem("part2_ready")
        parts_stored = sem("parts_stored")
        v2_mm = sem("v2_mm")
        v2_ready = sem("v2_ready")
        dots_mm = sem("dots_mm")
        dots_ready = sem("dots_ready")
        dott_tr = sem("dott_tr")
        nrm_ready = sem("nrm_ready")
        rnrm_ready = sem("rnrm_ready")
        cos_ready = sem("cos_ready")
        sim_ready = sem("sim_ready")
        ext_ready = sem("ext_ready")
        exta_ready = sem("exta_ready")
        zsum_ready = sem("zsum_ready")
        zall_mm = sem("zall_mm")
        cls_step = sem("cls_step")
        cls_ready = sem("cls_ready")
        clst_tr = sem("clst_tr")
        clst_ready = sem("clst_ready")
        cls_stored = sem("cls_stored")
        st_const = sem("st_const")
        stack_in = [sem(f"stack_in{i}") for i in range(2)]
        class_in = [sem(f"class_in{i}") for i in range(2)]
        class_put = [sem(f"class_put{i}") for i in range(2)]
        clsr_tr = sem("clsr_tr")
        qx_ready = [sem(f"qx_ready{i}") for i in range(2)]
        vst_ready = sem("vst_ready")
        resid_ready = sem("resid_ready")
        s1_mm = sem("s1_mm")
        max_ready = sem("max_ready")
        mxt_tr = sem("mxt_tr")
        mhi_ready = sem("mhi_ready")
        mean_step = sem("mean_step")
        raw_ready = sem("raw_ready")
        mrow_ready = sem("mrow_ready")
        mxr_ready = sem("mxr_ready")
        mrow_in = [sem(f"mrow_in{i}") for i in range(2)]
        s2_mm = sem("s2_mm")
        ex_ready = sem("ex_ready")
        pv_mm = sem("pv_mm")
        pv_ready = sem("pv_ready")
        tok_tr = sem("tok_tr")
        rsum_ready = sem("rsum_ready")
        tok_ready = sem("tok_ready")
        reg_sum = sem("reg_sum")
        att_ready = sem("att_ready")
        attt_tr = sem("attt_tr")
        attt_ready = sem("attt_ready")
        out_mm = sem("out_mm")
        out_ready = sem("out_ready")
        last_ready = sem("last_ready")
        out_stored = sem("out_stored")

        LOADS = 3
        LOADS_FFN = 3 + KC

        def wait(eng, s, value):
            if not isinstance(value, int) or value > 0:
                eng.wait_ge(s, value)

        carriers = []

        def wait_apart(eng, s, value):
            eng.wait_ge(s, value)
            if not isinstance(value, int):
                carriers.append(s)
                own = slice(len(carriers), len(carriers) + 1)
                if eng is nc.vector:
                    nc.vector.memset(carry_dve[:, own], 0.0)
                else:
                    nc.gpsimd.tensor_tensor(carry_pool[:, own], carry_pool[:, 0:1], carry_pool[:, 0:1], ALU.add)

        def phase1(eng, body):
            body(-1, False, False, True)
            body(0, True, False, True)
            with eng.Fori(1, NB - 1) as b:
                body(b, True, True, True)
            body(NB - 1, True, True, False)
            body(NB, False, True, False)

        def phase2(eng, body, tail):
            body(-1, 1, False, False, True)
            body(0, 0, True, False, True)
            with eng.Fori(0, NB // 2 - 1) as i:
                body(i * 2 + 1, 1, True, True, True)
                body(i * 2 + 2, 0, True, True, True)
            body(NB - 1, 1, True, True, False)
            tail(NB - 1, 1)

        def load_classes(eng, b, u, half):
            heads = slice(half * HH, (half + 1) * HH)
            for st, c in ((q_st, 0), (k_st, 2)):
                src = class_dram.rearrange("c (b t) -> b c t", b=NB)[b, c:c + 2, :]
                eng.dma_start(st[u][ROW_CLASS:ROW_MAX, heads, 0:S],
                              src.unsqueeze(1).to_broadcast([2, HH, S])).then_inc(class_in[half], 16)

        def put_classes(eng, which, h0, h1):
            dst = (q_st, k_st)[which][0][ROW_CLASS:ROW_MAX, h0:h1, 0:S]
            src = ps[ROW_CLASS:ROW_MAX, 4 + which, 0:S].unsqueeze(1).to_broadcast([2, h1 - h0, S])
            eng.wait_ge(clsr_tr, 1)
            if eng is nc.scalar:
                if which == 1:
                    eng.wait_ge(class_put[1], 1)
                nc.scalar.activation(dst, src, ACT.Copy).then_inc(class_put[which], 1)
            else:
                nc.vector.tensor_copy(dst, src).then_inc(class_put[which], 1)

        def first_of(w, columns=slice(None)):
            every = tuple(slice(None) for _ in w[1].shape[1:]) + (columns,)
            nc.scalar.activation(w[0][every], w[2][every], ACT.Copy).then_inc(whi_ready, 1)

        def second_of(w, columns=slice(None)):
            every = tuple(slice(None) for _ in w[1].shape[1:]) + (columns,)
            return nc.vector.tensor_tensor(w[1][every], w[2][every], w[0][every].bitcast(F32), ALU.subtract)

        block = ctx.enter_context(nc.Block())

        @block.sync
        def _(sp):
            sp.dma_start(ids[:, :], x).then_inc(ids_loaded, 16)
            sp.dma_start(w_tok[2][:, :], tok_kernel).then_inc(loaded_tok, 16)
            sp.dma_start(w_aqkv[2][:, :, :],
                         attn_qkv_t.rearrange("(k p) n -> p k n", p=P)).then_inc(loaded, 16)
            sp.dma_start(w_aproj[2][:, :, :],
                         attn_proj_t.rearrange("(k p) n -> p k n", p=P)).then_inc(loaded, 16)
            sp.dma_start(b_attn[:, :], attn_bias.unsqueeze(0).to_broadcast([P, C])).then_inc(loaded, 16)
            sp.wait_ge(gathered, 32 * T)
            sp.dma_start(w_fqkv[2][:, :, :],
                         ffn_qkv.rearrange("(k p) n -> p k n", p=P)).then_inc(loaded_ffn, 16)
            sp.dma_start(w_fproj[2][:, :, :],
                         ffn_proj.rearrange("(k p) n -> p k n", p=P)).then_inc(loaded_ffn, 16)
            sp.dma_start(b_ffn[:, :], ffn_bias.unsqueeze(0).to_broadcast([P, C])).then_inc(loaded_ffn, 16)
            for k in range(KC):
                sp.dma_start(gvec[:, k:k + 1], ffn_g[0, 0, k * P:(k + 1) * P].unsqueeze(1)).then_inc(loaded_ffn, 16)

            def store_parts(p):
                for part in range(PARTS):
                    store_part(p, part)

            def store_part(p, part):
                sp.wait_ge((part0_ready, part1_ready, part2_ready)[part], p + 1)
                for i, (img, slot) in enumerate(((q_img, part), (k_img, PARTS - 1 - part))):
                    for k in range(KC):
                        dst = img[p, slot * FD:(slot + 1) * FD, k * HH:(k + 1) * HH, :]
                        sp.dma_start(dst.rearrange("d h t -> h d t"),
                                     qk_parts[:, 2 * k + i, part, :]).then_inc(parts_stored, 16)

            def load_stack(b, u, half):
                heads = slice(half * HH, (half + 1) * HH)
                row = 0
                for n in RUNS:
                    sp.dma_start(q_st[u][row:row + n * FD, heads, 0:S],
                                 q_img[b, 0:n * FD, heads, :]).then_inc(stack_in[half], 16)
                    sp.dma_start(k_st[u][row:row + n * FD, heads, :],
                                 k_img[b, (PARTS - n) * FD:, heads, :]).then_inc(stack_in[half], 16)
                    row += n * FD

            AHEAD = 2
            with sp.Fori(0, AHEAD + 2) as p:
                store_parts(p)
            for b in range(AHEAD):
                for half in range(2):
                    sp.wait_ge(parts_stored, 16 + 16 * NSTORE * (AHEAD + 1 + b))
                    wait(sp, stack_in[half], b * 16 * NLOAD)
                    load_stack(b, b, half)
                store_parts(AHEAD + 2 + b)
            for p in range(2 * AHEAD + 2, NB - 1):
                store_parts(p)

            def send_max_rows(b, u, half):
                for c, ready in enumerate((mhi_ready, mrow_ready)):
                    sp.wait_ge(ready, 2 * b + half + 1)
                    sp.dma_start(q_st[u][ROW_MAX + c:ROW_MAX + c + 1, half * HH:(half + 1) * HH, :],
                                 mrow[:, half, c, :]).then_inc(mrow_in[half], 16)

            sp.wait_ge(clst_ready, 1)
            sp.dma_start(class_dram.rearrange("c (s t) -> (c s) t", t=P), cls_t[:, :]).then_inc(cls_stored, 16)
            sp.wait_ge(cls_stored, 16)
            load_classes(sp, 0, 0, 1)
            load_classes(sp, 1, 1, 0)
            sp.wait_ge(class_in[1], 32)
            load_classes(sp, 1, 1, 1)
            def store_output(b, u):
                sp.wait_ge(out_stored, (b + 2) * 16)
                sp.wait_ge(out_ready, b + 2)
                sp.dma_start(out[b].rearrange("(t p) c -> p t c", p=P),
                             fin[u][:, :].rearrange("p (t c) -> p t c", t=T)).then_inc(out_stored, 16)

            def body(b, u, cur, prev, nxt, load):
                if not isinstance(b, int) or b > 1:
                    store_output(b - 2, u)
                if cur:
                    send_max_rows(b, u, 1)
                if isinstance(b, int) and b == 1:
                    store_part(NB - 1, 2)
                if load:
                    sp.wait_ge(s2_mm, b * FH + HH)
                    load_stack(b + 2, u, 0)
                    sp.wait_ge(class_in[0], b * 32 + 32)
                    load_classes(sp, b + 2, u, 0)
                if nxt:
                    send_max_rows(b + 1, 1 - u, 0)
                if isinstance(b, int) and b == 0:
                    store_part(NB - 1, 1)
                if load:
                    sp.wait_ge(s2_mm, b * FH + FH)
                    load_stack(b + 2, u, 1)
                    sp.wait_ge(class_in[1], b * 32 + 64)
                    load_classes(sp, b + 2, u, 1)

            store_part(NB - 1, 0)
            body(-1, 1, False, False, True, False)
            body(0, 0, True, False, True, True)
            body(1, 1, True, True, True, True)
            sp.wait_ge(parts_stored, 16 + 16 * NSTORE * NB)
            with sp.Fori(0, (NB - 4) // 2) as i:
                body(i * 2 + 2, 0, True, True, True, True)
                body(i * 2 + 3, 1, True, True, True, True)
            body(NB - 2, 0, True, True, True, False)
            body(NB - 1, 1, True, True, False, False)
            store_output(NB - 2, 0)
            for i, t in enumerate((1, 0)):
                sp.wait_ge(last_ready, i + 1)
                sp.dma_start(out[NB - 1, t * P:(t + 1) * P, :],
                             fin[1][:, t * C:(t + 1) * C]).then_inc(out_stored, 16)
            sp.wait_ge(out_stored, 16 * (NB + 3))

        @block.gpsimd
        def _(pool):
            def gather(n):
                if not isinstance(n, int) or n > 0:
                    wait_apart(pool, gathered, n * 16 * T)
                nc.gpsimd.tensor_copy(ids_now[:, :], ids[:, bass.ds(n * T, T)]).then_inc(ids_ready, 1)
                wait(pool, embt_tr, n)
                wait_apart(pool, ids_ready, n + 1)
                for t in range(T):
                    nc.gpsimd.indirect_dma_start(
                        out=emb[:, t, :], out_offset=None, in_=embeddings,
                        in_offset=bass.IndirectOffsetOnAxis(ap=ids_now[:, t:t + 1].bitcast(U32), axis=0),
                    ).then_inc(gathered, 16)

            nc.gpsimd.memset(carry_pool[:, 0:1], 0.0)
            nc.gpsimd.memset(ident[:, :], 0.0).then_inc(const_pool, 1)
            nc.gpsimd.memset(blk8[:, :, :], 1.0).then_inc(const_pool, 1)
            nc.gpsimd.memset(blk16[:, :, :], 1.0).then_inc(const_pool, 1)
            pool.wait_ge(const_pool, 3)
            nc.gpsimd.affine_select(out=ident[:, :], in_=ident[:, :], compare_op=ALU.not_equal, fill=1.0, base=0,
                                    pattern=[[-1, P]], channel_multiplier=1).then_inc(const_pool, 1)
            nc.gpsimd.affine_select(out=blk8[:, :, :], in_=blk8[:, :, :], compare_op=ALU.is_ge, fill=0.0, base=0,
                                    pattern=[[-AD, AH], [0, AD]], channel_multiplier=1).then_inc(const_pool, 1)
            nc.gpsimd.affine_select(out=blk16[:, :, :], in_=blk16[:, :, :], compare_op=ALU.is_ge, fill=0.0, base=0,
                                    pattern=[[-FD, HH], [0, FD]], channel_multiplier=1).then_inc(const_pool, 1)
            pool.wait_ge(ids_loaded, 16)
            gather(0)
            pool.wait_ge(const_pool, 6)
            nc.gpsimd.affine_select(out=blk8[:, :, :], in_=blk8[:, :, :], compare_op=ALU.is_ge, fill=0.0, base=AD - 1,
                                    pattern=[[AD, AH], [0, AD]], channel_multiplier=-1).then_inc(const_pool, 1)
            nc.gpsimd.affine_select(out=blk16[:, :, :], in_=blk16[:, :, :], compare_op=ALU.is_ge, fill=0.0,
                                    base=FD - 1, pattern=[[FD, HH], [0, FD]],
                                    channel_multiplier=-1).then_inc(const_pool, 1)
            nc.gpsimd.memset(quad[:, :], 1.0).then_inc(const_pool, 1)
            nc.gpsimd.memset(reg_row[:, :], 0.0).then_inc(const_pool, 1)
            pool.wait_ge(const_pool, 10)
            nc.gpsimd.affine_select(out=quad[:, :], in_=quad[:, :], compare_op=ALU.is_ge, fill=0.0, base=0,
                                    pattern=[[-32, GH]], channel_multiplier=1).then_inc(const_pool, 1)
            pool.wait_ge(const_pool, 11)
            nc.gpsimd.affine_select(out=quad[:, :], in_=quad[:, :], compare_op=ALU.is_ge, fill=0.0, base=31,
                                    pattern=[[32, GH]], channel_multiplier=-1).then_inc(const_pool, 1)
            for g in range(GH):
                pool.wait_ge(const_pool, 12 + g)
                nc.gpsimd.affine_select(out=reg_row[:, :], in_=reg_row[:, :], compare_op=ALU.not_equal, fill=1.0,
                                        base=-(32 * g + WIN - REG), pattern=[[-1, REG]],
                                        channel_multiplier=1).then_inc(const_pool, 1)
            nc.gpsimd.memset(halves_t[:, :], 0.5).then_inc(const_pool, 1)

            def body(b, cur, prev, nxt):
                n, p = b + 1, b - 1
                if cur and nxt:
                    gather_next(n)
                if nxt:
                    pool.wait_ge(xn1_ready, n + 1)
                    nc.gpsimd.tensor_tensor(
                        h_all[:, n, :].rearrange("p (t c) -> p t c", t=T),
                        h_all[:, n, :].rearrange("p (t c) -> p t c", t=T),
                        b_attn[:, :].unsqueeze(1).to_broadcast([P, T, C]), ALU.add).then_inc(hb_ready, 1)
                if prev:
                    rest(p)
                    third_part(p)

            def gather_next(n):
                gather(n + 1)

            def rest(p):
                pool.wait_ge(part0_ready, p + 1)
                nc.gpsimd.tensor_tensor(qk_rest[:, :, :], qkf[:, :, :, :].rearrange("p k c t -> p (k c) t"),
                                        qk_parts[:, :, 0, :], ALU.subtract).then_inc(rest_ready, 1)

            def third_part(p):
                pool.wait_ge(part1_ready, p + 1)
                nc.gpsimd.tensor_tensor(qk_parts[:, :, 2, :], qk_rest[:, :, :], qk_parts[:, :, 1, :],
                                        ALU.subtract).then_inc(part2_ready, 1)

            gather(1)
            for u in range(2):
                for i, (dst, value) in enumerate(((q_st[u][ROW_CLASS:ROW_MAX, :, S:NQ], 1.0),
                                                  (q_st[u][ROW_CLASS:ROW_CLASS + 1, :, S:NQ], 0.0),
                                                  (k_st[u][ROW_CLASS:ROWS, :, :], 1.0),
                                                  (v_st[u][:, :, :, FD:2 * FD], 1.0))):
                    wait(pool, st_const, 4 * u + i)
                    nc.gpsimd.memset(dst, value).then_inc(st_const, 1)
            pool.wait_ge(st_const, 8)
            body(-1, False, False, True)
            body(0, True, False, True)
            with pool.Fori(1, NB - 2) as b:
                body(b, True, True, True)
            pool.wait_ge(xn1_ready, NB)
            nc.gpsimd.tensor_tensor(
                h_all[:, NB - 1, :].rearrange("p (t c) -> p t c", t=T),
                h_all[:, NB - 1, :].rearrange("p (t c) -> p t c", t=T),
                b_attn[:, :].unsqueeze(1).to_broadcast([P, T, C]), ALU.add).then_inc(hb_ready, 1)
            for p in (NB - 3, NB - 2):
                rest(p)
                third_part(p)

            def registers(b, u, half):
                heads = slice(half * HH, (half + 1) * HH)
                wait_apart(pool, stack_in[half], (b + 1) * (16 * NLOAD))
                nc.gpsimd.tensor_copy(q_st[u][0:ROW_CLASS, heads, S:NQ],
                                      q_st[u][0:ROW_CLASS, heads, 0:REG]).then_inc(qx_ready[half], 1)

            def values(b, u):
                if not isinstance(b, int) or b > 1:
                    wait_apart(pool, pv_mm, b * NG - NG)
                nc.gpsimd.tensor_copy(v_st[u][:, :, :, 0:FD],
                                      v_all[:, b, :].rearrange("p (t h d) -> p t h d", t=T, h=FH)
                                      ).then_inc(vst_ready, 1)

            def residual(b, u):
                wait(pool, out_ready, b)
                nc.gpsimd.tensor_tensor(
                    resid[u][:, :].rearrange("p (t c) -> p t c", t=T),
                    h_all[:, b, :].rearrange("p (t c) -> p t c", t=T),
                    b_ffn[:, :].unsqueeze(1).to_broadcast([P, T, C]), ALU.add).then_inc(resid_ready, 1)

            def max_rest(b, half):
                pool.wait_ge(mhi_ready, b * 2 + half + 1)
                nc.gpsimd.tensor_tensor(mrow[:, half, 1, :], mneg[:, half, :], mrow[:, half, 0, :],
                                        ALU.subtract).then_inc(mrow_ready, 1)

            def body(b, u, cur, prev, nxt, more):
                o = 1 - u
                if cur:
                    max_rest(b, 1)
                if cur and nxt:
                    registers(b + 1, o, 1)
                if cur and nxt:
                    values(b + 1, o)
                if cur:
                    residual(b, u)
                if prev:
                    pool.wait_ge(tok_ready, b * 3 - 1)
                    nc.gpsimd.tensor_tensor(attx[:, :, :], att[0:REG, 0], attx[:, :, :], ALU.add).then_inc(reg_sum, 1)
                    pool.wait_ge(reg_sum, b)
                    nc.gpsimd.tensor_tensor(att[0:REG, 0], attx[:, :, :],
                                            halves_t[:, :].unsqueeze(2).to_broadcast([REG, FH, FD]),
                                            ALU.mult).then_inc(att_ready, 1)
                if nxt:
                    max_rest(b + 1, 0)
                if more:
                    registers(b + 2, u, 0)
                if prev:
                    pool.wait_ge(out_stored, b * 16)
                    pool.wait_ge(raw_ready, b + 1)
                    pool.wait_ge(resid_ready, b)
                    nc.gpsimd.tensor_tensor(fin[o][:, :], raw[:, :], resid[o][:, :], ALU.add).then_inc(out_ready, 1)

            registers(0, 0, 0)
            registers(0, 0, 1)
            registers(1, 1, 0)

            pool.wait_ge(ext_ready, 2)
            nc.gpsimd.partition_all_reduce(exta[:, :], ext[:, :], P, RMAX).then_inc(exta_ready, 1)
            values(0, 0)
            rest(NB - 1)
            third_part(NB - 1)

            body(-1, 1, False, False, True, False)
            body(0, 0, True, False, True, True)
            with pool.Fori(0, (NB - 4) // 2) as i:
                body(i * 2 + 1, 1, True, True, True, True)
                body(i * 2 + 2, 0, True, True, True, True)
            body(NB - 3, 1, True, True, True, True)
            body(NB - 2, 0, True, True, True, False)
            body(NB - 1, 1, True, True, False, False)

        @block.scalar
        def _(act):
            act.wait_ge(const_dve, 4)
            nc.scalar.activation(sd1[:, 0:1], eps_t[:, :], ACT.Sqrt)
            act.wait_ge(loaded_tok, 16)
            first_of(w_tok)

            def halves(bank):
                return ps[:, bank, :].rearrange("p (k t) -> p k t", k=KC)

            def save_q2(p):
                act.wait_ge(qk2_mm, p * 2 + 1)
                nc.scalar.activation(qkf[:, :, 0, :], halves(6), ACT.Copy).then_inc(qkf_ready, 1)
                act.wait_ge(qkf_ready, p * 2 + 1)
                nc.scalar.activation(qsq[:, :, :], qkf[:, :, 0, :], ACT.Square).then_inc(qsq_ready, 1)

            def save_k2(p):
                act.wait_ge(qk2_mm, p * 2 + 2)
                nc.scalar.activation(qkf[:, :, 1, :], halves(7), ACT.Copy).then_inc(qkf_ready, 1)

            def save_v2(p):
                act.wait_ge(v2_mm, p + 1)
                nc.scalar.activation(v_all[:, p, :], ps[:, 3, :], ACT.Copy).then_inc(v2_ready, 1)

            def save_dots(p):
                act.wait_ge(dots_mm, p + 1)
                nc.scalar.activation(dots[:, 0:REG], ps[:, 0, REG:2 * REG], ACT.Copy)
                nc.scalar.activation(dots[:, REG:S], ps[:, 0, REG:S], ACT.Copy).then_inc(dots_ready, 1)

            def second_part(p):
                act.wait_ge(rest_ready, p + 1)
                nc.scalar.activation(qk_parts[:, :, 1, :], qk_rest[:, :, :], ACT.Copy).then_inc(part1_ready, 1)

            def norms(p):
                act.wait_ge(dott_tr, p + 1)
                by = ps[:, 6, 0:T * P].rearrange("p (t g c) -> p t g c", t=T, g=4)
                nc.scalar.activation(nrm[:, :, :, :], by[:, :, 2:4, 0:HH], ACT.Sqrt).then_inc(nrm_ready, 1)

            def save_embeddings(n):
                act.wait_ge(embt_tr, n + 1)
                nc.scalar.activation(emb_t[0][:, :], ps[:, 0, 0:S], ACT.Copy).then_inc(embt_ready, 1)

            def save_tokens(n):
                act.wait_ge(h_mm, n + 1)
                nc.scalar.activation(h_all[:, n, :], ps[:, 1, :], ACT.Copy).then_inc(h_saved, 1)
                if isinstance(n, int) and n == 0:
                    act.wait_ge(loaded, 16 * LOADS)
                    first_of(w_aqkv, slice(0, C))

            def save_xn2(p):
                act.wait_ge(xn2t_tr, p + 1)
                nc.scalar.activation(xn2_t[0][:, :, :], halves(2), ACT.Copy).then_inc(xn2t_ready, 1)

            def body(b, cur, prev, nxt):
                n, p = b + 1, b - 1
                if not cur and prev:
                    save_xn2(p)
                    first_of(w_fproj)
                    save_q2(p)
                    save_dots(p)
                    norms(p)
                    save_k2(p)
                    save_v2(p)
                    return
                if cur:
                    act.wait_ge(q1_mm, b + 1)
                    nc.scalar.activation(q1_t[:, :, :], halves(3), ACT.Relu).then_inc(q1_ready, 1)
                if nxt:
                    save_embeddings(n)
                if cur and not prev:
                    act.wait_ge(g_step, 3)
                    first_of(w_fqkv)
                if cur:
                    act.wait_ge(kv_mm, b * T + 2)
                    nc.scalar.activation(kv[:, 1, :, 0:P], ps[:, 5, :].rearrange("p (k t) -> p k t", k=4),
                                         ACT.Relu).then_inc(kv1_ready, 1)
                if prev:
                    save_xn2(p)
                if nxt:
                    save_tokens(n)
                if prev:
                    save_q2(p)
                if nxt:
                    act.wait_ge(ln1_var, n + 1)
                    nc.scalar.activation(sd1[:, :], mv1[:, :, 1], ACT.Sqrt, bias=eps_t[:, 0:1]).then_inc(ln1_root, 1)
                if not cur:
                    first_of(w_aqkv, slice(C, 3 * C))
                if cur and not prev:
                    act.wait_ge(g_sum, 1)
                    nc.scalar.activation(gnrm[:, :], ps[:, 6, 0:KC], ACT.Sqrt).then_inc(g_root, 1)
                if prev:
                    save_k2(p)
                    if nxt:
                        save_v2(p)
                    else:
                        save_dots(p)
                if cur:
                    act.wait_ge(mixt_tr, b + 1)
                    nc.scalar.activation(mix_t[0][:, :, :], halves(2), ACT.Copy).then_inc(mixt_ready, 1)
                if prev and nxt:
                    save_dots(p)
                if nxt:
                    act.wait_ge(xn1t_tr, n + 1)
                    nc.scalar.activation(xn1_t[0][:, :, :], halves(1), ACT.Copy).then_inc(xn1t_ready, 1)
                if not cur:
                    first_of(w_aproj)
                if prev:
                    norms(p)
                if prev and nxt:
                    second_part(p)
                if cur:
                    act.wait_ge(ln2_var, b + 1)
                    nc.scalar.activation(sd2[:, :], mv2[:, :, 1], ACT.Sqrt, bias=eps_t[:, 0:1]).then_inc(ln2_root, 1)
                if cur and prev and not nxt:
                    save_v2(p)
                    second_part(p)

            phase1(act, body)

            put_classes(nc.scalar, 0, 0, HH // 2)
            act.wait_ge(clst_tr, 1)
            nc.scalar.activation(cls_t[:, :], ps[0:4 * NB * T, 7, 0:P], ACT.Copy).then_inc(clst_ready, 1)
            put_classes(nc.scalar, 0, HH // 2, HH)
            put_classes(nc.scalar, 1, HH // 2, HH)
            act.wait_ge(parts_stored, (NB - 1) * (16 * NSTORE) + 16)
            nc.scalar.activation(qk_parts[:, :, 0, :], qkf[:, :, :, :].rearrange("p k c t -> p (k c) t"),
                                 ACT.Copy).then_inc(part0_ready, 1)
            second_part(NB - 1)

            def minus_max(b, half):
                act.wait_ge(mxt_tr, b * 2 + half + 1)
                wait(act, mrow_in[half], b * 32)
                nc.scalar.activation(mneg[:, half, :], ps[0:HH, 7, 0:NQ], ACT.Copy, scale=-1.0)
                nc.scalar.activation(mrow[:, half, 0, :], ps[0:HH, 7, 0:NQ], ACT.Copy,
                                     scale=-1.0).then_inc(mhi_ready, 1)

            def group_out(b, u, j):
                act.wait_ge(pv_mm, b * NG + j + 1)
                nc.scalar.activation(pv[u][:, j, :], ps[:, 6, 0:NQ], ACT.Copy).then_inc(pv_ready, 1)

            def body(b, u, cur, prev, nxt):
                for h in range(FH):
                    if cur:
                        j = h // GH
                        act.wait_ge(s2_mm, b * FH + h + 1)
                        if h % GH == 0:
                            wait(act, pv_mm, b * NG + j - 1)
                        nc.scalar.activation(ex[j % 2][:, h % GH, :, :],
                                             ps[:, 2 + 2 * (h % 2):4 + 2 * (h % 2), 0:NQ],
                                             ACT.Exp).then_inc(ex_ready, 1)
                    if prev and h == 1:
                        group_out(b - 1, 1 - u, NG - 1)
                    if cur and h == 2:
                        minus_max(b, 1)
                    if cur and h in (7, 11, 13):
                        group_out(b, u, (h - 7) // 3)
                    if nxt and h == 10:
                        minus_max(b + 1, 0)
                    if prev and h == 12:
                        act.wait_ge(attt_tr, b)
                        nc.scalar.activation(att_t[0][:, :, :], ps[:, 7, :].rearrange("p (k t) -> p k t", k=KC),
                                             ACT.Copy).then_inc(attt_ready, 1)
                    if prev and h == 15:
                        act.wait_ge(out_mm, b)
                        nc.scalar.activation(raw[:, :], ps[:, 7, :], ACT.Copy).then_inc(raw_ready, 1)

            def tail(b, u):
                group_out(b, u, NG - 1)
                for i, t in enumerate((1, 0)):
                    act.wait_ge(attt_tr, b + 1 + i)
                    nc.scalar.activation(att_t[0][:, :, t * P:(t + 1) * P],
                                         ps[:, 3 + i, 0:C].rearrange("p (k t) -> p k t", k=KC),
                                         ACT.Copy).then_inc(attt_ready, 1)

            phase2(act, body, tail)

        @block.vector
        def _(dve):
            nc.vector.memset(parts_mark[:, :], 0.0).then_inc(parts_stored, 16)
            nc.vector.memset(fin[0][:, 0:1], 0.0).then_inc(out_stored, 16)
            nc.vector.memset(fin[1][:, 0:1], 0.0).then_inc(out_stored, 16)
            nc.vector.memset(resid[1][:, 0:1], 0.0).then_inc(out_ready, 1)
            nc.vector.memset(raw[:, 0:1], 0.0).then_inc(raw_ready, 1)
            nc.vector.memset(ones[:, :], 1.0).then_inc(const_dve, 1)
            nc.vector.memset(eps_t[:, :], LN_EPS).then_inc(const_dve, 1)
            nc.vector.memset(kv[:, :, :, P:P + 1], 1.0).then_inc(const_dve, 1)
            nc.vector.memset(reg_is[:, :], 0.0).then_inc(const_dve, 1)
            dve.wait_ge(const_dve, 4)
            nc.vector.memset(reg_is[0:REG, 0:NB * T:T], 1.0).then_inc(const_dve, 1)
            def scale_weights():
                dve.wait_ge(const_pool, 8)
                nc.vector.memset(head_of[:, :], 0.0).then_inc(g_step, 1)
                dve.wait_ge(g_step, 1)
                nc.vector.tensor_copy(head_of[:, 0:HH], blk16[:, :, 0]).then_inc(g_step, 1)
                dve.wait_ge(loaded_ffn, 16 * LOADS_FFN)
                nc.vector.tensor_scalar(w_fqkv[2][:, :, 0:C], w_fqkv[2][:, :, 0:C],
                                        float(FD) ** -0.5, None, ALU.mult).then_inc(g_step, 1)
                nc.vector.tensor_tensor(gtmp[:, :], gvec[:, :], gvec[:, :], ALU.mult).then_inc(g_sq, 1)

            def guide():
                dve.wait_ge(g_root, 1)
                dve.wait_ge(g_sum, 1)
                nc.vector.reciprocal(gtmp[:, :], gnrm[:, :]).then_inc(g_step, 1)
                dve.wait_ge(g_step, 4)
                nc.vector.scalar_tensor_tensor(out=gnrm[:, :], in0=gvec[:, :], scalar=1.0 / FH, in1=gtmp[:, :],
                                               op0=ALU.mult, op1=ALU.mult).then_inc(g_step, 1)
                dve.wait_ge(g_step, 5)
                for k in range(KC):
                    nc.vector.tensor_scalar(g_dot[:, k, :], head_of[:, :], gnrm[:, k:k + 1], None,
                                            ALU.mult).then_inc(g_ready, 1)

            def second_of_psum(ready, value, t, bank, done):
                dve.wait_ge(ready, value)
                nc.vector.tensor_tensor(t[1][:, :, :], ps[:, bank, :].rearrange("p (k t) -> p k t", k=KC),
                                        t[0][:, :, :].bitcast(F32), ALU.subtract).then_inc(done, 1)

            def second_of_embeddings(n):
                dve.wait_ge(embt_ready, n + 1)
                nc.vector.tensor_tensor(emb_t[1][:, :], ps[:, 0, 0:S], emb_t[0][:, :].bitcast(F32),
                                        ALU.subtract).then_inc(embl_ready, 1)

            def first_part(p):
                dve.wait_ge(qkf_ready, p * 2 + 2)
                dve.wait_ge(parts_stored, p * (16 * NSTORE) + 16)
                src = qkf[:, :, :, :].rearrange("p k c t -> p (k c) t")
                nc.vector.tensor_copy(qk_parts[:, :, 0, :], src).then_inc(part0_ready, 1)

            def layernorm1(n):
                wait_apart(dve, h_saved, n + 1)
                hv = h_all[:, n, :].rearrange("p (t c) -> p t c", t=T)
                for t in range(T):
                    nc.vector.bn_stats(bst1[:, t, :], hv[:, t, :]).then_inc(ln1_stats, 1)
                wait_apart(dve, ln1_stats, n * T + T)
                for t in range(T):
                    ins = nc.vector.bn_aggr(mv1[:, t, :], bst1[:, t, :])
                ins.then_inc(ln1_var, 1)

            def layernorm1_apply(n):
                hv = h_all[:, n, :].rearrange("p (t c) -> p t c", t=T)
                dve.wait_ge(ln1_root, n + 1)
                nc.vector.reciprocal(rs1[:, :], sd1[:, :]).then_inc(ln1_scale, 1)
                dve.wait_ge(ln1_scale, n + 1)
                for t in range(T):
                    ins = nc.vector.tensor_scalar(xn1[:, t, :], hv[:, t, :], mv1[:, t, 0:1], rs1[:, t:t + 1],
                                                  ALU.subtract, ALU.mult)
                ins.then_inc(xn1_ready, 1)

            def similarity(p):
                dve.wait_ge(nrm_ready, p + 1)
                nc.vector.reciprocal(rnrm[:, :, :, :], nrm[:, :, :, :]).then_inc(rnrm_ready, 1)
                dve.wait_ge(rnrm_ready, p + 1)
                sims = ps[:, 6, 0:T * P].rearrange("p (t g c) -> p t g c", t=T, g=4)
                nc.vector.tensor_tensor(cosb[:, :, :, :], sims[:, :, 0:2, 0:HH], rnrm[:, :, :, :],
                                        ALU.mult).then_inc(cos_ready, 1)
                dve.wait_ge(cos_ready, p + 1)
                nc.vector.tensor_reduce(sim_all[:, bass.ds(p * T, T)], cosb[:, :, :, :], axis=AX.XY,
                                        op=ALU.add).then_inc(sim_ready, 1)

            def body(b, cur, prev, nxt):
                n, p = b + 1, b - 1
                if not cur and prev:
                    second_of_psum(xn2t_ready, p + 1, xn2_t, 2, xn2l_ready)
                    dve.wait_ge(whi_ready, 6)
                    second_of(w_fproj).then_inc(wlo_ready, 1)
                    similarity(p)
                    return
                if not cur:
                    dve.wait_ge(whi_ready, 1)
                    second_of(w_tok).then_inc(wlo_ready, 1)
                    second_of_embeddings(n)
                if cur and not prev:
                    dve.wait_ge(whi_ready, 3)
                    second_of(w_aqkv, slice(C, 3 * C)).then_inc(wlo_ready, 1)
                    scale_weights()
                    dve.wait_ge(whi_ready, 4)
                    second_of(w_aproj).then_inc(wlo_ready, 1)
                if cur and nxt:
                    second_of_embeddings(n)
                if cur:
                    dve.wait_ge(kv_mm, b * T + 1)
                    nc.vector.tensor_scalar(kv[:, 0, :, 0:P], ps[:, 4, :].rearrange("p (k t) -> p k t", k=4),
                                            0.0, None, ALU.max).then_inc(kv0_ready, 1)
                    if prev:
                        second_of_psum(xn2t_ready, p + 1, xn2_t, 2, xn2l_ready)
                    if not prev:
                        dve.wait_ge(whi_ready, 5)
                        second_of(w_fqkv).then_inc(wlo_ready, 1)
                    dve.wait_ge(vk_mm, b + 1)
                    prod = ps[:, 3, 0:KC * (P + 1)].rearrange("p (k c) -> p k c", k=KC)
                    nc.vector.tensor_tensor(
                        vk[:, :, 0:P], prod[:, :, 0:P],
                        blk8[:, :, :].rearrange("p h e -> p (h e)").unsqueeze(1).to_broadcast([P, KC, P]), ALU.mult)
                    nc.vector.tensor_tensor(
                        vk[:, :, P:P + AH], prod[:, :, P:P + 1].to_broadcast([P, KC, AH]),
                        blk8[:, :, 0].unsqueeze(1).to_broadcast([P, KC, AH]), ALU.mult).then_inc(vk_ready, 1)
                if nxt:
                    layernorm1(n)
                if not cur:
                    layernorm1_apply(n)
                    dve.wait_ge(whi_ready, 2)
                    second_of(w_aqkv, slice(0, C)).then_inc(wlo_ready, 1)
                if cur:
                    dve.wait_ge(nd_mm, b + 1)
                    by = ps[:, 4:6, 0:KC * (P + AH)].rearrange("p t (k c) -> p t k c", k=KC)
                    nc.vector.tensor_scalar(den[:, :, :, :], by[:, :, :, P:P + AH], DEN_EPS, None,
                                            ALU.add).then_inc(den_ready, 1)
                    dve.wait_ge(den_ready, b + 1)
                    nc.vector.reciprocal(rden[:, :, :, :], den[:, :, :, :]).then_inc(rden_ready, 1)
                    dve.wait_ge(rden_ready, b + 1)
                    for t in range(T):
                        ins = nc.vector.tensor_tensor(
                            mix[:, t, :, :, :], by[:, t, :, 0:P].rearrange("p k (h e) -> p k h e", h=AH),
                            rden[:, t, :, :].unsqueeze(3).to_broadcast([P, KC, AH, AD]), ALU.mult)
                    ins.then_inc(mix_ready, 1)
                if cur and nxt:
                    layernorm1_apply(n)
                if cur:
                    second_of_psum(mixt_ready, b + 1, mix_t, 2, mixl_ready)
                if cur and prev:
                    first_part(p)
                if cur and not nxt:
                    similarity(p)
                if nxt:
                    second_of_psum(xn1t_ready, n + 1, xn1_t, 1, xn1l_ready)
                if cur and not prev:
                    guide()
                if cur:
                    dve.wait_ge(proj_mm, b + 1)
                    dve.wait_ge(hb_ready, b + 1)
                    h1v = h_all[:, b, :].rearrange("p (t c) -> p t c", t=T)
                    nc.vector.tensor_tensor(h1v, ps[:, 4:4 + T, 0:C], h1v, ALU.add).then_inc(h1_ready, 1)
                    wait_apart(dve, h1_ready, b + 1)
                    for t in range(T):
                        nc.vector.bn_stats(bst2[:, t, :], h1v[:, t, :]).then_inc(ln2_stats, 1)
                    wait_apart(dve, ln2_stats, b * T + T)
                    for t in range(T):
                        ins = nc.vector.bn_aggr(mv2[:, t, :], bst2[:, t, :])
                    ins.then_inc(ln2_var, 1)
                    if prev and nxt:
                        similarity(p)
                    dve.wait_ge(ln2_root, b + 1)
                    nc.vector.reciprocal(rs2[:, :], sd2[:, :]).then_inc(ln2_scale, 1)
                    dve.wait_ge(ln2_scale, b + 1)
                    for t in range(T):
                        ins = nc.vector.tensor_scalar(xn2[:, t, :], h1v[:, t, :], mv2[:, t, 0:1], rs2[:, t:t + 1],
                                                      ALU.subtract, ALU.mult)
                    ins.then_inc(xn2_ready, 1)

            phase1(dve, body)

            dve.wait_ge(sim_ready, NB)
            nc.vector.tensor_reduce(ext[:, 0:1], sim_all[:, :], axis=AX.X, op=ALU.max).then_inc(ext_ready, 1)
            nc.vector.tensor_reduce(ext[:, 1:2], sim_all[:, :], axis=AX.X, op=ALU.min,
                                    negate=True).then_inc(ext_ready, 1)
            nc.vector.tensor_reduce(zsum[:, 0:1], sim_all[:, :], axis=AX.X, op=ALU.add).then_inc(cls_step, 1)
            dve.wait_ge(cls_step, 1)
            nc.vector.tensor_scalar(zsum[:, 1:2], zsum[:, 0:1], 0.0, None, ALU.mult).then_inc(zsum_ready, 1)
            dve.wait_ge(exta_ready, 1)
            nc.vector.tensor_tensor(thr[:, 0:1], exta[:, 0:1], exta[:, 1:2], ALU.add).then_inc(cls_step, 1)
            dve.wait_ge(zall_mm, 1)
            dve.wait_ge(cls_step, 2)
            nc.vector.scalar_tensor_tensor(out=thr[:, 1:2], in0=thr[:, 0:1], scalar=0.9, in1=ps[:, 4, 0:1],
                                           op0=ALU.mult, op1=ALU.add).then_inc(cls_step, 1)
            dve.wait_ge(cls_step, 3)
            nc.vector.tensor_scalar(pos[:, :], sim_all[:, :], exta[:, 1:2], thr[:, 1:2], ALU.add,
                                    ALU.is_gt).then_inc(cls_step, 1)
            dve.wait_ge(cls_step, 4)
            nc.vector.tensor_tensor(cls[:, 0, :], pos[:, :], reg_is[:, :], ALU.max).then_inc(cls_step, 1)
            nc.vector.tensor_scalar(neg[:, :], pos[:, :], -1.0, 1.0, ALU.mult, ALU.add).then_inc(cls_step, 1)
            dve.wait_ge(cls_step, 6)
            nc.vector.tensor_tensor(pos[:, :], neg[:, :], reg_is[:, :], ALU.max).then_inc(cls_step, 1)
            nc.vector.tensor_scalar(cls[:, 1, :], cls[:, 0, :], -1.0, 1.0, ALU.mult, ALU.add)
            nc.vector.tensor_scalar(cls[:, 2, :], cls[:, 0, :], -1.0, BIG, ALU.add, ALU.mult)
            dve.wait_ge(cls_step, 7)
            nc.vector.tensor_scalar(cls[:, 3, :], pos[:, :], -1.0, BIG, ALU.add, ALU.mult).then_inc(cls_ready, 1)
            put_classes(nc.vector, 1, 0, HH // 2)

            def max_of(b, v, half, to):
                dve.wait_ge(s1_mm, b * UNITS + v + 1)
                if v % (HH + 1) == 0:
                    wait(dve, mxt_tr, b * 2 + half - 1)
                nc.vector.tensor_reduce(to, ps[:, v % 2, :].rearrange("p (t q) -> p t q", t=2), axis=AX.X,
                                        op=ALU.max).then_inc(max_ready, 1)

            OUTS = ((REG, attx[:, :, :], rsumx), (P, att[:, 0], rsum), (P, att[:, 1], rsum))

            def normalise(b, what):
                rows, dst, rs = OUTS[what]
                by = ps[0:rows, 7, :].rearrange("p (h c) -> p h c", h=FH)
                dve.wait_ge(tok_tr, b * 3 + what + 1)
                nc.vector.reciprocal(rs[:, :], by[:, :, FD]).then_inc(rsum_ready, 1)
                dve.wait_ge(rsum_ready, b * 3 + what + 1)
                nc.vector.tensor_tensor(dst, by[:, :, 0:FD], rs[:, :].unsqueeze(2).to_broadcast([rows, FH, FD]),
                                        ALU.mult).then_inc(tok_ready, 1)

            def body(b, u, cur, prev, nxt):
                for h in range(FH):
                    half, hh = h // HH, h % HH
                    if nxt:
                        max_of(b + 1, h + half, half, mx[:, half, hh:hh + HH + 1:HH])
                        if hh == HH - 1:
                            max_of(b + 1, h + half + 1, half, mx[:, half, 2 * HH:2 * HH + 2])
                            dve.wait_ge(max_ready, b * UNITS + UNITS + (HH + 1) * (half + 1))
                            nc.vector.tensor_tensor(
                                mxr[:, half, :, :],
                                mx[:, half, 2 * HH:2 * HH + 2].unsqueeze(2).to_broadcast([P, HH // GH, GH]),
                                quad[:, :].unsqueeze(1).to_broadcast([P, HH // GH, GH]),
                                ALU.mult).then_inc(mxr_ready, 1)
                    if prev and h in (4, 6, 8):
                        normalise(b - 1, (h - 4) // 2)
                    if prev and h == 12:
                        second_of_psum(attt_ready, b, att_t, 7, attl_ready)

            def tail(b, u):
                dve.wait_ge(tok_tr, b * 3 + 3)
                by = [ps[0:rows, i, :].rearrange("p (h c) -> p h c", h=FH) for i, (rows, _, _) in enumerate(OUTS)]
                sums = (rsumx, rsum, rsum2)
                for i in range(3):
                    nc.vector.reciprocal(sums[i][:, :], by[i][:, :, FD]).then_inc(rsum_ready, 1)

                def divide(i):
                    rows, dst, _ = OUTS[i]
                    dve.wait_ge(rsum_ready, b * 3 + i + 1)
                    nc.vector.tensor_tensor(dst, by[i][:, :, 0:FD],
                                            sums[i][:, :].unsqueeze(2).to_broadcast([rows, FH, FD]),
                                            ALU.mult).then_inc(tok_ready, 1)

                divide(0)
                divide(1)
                dve.wait_ge(tok_ready, b * 3 + 2)
                nc.vector.tensor_tensor(attx[:, :, :], att[0:REG, 0], attx[:, :, :], ALU.add).then_inc(mean_step, 1)
                divide(2)
                dve.wait_ge(mean_step, 1)
                nc.vector.tensor_scalar(att[0:REG, 0], attx[:, :, :], 0.5, None, ALU.mult).then_inc(mean_step, 1)
                for i, t in enumerate((1, 0)):
                    dve.wait_ge(attt_ready, b + 1 + i)
                    nc.vector.tensor_tensor(att_t[1][:, :, t * P:(t + 1) * P],
                                            ps[:, 3 + i, 0:C].rearrange("p (k t) -> p k t", k=KC),
                                            att_t[0][:, :, t * P:(t + 1) * P].bitcast(F32),
                                            ALU.subtract).then_inc(attl_ready, 1)
                dve.wait_ge(resid_ready, b + 1)
                dve.wait_ge(out_stored, b * 16 + 16)
                for i, t in enumerate((1, 0)):
                    dve.wait_ge(out_mm, b + 1 + i)
                    nc.vector.tensor_tensor(fin[u][:, t * C:(t + 1) * C], ps[:, 5 + i, 0:C],
                                            resid[u][:, t * C:(t + 1) * C], ALU.add).then_inc(last_ready, 1)

            phase2(dve, body, tail)

        @block.tensor
        def _(pe):
            mm = nc.tensor.matmul
            pe.wait_ge(const_pool, 4)

            def keep_warm(n, bank):
                for _ in range(n):
                    mm(ps[:, bank, 0:P], ident[:, :], ident[:, :], start=True, stop=True)

            def guide_norms():
                pe.wait_ge(const_pool, 8)
                pe.wait_ge(g_sq, 1)
                mm(ps[:, 6, 0:KC], blk16[:, :, :].rearrange("p h d -> p (h d)"), gtmp[:, :],
                   start=True, stop=True).then_inc(g_sum, 1)

            def to_channels(src, bank):
                for k in range(KC):
                    for t in range(T):
                        ins = nc.tensor.transpose(ps[:, bank, k * S + t * P:k * S + (t + 1) * P],
                                                  src[:, t, k * P:(k + 1) * P], ident[:, :])
                return ins

            def products(outs, lhs, rhs, data_left, lo_ready, lo_count, terms=KC, own_banks=False):
                pairs = ((0, 0), (0, 1), (1, 0))
                order = [(i, pair) for i in range(len(outs)) for pair in pairs]
                if own_banks:
                    order.sort(key=lambda x: x[1][0])
                first = order.index((0, pairs[2]))
                for n, (i, (data, weight)) in enumerate(order):
                    if n == first:
                        pe.wait_ge(lo_ready, lo_count)
                    left, right = (data, weight) if data_left else (weight, data)
                    for k in range(terms):
                        ins = mm(outs[i], lhs(i, k)[left], rhs(i, k)[right],
                                 start=(data + weight + k == 0), stop=(data == 1 and k == terms - 1))
                return ins

            def q_product(b):
                pe.wait_ge(xn1t_ready, b + 1)
                if isinstance(b, int):
                    pe.wait_ge(wlo_ready, 2)
                ins = products([ps[:, 3, m * S:(m + 1) * S] for m in range(KC)],
                               lambda m, k: [w[:, k, m * P:(m + 1) * P] for w in w_aqkv[:2]],
                               lambda m, k: [x[:, k, :] for x in xn1_t], False, xn1l_ready, b + 1)
                ins.then_inc(q1_mm, 1)

            def kv_product(b, t):
                if t == 0:
                    wait(pe, h1_ready, b)
                    if isinstance(b, int):
                        pe.wait_ge(wlo_ready, 3)
                ins = products([ps[:, 4 + t, :]], lambda i, k: [x[:, k, t * P:(t + 1) * P] for x in xn1_t],
                               lambda i, k: [w[:, k, C:3 * C] for w in w_aqkv[:2]], True, xn1l_ready, b + 1)
                ins.then_inc(kv_mm, 1)

            def turn_xn2(p, cur):
                pe.wait_ge(xn2_ready, p + 1)
                if cur:
                    pe.wait_ge(xn1t_ready, p + 2)
                to_channels(xn2, 2).then_inc(xn2t_tr, 1)

            def turn_embeddings(n):
                pe.wait_ge(gathered, n * (16 * T) + 16 * T)
                for t in range(T):
                    ins = nc.tensor.transpose(ps[:, 0, t * P:(t + 1) * P], emb[:, t, :], ident[:, :])
                ins.then_inc(embt_tr, 1)

            def vk_product(b):
                pe.wait_ge(kv0_ready, b + 1)
                pe.wait_ge(kv1_ready, b + 1)
                pe.wait_ge(q1_ready, b + 1)
                for k in range(KC):
                    for t in range(T):
                        ins = mm(ps[:, 3, k * (P + 1):(k + 1) * (P + 1)], kv[:, t, k, 0:P], kv[:, t, KC + k, :],
                                 start=(t == 0), stop=(t == T - 1))
                ins.then_inc(vk_mm, 1)

            def token_product(n):
                pe.wait_ge(embt_ready, n + 1)
                if isinstance(n, int):
                    pe.wait_ge(wlo_ready, 1)
                ins = products([ps[:, 1, t * C:(t + 1) * C] for t in range(T)],
                               lambda t, k: [x[:, t * P:(t + 1) * P] for x in emb_t],
                               lambda t, k: [w[:, :] for w in w_tok[:2]], True, embl_ready, n + 1, terms=1)
                ins.then_inc(h_mm, 1)

            def qk2_product(p, i):
                pe.wait_ge(xn2t_ready, p + 1)
                if i == 0:
                    wait(pe, cos_ready, p)
                pe.wait_ge(g_step, 4)
                pe.wait_ge(wlo_ready, 5)
                ins = products([ps[:, 6 + i, m * S:(m + 1) * S] for m in range(KC)],
                               lambda m, k: [w[:, k, i * C + m * P:i * C + (m + 1) * P] for w in w_fqkv[:2]],
                               lambda m, k: [x[:, k, :] for x in xn2_t], False, xn2l_ready, p + 1)
                ins.then_inc(qk2_mm, 1)

            def nd_product(b):
                pe.wait_ge(vk_ready, b + 1)
                for t in range(T):
                    for k in range(KC):
                        ins = mm(ps[:, 4 + t, k * (P + AH):(k + 1) * (P + AH)], q1_t[:, k, t * P:(t + 1) * P],
                                 vk[:, k, :], start=True, stop=True)
                ins.then_inc(nd_mm, 1)

            def v2_product(p, cur):
                if cur:
                    pe.wait_ge(vk_ready, p + 2)
                ins = products([ps[:, 3, t * C:(t + 1) * C] for t in range(T)],
                               lambda t, k: [x[:, k, t * P:(t + 1) * P] for x in xn2_t],
                               lambda t, k: [w[:, k, 2 * C:3 * C] for w in w_fqkv[:2]], True, xn2l_ready, p + 1)
                ins.then_inc(v2_mm, 1)

            def dot_products(p):
                pe.wait_ge(qsq_ready, p + 1)
                pe.wait_ge(g_ready, KC)
                for g in range(4):
                    w = g_dot[:, g, :] if g < KC else head_of[:, :]
                    r = qkf[:, g, 0, :] if g < KC else qsq[:, g - KC, :]
                    ins = mm(ps[32 * g:32 * g + 32, 0, 0:S], w, r, start=True, stop=True)
                ins.then_inc(dots_mm, 1)

            def turn_mix(b, prev):
                pe.wait_ge(mix_ready, b + 1)
                if prev:
                    pe.wait_ge(xn2t_ready, b)
                to_channels(mix[:, :, :, :, :].rearrange("p t k h e -> p t (k h e)"), 2).then_inc(mixt_tr, 1)

            def turn_dots(p):
                pe.wait_ge(dots_ready, p + 1)
                for t in range(T):
                    ins = nc.tensor.transpose(ps[:, 6, t * P:(t + 1) * P], dots[:, t * P:(t + 1) * P], ident[:, :])
                ins.then_inc(dott_tr, 1)

            def turn_xn1(n):
                pe.wait_ge(xn1_ready, n + 1)
                to_channels(xn1, 1).then_inc(xn1t_tr, 1)

            def mix_projection(b):
                pe.wait_ge(mixt_ready, b + 1)
                if isinstance(b, int):
                    pe.wait_ge(wlo_ready, 4)
                ins = products([ps[:, 4 + t, 0:C] for t in range(T)],
                               lambda t, k: [x[:, k, t * P:(t + 1) * P] for x in mix_t],
                               lambda t, k: [w[:, k, :] for w in w_aproj[:2]], True, mixl_ready, b + 1, own_banks=True)
                ins.then_inc(proj_mm, 1)

            def body(b, cur, prev, nxt):
                n, p = b + 1, b - 1
                if not cur and prev:
                    pe.wait_ge(qkf_ready, 2 * p)
                    keep_warm(7, 7)
                    turn_xn2(p, cur)
                    qk2_product(p, 0)
                    keep_warm(6, 5)
                    dot_products(p)
                    keep_warm(3, 5)
                    turn_dots(p)
                    qk2_product(p, 1)
                    return
                if cur:
                    q_product(b)
                if not cur:
                    keep_warm(12, 7)
                if nxt:
                    turn_embeddings(n)
                if cur:
                    kv_product(b, 0)
                    kv_product(b, 1)
                if prev:
                    turn_xn2(p, cur)
                if nxt:
                    token_product(n)
                if cur:
                    vk_product(b)
                if cur and not prev:
                    guide_norms()
                if prev:
                    qk2_product(p, 0)
                if cur:
                    nd_product(b)
                if prev:
                    qk2_product(p, 1)
                    if nxt:
                        v2_product(p, cur)
                    else:
                        dot_products(p)
                if not cur:
                    keep_warm(16, 7)
                if cur and not prev:
                    keep_warm(8, 7)
                if cur:
                    turn_mix(b, prev)
                if prev and nxt:
                    dot_products(p)
                if nxt:
                    turn_xn1(n)
                if prev and not nxt:
                    turn_dots(p)
                if cur:
                    mix_projection(b)
                if prev and nxt:
                    turn_dots(p)
                if prev and not nxt:
                    v2_product(p, cur)

            phase1(pe, body)
            pe.wait_ge(const_pool, 12 + GH)

            pe.wait_ge(zsum_ready, 1)
            pe.wait_ge(h1_ready, NB)
            mm(ps[:, 4, 0:1], ones[:, :], zsum[:, 1:2], start=True, stop=True).then_inc(zall_mm, 1)
            v2_product(NB - 1, False)
            pe.wait_ge(cos_ready, NB)
            pe.wait_ge(dots_ready, NB)
            pe.wait_ge(qkf_ready, 2 * NB)
            pe.wait_ge(wlo_ready, 6)
            pe.wait_ge(cls_ready, 1)
            for i in range(2):
                for t in range(T):
                    ins = mm(ps[ROW_CLASS:ROW_MAX, 4 + i, t * P:(t + 1) * P], cls[:, 2 * i:2 * i + 2, t],
                             ident[:, :], start=True, stop=True)
            ins.then_inc(clsr_tr, 1)
            nc.tensor.transpose(ps[0:4 * NB * T, 7, 0:P], cls[:, :, :].rearrange("p c s -> p (c s)"),
                                ident[:, :]).then_inc(clst_tr, 1)
            keep_warm(8, 0)
            pe.wait_ge(clst_ready, 1)
            pe.wait_ge(v2_ready, NB)

            def send_max(b, half):
                pe.wait_ge(mxr_ready, b * 2 + half + 1)
                for t in range(T):
                    nc.tensor.transpose(ps[0:HH, 7, t * P:(t + 1) * P], mx[:, half, t * HH:(t + 1) * HH],
                                        ident[:, :])
                mm(ps[0:HH, 7, S:NQ], mxr[:, half, :, :].rearrange("p j g -> p (j g)"), reg_row[:, :],
                   start=True, stop=True).then_inc(mxt_tr, 1)

            def group(b, u, j, t):
                if t == 0:
                    pe.wait_ge(ex_ready, b * FH + GH * (j + 1))
                    pe.wait_ge(vst_ready, b + 1)
                    wait(pe, pv_ready, b * NG + j)
                for g in range(GH):
                    ins = mm(ps[32 * g:32 * g + 32, 6, 0:NQ], v_st[u][:, t, GH * j + g, :],
                             ex[j % 2][:, g, t, :], start=(t == 0), stop=(t == T - 1))
                if t == T - 1:
                    ins.then_inc(pv_mm, 1)

            def out_projection(t, bank, c0, lo_count):
                return products([ps[:, bank, c0:c0 + C]], lambda i, k: [x[:, k, t * P:(t + 1) * P] for x in att_t],
                                lambda i, k: [w[:, k, :] for w in w_fproj[:2]], True, attl_ready, lo_count)

            def to_tokens(u, q0, nq, bank=7):
                for j in range(NG):
                    ins = nc.tensor.transpose(ps[0:nq, bank, j * P:(j + 1) * P], pv[u][:, j, q0:q0 + nq], ident[:, :])
                ins.then_inc(tok_tr, 1)

            def body(b, u, cur, prev, nxt):
                o = 1 - u
                for h in range(FH):
                    half = h // HH
                    if cur:
                        if h % HH == 0:
                            pe.wait_ge(mrow_in[half], b * 32 + 32)
                        wait(pe, ex_ready, b * FH + h - 1)
                        for t in range(T):
                            ins = mm(ps[:, 2 + 2 * (h % 2) + t, 0:NQ], k_st[u][:, h, t * P:(t + 1) * P],
                                     q_st[u][:, h, :], start=True, stop=True)
                        ins.then_inc(s2_mm, 1)
                    if nxt:
                        v = h + half
                        if h % HH == 0:
                            pe.wait_ge(qx_ready[half], b + 2)
                            if not cur and half == 0:
                                for i in range(2):
                                    pe.wait_ge(class_put[i], 1)
                            if cur or half == 1:
                                pe.wait_ge(class_in[half], b * 32 + 32 * (half + 1))
                        if not cur and h == HH // 2:
                            for i in range(2):
                                pe.wait_ge(class_put[i], 2)
                        wait(pe, max_ready, b * UNITS + UNITS + v - 1)
                        for t in range(T):
                            ins = mm(ps[:, v % 2, t * S:(t + 1) * S], q_st[o][0:ROW_MAX, h, t * P:(t + 1) * P],
                                     k_st[o][0:ROW_MAX, h, :], start=True, stop=True)
                        ins.then_inc(s1_mm, 1)
                        if not cur:
                            keep_warm(1, 6)
                        if h % HH == HH - 1:
                            v = v + 1
                            wait(pe, max_ready, b * UNITS + UNITS + v - 1)
                            for j in range(HH // GH):
                                for g in range(GH):
                                    ins = mm(ps[32 * g:32 * g + 32, v % 2, j * S:(j + 1) * S],
                                             q_st[o][0:ROW_MAX, half * HH + j * GH + g, NQ - WIN:NQ],
                                             k_st[o][0:ROW_MAX, half * HH + j * GH + g, :],
                                             start=True, stop=True)
                            ins.then_inc(s1_mm, 1)
                    if prev and h in (0, 1):
                        group(b - 1, o, NG - 1, h)
                    if cur and h == 2:
                        if prev:
                            pe.wait_ge(raw_ready, b)
                        send_max(b, 1)
                    if prev and h == 4:
                        pe.wait_ge(pv_ready, b * NG)
                        if cur:
                            pe.wait_ge(mhi_ready, b * 2 + 2)
                        else:
                            pe.wait_ge(raw_ready, b)
                        to_tokens(o, S, REG)
                    if cur and h in (5, 7):
                        group(b, u, 0, (h - 5) // 2)
                    if prev and h == 6:
                        pe.wait_ge(tok_ready, b * 3 - 2)
                        to_tokens(o, 0, P)
                    if prev and h == 8:
                        pe.wait_ge(tok_ready, b * 3 - 1)
                        to_tokens(o, P, P)
                    if cur and h in (9, 11):
                        group(b, u, 1, (h - 9) // 2)
                    if nxt and h == (10 if cur else 9):
                        if prev:
                            pe.wait_ge(tok_ready, b * 3)
                        elif cur:
                            pe.wait_ge(mhi_ready, 2)
                        send_max(b + 1, 0)
                    if prev and h == 12:
                        pe.wait_ge(att_ready, b)
                        if nxt:
                            pe.wait_ge(mhi_ready, b * 2 + 3)
                        else:
                            pe.wait_ge(tok_ready, b * 3)
                        to_channels(att[:, :, :, :].rearrange("p t h d -> p t (h d)"), 7).then_inc(attt_tr, 1)
                    if cur and h == 13:
                        group(b, u, 2, 0)
                        group(b, u, 2, 1)
                    tiles = [h - (FH - T)] if nxt and h >= FH - T else list(range(T)) if not nxt and h == FH - 1 else []
                    for t in tiles if prev else []:
                        if t == 0:
                            pe.wait_ge(attt_ready, b)
                            pe.wait_ge(attl_ready, b)
                        ins = out_projection(t, 7, t * C, b)
                        if t == T - 1:
                            ins.then_inc(out_mm, 1)

            def tail(b, u):
                for t in range(T):
                    group(b, u, NG - 1, t)
                pe.wait_ge(max_ready, NB * UNITS)
                keep_warm(2, 0)
                pe.wait_ge(pv_ready, b * NG + NG)
                to_tokens(u, S, REG, 0)
                to_tokens(u, 0, P, 1)
                to_tokens(u, P, P, 2)
                for i, t in enumerate((1, 0)):
                    keep_warm(3, 7 - i)
                    if t:
                        pe.wait_ge(tok_ready, b * 3 + 3)
                    else:
                        pe.wait_ge(mean_step, 2)
                    for k in range(KC):
                        ins = nc.tensor.transpose(
                            ps[:, 3 + i, k * P:(k + 1) * P],
                            att[:, t, :, :].rearrange("p h d -> p (h d)")[:, k * P:(k + 1) * P], ident[:, :])
                    ins.then_inc(attt_tr, 1)
                for i, t in enumerate((1, 0)):
                    pe.wait_ge(attt_ready, b + 1 + i)
                    ins = out_projection(t, 5 + i, 0, b + 1 + i)
                    ins.then_inc(out_mm, 1)

            phase2(pe, body, tail)


def kernel(x, L0_tok_embeddings, L0_tok_project_kernel, L0_attn_qkv_weight, L0_attn_proj_weight,
           L0_attn_proj_bias, L0_ffn_g_info, L0_ffn_W_qkv, L0_ffn_W_proj, L0_ffn_b_proj):
    import numpy as np
    import concourse.bacc as bacc
    from concourse import mybir as mb
    from concourse.bass_utils import run_bass_kernel_spmd

    x = np.asarray(x)
    arrays = {
        "ids": np.ascontiguousarray(x.reshape(-1, P).T),
        "embeddings": np.ascontiguousarray(L0_tok_embeddings),
        "tok_kernel": np.ascontiguousarray(L0_tok_project_kernel),
        "attn_qkv_t": np.ascontiguousarray(np.asarray(L0_attn_qkv_weight).T),
        "attn_proj_t": np.ascontiguousarray(np.asarray(L0_attn_proj_weight).T),
        "attn_bias": np.ascontiguousarray(L0_attn_proj_bias),
        "ffn_g": np.ascontiguousarray(L0_ffn_g_info),
        "ffn_qkv": np.ascontiguousarray(L0_ffn_W_qkv),
        "ffn_proj": np.ascontiguousarray(L0_ffn_W_proj),
        "ffn_bias": np.ascontiguousarray(L0_ffn_b_proj),
    }
    nc = bacc.Bacc("TRN2", target_bir_lowering=False, num_devices=1)
    args = [nc.dram_tensor("in_" + n, a.shape, mb.dt.from_np(a.dtype), kind="ExternalInput").ap()
            for n, a in arrays.items()]
    out = nc.dram_tensor("out", (*x.shape, arrays["tok_kernel"].shape[1]), F32, kind="ExternalOutput").ap()
    lm_tower(nc, *args, out)
    r = run_bass_kernel_spmd(nc, [{"in_" + n: a for n, a in arrays.items()}], core_ids=[0])
    return r.results[0]["out"]
```
